# Optimizing a Trainium2 kernel written in Bass

```python
import numpy as np
import jax
import jax.numpy as jnp

def _softmax(x, axis=-1):
    return jax.nn.softmax(x, axis=axis)

def _gelu(x):
    return jax.nn.gelu(x, approximate=True)

def _silu(x):
    return jax.nn.silu(x)

def _sigmoid(x):
    return jax.nn.sigmoid(x)

def _layernorm(x, axis=-1, eps=1e-05):
    m = jnp.mean(x, axis=axis, keepdims=True)
    v = jnp.var(x, axis=axis, keepdims=True)
    return (x - m) / jnp.sqrt(v + eps)

def _scatter_add(tgt, idx, src, axis=0):
    return tgt.at[idx].add(src)

def _segment_sum(src, seg, n):
    return jax.ops.segment_sum(src, seg, n)
kernel_name = 'mk_flamingo_gated_d2_seqx_r8_60c9e1'

def setup_inputs(seed: int=0):
    np.random.seed(seed)
    _w = jnp.asarray

    def _rec_inputs():
        import jax
        import jax.numpy as jnp
        _rk = jax.random.key(seed)
        x = -0.0005207 + 1.001 * jax.random.normal(jax.random.fold_in(_rk, 1), (8, 128, 512), jnp.float32)
        _lenS = 128 - jax.random.randint(jax.random.fold_in(_rk, 7), (8,), 0, max(1, 128 // 4) + 1, jnp.int32)
        _lenS2 = 128 - jax.random.randint(jax.random.fold_in(_rk, 8), (8,), 0, max(1, 128 // 4) + 1, jnp.int32)
        _ctx_4096P = jax.random.normal(jax.random.fold_in(_rk, 11), (8, 16, 512), jnp.float32)
        _ctx_4096c = jax.random.dirichlet(jax.random.fold_in(_rk, 511), 0.3 * jnp.ones((16,), jnp.float32), (8, 128))
        _ctx_4096t = jnp.einsum('bsk,bkd->bsd', _ctx_4096c, _ctx_4096P)
        _ctx_4096t = _ctx_4096t * jax.lax.rsqrt(jnp.mean(jnp.square(_ctx_4096t)) + 1e-12) * 0.953939
        ctx_4096 = -0.00010331 + 0.999899 * (_ctx_4096t + 0.3 * jax.random.normal(jax.random.fold_in(_rk, 611), (8, 128, 512), jnp.float32))
        _validS = jnp.arange(128)[None, :] < _lenS[:, None]
        _validS2 = jnp.arange(128)[None, :] < _lenS2[:, None]
        _causal = jnp.tril(jnp.ones((128, 128), dtype=bool))
        mask_SxS2_bk0 = jnp.logical_not(jnp.broadcast_to(_validS2[0:1, :], (128, 128)))
        _g = jax.random.normal(jax.random.fold_in(_rk, 9001), (2, 2), jnp.float32)
        _g = jnp.sign(_g) * jnp.maximum(jnp.abs(_g), 1.0) + (_g == 0) * 1.0
        g_xattn = _g[0]
        g_ffn = _g[1]
        return (x, ctx_4096, mask_SxS2_bk0, g_xattn, g_ffn)
    x, ctx_4096, mask_SxS2_bk0, g_xattn, g_ffn = _rec_inputs()

    def _L0_xattn_setup():
        import jax, jax.numpy as jnp
        import numpy as np
        import math
        HIDDEN = 512
        N_HEADS = 32
        HEAD_DIM = 128
        N_KV_HEADS = 4
        N_GROUPS = N_HEADS // N_KV_HEADS
        key = jax.random.key(seed)
        ks = jax.random.split(key, 6)
        B, NL, S = (8, 64, 512)
        latents = jax.random.normal(ks[0], (B, NL, HIDDEN), dtype=jnp.float32)
        context = jax.random.normal(ks[1], (B, S, HIDDEN), dtype=jnp.float32)
        scale = 1.0 / math.sqrt(HIDDEN)
        Wq = jax.random.normal(ks[2], (HIDDEN, N_HEADS * HEAD_DIM), dtype=jnp.float32) * scale
        Wk = jax.random.normal(ks[3], (HIDDEN, N_KV_HEADS * HEAD_DIM), dtype=jnp.float32) * scale
        Wv = jax.random.normal(ks[4], (HIDDEN, N_KV_HEADS * HEAD_DIM), dtype=jnp.float32) * scale
        Wo = jax.random.normal(ks[5], (N_HEADS * HEAD_DIM, HIDDEN), dtype=jnp.float32) * scale
        return {'latents': latents, 'context': context, 'Wq': Wq, 'Wk': Wk, 'Wv': Wv, 'Wo': Wo}
    _L0_xattn_all = _L0_xattn_setup()
    _L0_xattn_in = {k: v for k, v in _L0_xattn_all.items() if k in ('Wq', 'Wk', 'Wv', 'Wo')}
    del _L0_xattn_all

    def _L0_ffn_setup():
        import jax, jax.numpy as jnp
        import numpy as np
        HID, INT, LAT, NE, K = (512, 1024, 256, 8, 2)
        LN_EPS = 1e-05

        def _layernorm(x, gamma, beta):
            mu = jnp.mean(x, axis=-1, keepdims=True)
            var = jnp.var(x, axis=-1, keepdims=True)
            return (x - mu) * jax.lax.rsqrt(var + LN_EPS) * gamma + beta
        key = jax.random.key(seed)
        ks = jax.random.split(key, 8)
        s = lambda d: 1.0 / np.sqrt(d)
        return {'hidden_states': jax.random.normal(ks[0], (4, 256, HID), jnp.float32), 'gate_w': jax.random.normal(ks[1], (HID, NE), jnp.float32) * s(HID), 'up_w': jax.random.normal(ks[2], (HID, INT), jnp.float32) * s(HID), 'down_w': jax.random.normal(ks[3], (INT, HID), jnp.float32) * s(INT), 'fc1_w': jax.random.normal(ks[4], (HID, LAT), jnp.float32) * s(HID), 'fc2_w': jax.random.normal(ks[5], (LAT, HID), jnp.float32) * s(LAT), 'expert_w': jax.random.normal(ks[6], (LAT, LAT), jnp.float32), 'ln_gamma': jnp.ones((HID,), jnp.float32), 'ln_beta': jnp.zeros((HID,), jnp.float32)}
    _L0_ffn_all = _L0_ffn_setup()
    _L0_ffn_in = {k: v for k, v in _L0_ffn_all.items() if k in ('gate_w', 'up_w', 'down_w', 'fc1_w', 'fc2_w', 'expert_w', 'ln_gamma', 'ln_beta')}
    del _L0_ffn_all

    def _L1_xattn_setup():
        import jax, jax.numpy as jnp
        import numpy as np
        N_HEAD = 32
        D_MODEL = 512
        N_KV_GROUPS = 8
        D_HEAD = D_MODEL // N_HEAD
        H_PER_G = N_HEAD // N_KV_GROUPS
        KV_DIM = N_KV_GROUPS * D_HEAD
        B, S = (2, 256)
        key = jax.random.key(seed)
        ks = jax.random.split(key, 8)
        q = jax.random.normal(ks[0], (B, S, D_MODEL), dtype=jnp.float32)
        k = jax.random.normal(ks[1], (B, S, D_MODEL), dtype=jnp.float32)
        v = jax.random.normal(ks[2], (B, S, D_MODEL), dtype=jnp.float32)
        mask = jnp.tril(jnp.ones((S, S), dtype=bool))
        w_q = jax.random.uniform(ks[3], (D_MODEL, D_MODEL), dtype=jnp.float32) * 0.02
        w_k = jax.random.uniform(ks[4], (KV_DIM, D_MODEL), dtype=jnp.float32) * 0.02
        w_v = jax.random.uniform(ks[5], (KV_DIM, D_MODEL), dtype=jnp.float32) * 0.02
        w_out = jax.random.uniform(ks[6], (D_MODEL, D_MODEL), dtype=jnp.float32) * 0.02
        return {'q': q, 'k': k, 'v': v, 'w_q': w_q, 'w_k': w_k, 'w_v': w_v, 'w_out': w_out, 'mask': mask}
    _L1_xattn_all = _L1_xattn_setup()
    _L1_xattn_in = {k: v for k, v in _L1_xattn_all.items() if k in ('w_q', 'w_k', 'w_v', 'w_out')}
    del _L1_xattn_all

    def _L1_ffn_setup():
        import jax, jax.numpy as jnp
        import numpy as np
        NUM_EXPERTS = 8
        D_IN = 512
        D_OUT = 512
        key = jax.random.key(seed)
        k_x, k_gw, k_gb, k_ew, k_eb = jax.random.split(key, 5)
        x = jax.random.normal(k_x, (4, 256, D_IN), dtype=jnp.float32)
        gate_w = jax.random.normal(k_gw, (NUM_EXPERTS, D_IN), dtype=jnp.float32) * 0.02
        gate_b = jax.random.normal(k_gb, (NUM_EXPERTS,), dtype=jnp.float32) * 0.02
        expert_w = jax.random.normal(k_ew, (NUM_EXPERTS, D_OUT, D_IN), dtype=jnp.float32) * 0.02
        expert_b = jax.random.normal(k_eb, (NUM_EXPERTS, D_OUT), dtype=jnp.float32) * 0.02
        return {'x': x, 'gate_w': gate_w, 'gate_b': gate_b, 'expert_w': expert_w, 'expert_b': expert_b}
    _L1_ffn_all = _L1_ffn_setup()
    _L1_ffn_in = {k: v for k, v in _L1_ffn_all.items() if k in ('gate_w', 'gate_b', 'expert_w', 'expert_b')}
    del _L1_ffn_all
    return {'x': x, 'ctx_4096': ctx_4096, 'mask_SxS2_bk0': mask_SxS2_bk0, 'g_xattn': g_xattn, 'g_ffn': g_ffn, 'L0_xattn_Wq': _L0_xattn_in['Wq'], 'L0_xattn_Wk': _L0_xattn_in['Wk'], 'L0_xattn_Wv': _L0_xattn_in['Wv'], 'L0_xattn_Wo': _L0_xattn_in['Wo'], 'L0_ffn_gate_w': _L0_ffn_in['gate_w'], 'L0_ffn_up_w': _L0_ffn_in['up_w'], 'L0_ffn_down_w': _L0_ffn_in['down_w'], 'L0_ffn_fc1_w': _L0_ffn_in['fc1_w'], 'L0_ffn_fc2_w': _L0_ffn_in['fc2_w'], 'L0_ffn_expert_w': _L0_ffn_in['expert_w'], 'L0_ffn_ln_gamma': _L0_ffn_in['ln_gamma'], 'L0_ffn_ln_beta': _L0_ffn_in['ln_beta'], 'L1_xattn_w_q': _L1_xattn_in['w_q'], 'L1_xattn_w_k': _L1_xattn_in['w_k'], 'L1_xattn_w_v': _L1_xattn_in['w_v'], 'L1_xattn_w_out': _L1_xattn_in['w_out'], 'L1_ffn_gate_w': _L1_ffn_in['gate_w'], 'L1_ffn_gate_b': _L1_ffn_in['gate_b'], 'L1_ffn_expert_w': _L1_ffn_in['expert_w'], 'L1_ffn_expert_b': _L1_ffn_in['expert_b']}

def reference(x, ctx_4096, mask_SxS2_bk0, g_xattn, g_ffn, L0_xattn_Wq, L0_xattn_Wk, L0_xattn_Wv, L0_xattn_Wo, L0_ffn_gate_w, L0_ffn_up_w, L0_ffn_down_w, L0_ffn_fc1_w, L0_ffn_fc2_w, L0_ffn_expert_w, L0_ffn_ln_gamma, L0_ffn_ln_beta, L1_xattn_w_q, L1_xattn_w_k, L1_xattn_w_v, L1_xattn_w_out, L1_ffn_gate_w, L1_ffn_gate_b, L1_ffn_expert_w, L1_ffn_expert_b):
    import jax
    import jax.numpy as jnp

    def _L0_xattn_ref(latents, context, Wq, Wk, Wv, Wo):
        import jax, jax.numpy as jnp
        import numpy as np
        import math
        HIDDEN = 512
        N_HEADS = 32
        HEAD_DIM = 128
        N_KV_HEADS = 4
        N_GROUPS = N_HEADS // N_KV_HEADS
        b, q_len, _ = latents.shape
        kv_len = q_len + context.shape[1]
        hidden_states = jnp.concatenate([context, latents], axis=1)
        q = (latents @ Wq).reshape(b, q_len, N_KV_HEADS, N_GROUPS, HEAD_DIM)
        k = (hidden_states @ Wk).reshape(b, kv_len, N_KV_HEADS, HEAD_DIM)
        v = (hidden_states @ Wv).reshape(b, kv_len, N_KV_HEADS, HEAD_DIM)
        scale = 1.0 / math.sqrt(HEAD_DIM)
        scores = jnp.einsum('bqhgd,bkhd->bhgqk', q, k) * scale
        attn = jax.nn.softmax(scores.astype(jnp.float32), axis=-1).astype(q.dtype)
        out = jnp.einsum('bhgqk,bkhd->bqhgd', attn, v)
        out = out.reshape(b, q_len, N_HEADS * HEAD_DIM)
        return out @ Wo

    def _L0_ffn_ref(hidden_states, gate_w, up_w, down_w, fc1_w, fc2_w, expert_w, ln_gamma, ln_beta):
        import jax, jax.numpy as jnp
        import numpy as np
        HID, INT, LAT, NE, K = (512, 1024, 256, 8, 2)
        LN_EPS = 1e-05

        def _layernorm(x, gamma, beta):
            mu = jnp.mean(x, axis=-1, keepdims=True)
            var = jnp.var(x, axis=-1, keepdims=True)
            return (x - mu) * jax.lax.rsqrt(var + LN_EPS) * gamma + beta
        logits = jnp.einsum('bsh,he->bse', hidden_states, gate_w)
        routing_weights, selected_experts = jax.lax.top_k(logits, K)
        h = jax.nn.relu(jnp.einsum('bsh,hi->bsi', hidden_states, up_w)) ** 2
        shared_out = jnp.einsum('bsi,ih->bsh', h, down_w)
        x_latent = jnp.einsum('bsh,hl->bsl', hidden_states, fc1_w)
        expert_out = jnp.einsum('bsl,lm->bsm', x_latent, expert_w)
        moe_out = expert_out * jnp.sum(routing_weights, axis=-1, keepdims=True)
        routed_out = jnp.einsum('bsl,lh->bsh', moe_out, fc2_w)
        return _layernorm(shared_out + routed_out, ln_gamma, ln_beta)

    def _L1_xattn_ref(q, k, v, w_q, w_k, w_v, w_out, mask):
        import jax, jax.numpy as jnp
        import numpy as np
        N_HEAD = 32
        D_MODEL = 512
        N_KV_GROUPS = 8
        D_HEAD = D_MODEL // N_HEAD
        H_PER_G = N_HEAD // N_KV_GROUPS
        KV_DIM = N_KV_GROUPS * D_HEAD
        B, S = (2, 256)
        b, n, _ = q.shape
        s = k.shape[1]
        query = q @ w_q.T
        key = k @ w_k.T
        value = v @ w_v.T
        query = query.reshape(b, n, N_HEAD, D_HEAD).transpose(0, 2, 1, 3)
        query = query.reshape(b, N_KV_GROUPS, H_PER_G, n, D_HEAD)
        key = key.reshape(b, s, N_KV_GROUPS, D_HEAD).transpose(0, 2, 1, 3)
        value = value.reshape(b, s, N_KV_GROUPS, D_HEAD).transpose(0, 2, 1, 3)
        scores = jnp.einsum('bghnd,bgsd->bghns', query, key) / D_HEAD ** 0.5
        scores = jnp.where(mask, scores, jnp.finfo(scores.dtype).min)
        attention = jax.nn.softmax(scores, axis=-1)
        out = jnp.einsum('bghns,bgsd->bghnd', attention, value)
        out = out.transpose(0, 3, 1, 2, 4).reshape(b, n, D_MODEL)
        return out @ w_out.T

    def _L1_ffn_ref(x, gate_w, gate_b, expert_w, expert_b):
        import jax, jax.numpy as jnp
        import numpy as np
        NUM_EXPERTS = 8
        D_IN = 512
        D_OUT = 512
        orig_shape = x.shape
        xf = x.reshape(-1, x.shape[-1])
        gate_logits = xf @ gate_w.T + gate_b
        gates = jax.nn.softmax(gate_logits, axis=-1)
        selected = jnp.argmax(gates, axis=-1)
        out = jnp.zeros((xf.shape[0], expert_w.shape[1]), dtype=xf.dtype)
        for j in range(expert_w.shape[0]):
            yj = xf @ expert_w[j].T + expert_b[j]
            out = out + jnp.where((selected == j)[:, None], yj, 0.0)
        return out.reshape(*orig_shape[:-1], expert_w.shape[1])
    x = x + jnp.tanh(g_xattn[0]) * _L0_xattn_ref(_layernorm(x, axis=-1), ctx_4096, L0_xattn_Wq, L0_xattn_Wk, L0_xattn_Wv, L0_xattn_Wo)
    x = x + jnp.tanh(g_ffn[0]) * _L0_ffn_ref(_layernorm(x, axis=-1), L0_ffn_gate_w, L0_ffn_up_w, L0_ffn_down_w, L0_ffn_fc1_w, L0_ffn_fc2_w, L0_ffn_expert_w, L0_ffn_ln_gamma, L0_ffn_ln_beta)
    x = x + jnp.tanh(g_xattn[1]) * _L1_xattn_ref(_layernorm(x, axis=-1), ctx_4096, ctx_4096, L1_xattn_w_q, L1_xattn_w_k, L1_xattn_w_v, L1_xattn_w_out, mask_SxS2_bk0)
    x = x + jnp.tanh(g_ffn[1]) * _L1_ffn_ref(_layernorm(x, axis=-1), L1_ffn_gate_w, L1_ffn_gate_b, L1_ffn_expert_w, L1_ffn_expert_b)
    return x

_drawn_inputs = setup_inputs


def setup_inputs(seed=0):
    import zlib

    import numpy as np

    out = dict(_drawn_inputs(seed))
    spreads = {'g_ffn': (-1.0, 0.2), 'L0_ffn_ln_gamma': (1.0, 0.2), 'L0_ffn_ln_beta': (0.0, 0.1)}
    factors = {'L1_ffn_expert_b': 5.327}
    for name, (base, spread) in spreads.items():
        noise = np.random.default_rng([zlib.crc32(name.encode()), seed]).standard_normal(out[name].shape)
        drawn = base * np.exp(spread * noise) if base else spread * noise
        out[name] = jnp.asarray(drawn.astype(out[name].dtype))
    for name, factor in factors.items():
        out[name] = (out[name] * factor).astype(out[name].dtype)
    return out
```

```python
from contextlib import ExitStack

import concourse.bass as bass
from concourse import mybir


ALU = mybir.AluOpType
ACT = mybir.ActivationFunctionType
F32 = mybir.dt.float32
F32R = mybir.dt.float32r
U8 = mybir.dt.uint8
U32 = mybir.dt.uint32
AX_X = mybir.AxisListType.X

P = 128
B = 8
D = 512
KT = D // P
HALF = 4
LN_EPS = 1e-5

KVH = 4
GROUP = 8
QUAD = 4
NQUAD = KVH * GROUP // QUAD
STEPS = NQUAD * B
KEYS = 2 * P
SCALE0 = float(P) ** -0.5

H1 = 32
D1 = D // H1
G1 = 8
HT1 = P // D1
M1 = H1 // HT1
SCALE1 = float(D1) ** -0.5
MASKED = -3.0e38

NE = 8
INT = 1024
LAT = 256
IT = INT // P
LT = LAT // P


def program(nc, x, ctxT, mask, g_xattn, g_ffn, Wq, Wk, Wv, Wo, gate0, up_w, down_w, fc1_w, fc2_w,
            latent_w, ln_gamma, ln_beta, wqT, wkT, wvT, woutT, gate1T, gate1_b, expertT, expert_b, out):
    ctx = ExitStack()
    with ctx:
        def sb(name, shape, dt=F32):
            return ctx.enter_context(nc.sbuf_tensor(name, shape, dt))

        def sem(name):
            return ctx.enter_context(nc.semaphore(name))

        PS = ctx.enter_context(nc.psum_tensor("PS", [P, 8, 512], F32))
        bank = [PS[:, k, :] for k in range(8)]

        X = sb("X", [P, B, D])
        work = sb("work", [P, 8, 512])
        prob = work[:, 0:4, :].rearrange("p (s a) c -> p s (a c)", s=2)
        probT = work[:, 4:8, :].rearrange("p (s a) c -> p s (a c)", s=2)
        gam = work[:, 4, :]
        bet = work[:, 5, :]
        zrow = work[:, 6:8, :]
        raw = sb("raw", [P, 4, 512])
        hrow = sb("hrow", [P, 2, 512])
        V1 = sb("V1", [P, B, G1, D1 + 1])
        ident = sb("ident", [P, P])
        iota8 = sb("iota8", [P, NE])
        graw = sb("graw", [P, 4])
        gate = sb("gate", [P, 4])
        stats = sb("stats", [P, 2, 6])
        meanvar = sb("meanvar", [P, B, 2])
        vareps = sb("vareps", [P, B])
        rstd = sb("rstd", [P, B])
        mhalf = sb("mhalf", [P, 1])
        zmv = sb("zmv", [P, B, 2])
        zve = sb("zve", [P, B])
        zrs = sb("zrs", [P, B])
        nmax = sb("nmax", [P, 2, QUAD])
        psumr = sb("psumr", [P, 2, QUAD])
        rinv = sb("rinv", [P, 2, QUAD])
        top0 = sb("top0", [P, HALF, 8])
        route = sb("route", [P, B])
        max1 = sb("max1", [P, 2, HT1])
        rsum1 = sb("rsum1", [P, 2, 16])
        gb1 = sb("gb1", [P, NE])
        logit1 = sb("logit1", [P, B, NE])
        top1 = sb("top1", [P, B, 8])
        idx1 = sb("idx1", [P, B, 8], U32)
        idxf = sb("idxf", [P, B])
        sel = sb("sel", [P, B, NE])
        graww = hrow[:, 1, 512 - 2 * KT * NE:512].rearrange("p (l k n) -> p l k n", l=2, k=KT)
        mask8 = sb("mask8", [P, P], U8)

        arena = sb("arena", [P, 40064 + 2 * 2 * KT * NE], F32R)

        def region(at, words):
            return arena[:, at:at + words]

        HT = region(0, 8192).rearrange("p (s k t) -> p s k t", s=2, k=KT)
        RA, RB, RC, RD, RE = 8192, 16384, 24576, 32768, 37888
        Wk_r = region(RB, 4096).rearrange("p (s k n) -> p s k n", s=2, k=KT)
        Wv_r = region(RB + 4096, 4096).rearrange("p (s k n) -> p s k n", s=2, k=KT)
        CT = region(RC, 8192).rearrange("p (s k t) -> p s k t", s=2, k=KT)
        wk1_r = region(RA + 4096, 1024).rearrange("p (s k n) -> p s k n", s=2, k=KT)
        wv1_r = region(RA + 5120, 1024).rearrange("p (s k n) -> p s k n", s=2, k=KT)
        stage = region(RD, 4096).rearrange("p (j s n) -> p j s n", j=4, s=2)
        Wq_r = region(RA, 8192).rearrange("p (j s k n) -> p j s k n", j=2, s=2, k=KT)
        Wo_r = region(RB, 8192).rearrange("p (j s h n) -> p j s h n", j=2, s=2, h=QUAD)
        qT = region(RC, 8192).rearrange("p (j s h t) -> p j s h t", j=2, s=2, h=QUAD)
        Kb = region(RD, 1024).rearrange("p (j s t) -> p j s t", j=2, s=2)
        Vb = region(RD + 1024, 1024).rearrange("p (j s k n) -> p j s k n", j=2, s=2, k=2)
        PT = region(RD + 2048, 2048).rearrange("p (s k n) -> p s k n", s=2, k=2)
        OT = region(RD + 4096, 1024).rearrange("p (s n) -> p s n", s=2)
        up_r = region(RA, 8192).rearrange("p (s k n) -> p s k n", s=2, k=KT)
        down_r = region(RB, 8192).rearrange("p (s k n) -> p s k n", s=2, k=IT)
        actT = region(RC, 8192).rearrange("p (s k t) -> p s k t", s=2, k=IT)
        xlT = region(RC, 2048).rearrange("p (s k t) -> p s k t", s=2, k=LT)
        eoT = region(RC + 2048, 2048).rearrange("p (s k t) -> p s k t", s=2, k=LT)
        fc1_r = region(RD, 2048).rearrange("p (s k n) -> p s k n", s=2, k=KT)
        lat_r = region(RD + 2048, 1024).rearrange("p (s k n) -> p s k n", s=2, k=LT)
        fc2_r = region(RD + 3072, 2048).rearrange("p (s k n) -> p s k n", s=2, k=LT)
        wq1_r = region(RA, 4096).rearrange("p (s k n) -> p s k n", s=2, k=KT)
        wout_r = region(RA + 4096, 4096).rearrange("p (s k n) -> p s k n", s=2, k=KT)
        KB = region(RB, 8192).rearrange("p (m s h t) -> p m s h t", m=M1, s=2, h=HT1)
        qT1 = region(RC, 8192).rearrange("p (s m t) -> p s m t", s=2, m=M1)
        OT1 = region(RD, 2048).rearrange("p (j s k t) -> p j s k t", j=2, s=2, k=KT)
        maskr = region(RD + 2048, 512)
        KT1 = region(RE, 2048).rearrange("p (s t) -> p s t", s=2)
        Ex = [region(RA, 4096).rearrange("p (s k n) -> p s k n", s=2, k=KT),
              region(RB, 4096).rearrange("p (s k n) -> p s k n", s=2, k=KT)]
        identr = region(RE + 2048, P)
        gw = region(RE + 2048 + P, 2 * 2 * KT * NE).rearrange("p (l s k n) -> p l s k n", l=2, s=2, k=KT)

        Kscr = nc.dram_tensor("Kscr", [KVH, B, P, 2, KEYS], F32).ap()
        Vscr = nc.dram_tensor("Vscr", [KVH, B, P, 2, 2, P], F32).ap()

        small_loaded = sem("small_loaded")
        gates_tanh = sem("gates_tanh")
        consts_made = sem("consts_made")
        identr_made = sem("identr_made")
        gatew_hi = sem("gatew_hi")
        gatew_lo = sem("gatew_lo")
        x_loaded = [sem(f"x_loaded{b}") for b in range(B)]
        a_loaded = [sem(f"a_loaded{k}") for k in range(8)]
        a_hi = sem("a_hi")
        a_lo = sem("a_lo")
        raw_loaded = [sem(f"raw_loaded{k}") for k in range(4)]
        chunk_hi = sem("chunk_hi")
        step_hi = sem("step_hi")
        ex_hi = sem("ex_hi")
        chunk_split = sem("chunk_split")
        ln_stat = sem("ln_stat")
        ln_rstd = sem("ln_rstd")
        ln_row = sem("ln_row")
        ln_T = sem("ln_T")
        ln_hi = sem("ln_hi")
        ln_lo = sem("ln_lo")
        kv_mm = sem("kv_mm")
        kv_hi = sem("kv_hi")
        kv_lo = sem("kv_lo")
        kv_stored = [sem(f"kv_stored{k}") for k in range(4)]
        k_loaded = [sem(f"k_loaded{k}") for k in range(2)]
        v_loaded = [sem(f"v_loaded{k}") for k in range(2)]
        q_mm = sem("q_mm")
        q_hi = sem("q_hi")
        q_lo = sem("q_lo")
        s_mm = sem("s_mm")
        s_max = sem("s_max")
        s_exp = sem("s_exp")
        s_rcp = sem("s_rcp")
        p_norm = sem("p_norm")
        p_T = sem("p_T")
        pt_hi = sem("pt_hi")
        pt_lo = sem("pt_lo")
        o_mm = sem("o_mm")
        o_hi = sem("o_hi")
        o_lo = sem("o_lo")
        y_mm = sem("y_mm")
        y_acc = sem("y_acc")
        chain = sem("chain")
        gb_loaded = sem("gb_loaded")
        eb_loaded = sem("eb_loaded")
        gb_made = sem("gb_made")
        xbeta = sem("xbeta")
        m_gate = sem("m_gate")
        m_route = sem("m_route")
        m_xl = sem("m_xl")
        m_xl_hi = sem("m_xl_hi")
        m_xl_lo = sem("m_xl_lo")
        m_fc2 = sem("m_fc2")
        m_fc2_out = sem("m_fc2_out")
        m_up = sem("m_up")
        m_relu = sem("m_relu")
        m_sq = sem("m_sq")
        m_sq_hi = sem("m_sq_hi")
        m_sq_lo = sem("m_sq_lo")
        m_down = sem("m_down")
        z_stat = sem("z_stat")
        z_rstd = sem("z_rstd")
        mask_made = sem("mask_made")
        kb_zero = sem("kb_zero")
        kb_loaded = [sem(f"kb_loaded{m}") for m in range(M1)]
        q1_mm = sem("q1_mm")
        q1_hi = sem("q1_hi")
        q1_lo = sem("q1_lo")
        s1_mm = sem("s1_mm")
        s1_max = sem("s1_max")
        s1_sub = sem("s1_sub")
        s1_exp = sem("s1_exp")
        p1_T = sem("p1_T")
        p1_copy = sem("p1_copy")
        o1_mm = sem("o1_mm")
        o1_rcp = sem("o1_rcp")
        o1_row = sem("o1_row")
        o1_T = sem("o1_T")
        o1_hi = sem("o1_hi")
        o1_lo = sem("o1_lo")
        y1_mm = sem("y1_mm")
        y1_acc = sem("y1_acc")
        g1_mm = sem("g1_mm")
        g1_sel = sem("g1_sel")
        g1_T = sem("g1_T")
        g1_copy = sem("g1_copy")
        b1_mm = sem("b1_mm")
        b1_acc = sem("b1_acc")
        e_mm = sem("e_mm")
        e_acc = sem("e_acc")
        out_stored = sem("out_stored")

        def kv_jobs(part):
            out = []
            for half in range(2):
                out += [("K", part, h, half) for h in range(KVH)]
                out += [("V", part, half * HALF + b) for b in range(HALF)]
            return out

        JOBS = kv_jobs(0) + [("k1", 0), ("k1", 1), ("v1", 0), ("v1", 1), ("v1t", 0), ("v1t", 1)] + kv_jobs(1)
        HAS_LO = [j[0] in ("K", "V", "k1") for j in JOBS]
        LOS = [sum(HAS_LO[:n + 1]) for n in range(len(JOBS))]
        STORE = [sum(j[0] in "KV" for j in JOBS[:n]) for n in range(len(JOBS))]
        NCTX = 16
        NA = 16

        C_WQ0 = 2
        C_WO0 = C_WQ0 + KT
        C_STEP = C_WO0 + QUAD
        C_UP = C_STEP + STEPS - B
        C_FC = C_UP + 8
        C_DOWN = C_FC + 5
        C_WQ1 = C_DOWN + IT
        C_WOUT = C_WQ1 + KT
        C_EX = C_WOUT + KT
        C_ALL = C_EX + NE * KT

        Wq_v = Wq.rearrange("(k p) n -> k p n", p=P)
        Wo_v = Wo.rearrange("(h p) n -> h p n", p=P)
        up_v = up_w.rearrange("(k p) n -> p k n", p=P)
        down_v = down_w.rearrange("(k p) n -> p k n", p=P)
        fc1_v = fc1_w.rearrange("(k p) n -> p k n", p=P)
        fc2_v = fc2_w.rearrange("(k p) n -> p k n", p=P)
        lat_v = latent_w.rearrange("(k p) n -> p k n", p=P)
        wq1_v = wqT.rearrange("(k p) n -> p k n", p=P)
        wout_v = woutT.rearrange("(k p) n -> p k n", p=P)
        ex_v = expertT.rearrange("e (k p) n -> e k p n", p=P)
        ctx_v = ctxT.rearrange("(k p) t -> p k t", p=P)
        Wk_v = Wk.rearrange("(k p) n -> p k n", p=P)
        Wv_v = Wv.rearrange("(k p) n -> p k n", p=P)

        def raw_as(c, parts):
            return raw[:, c % 4, :].rearrange("p (k n) -> p k n", k=parts)

        def mlp_chunk(c):
            if c < C_FC:
                k, n = (c - C_UP) // 2, (c - C_UP) % 2 * 512
                return up_v[:, k, n:n + 512], up_r[:, 0, k, n:n + 512], up_r[:, 1, k, n:n + 512], raw[:, c % 4, :]
            if c < C_FC + 2:
                k = (c - C_FC) * 2
                return fc1_v[:, k:k + 2, :], fc1_r[:, 0, k:k + 2, :], fc1_r[:, 1, k:k + 2, :], raw_as(c, 2)
            if c < C_FC + 3:
                return lat_v, lat_r[:, 0], lat_r[:, 1], raw_as(c, 2)
            if c < C_DOWN:
                k = c - C_FC - 3
                return fc2_v[:, k, :], fc2_r[:, 0, k, :], fc2_r[:, 1, k, :], raw[:, c % 4, :]
            if c < C_WQ1:
                k = c - C_DOWN
                return down_v[:, k, :], down_r[:, 0, k, :], down_r[:, 1, k, :], raw[:, c % 4, :]
            if c < C_WOUT:
                k = c - C_WQ1
                return wq1_v[:, k, :], wq1_r[:, 0, k, :], wq1_r[:, 1, k, :], raw[:, c % 4, :]
            k = c - C_WOUT
            return wout_v[:, k, :], wout_r[:, 0, k, :], wout_r[:, 1, k, :], raw[:, c % 4, :]

        def first_chunk(a):
            k, kind = a % 4, a // 4
            if kind == 0:
                return Wk_v[:, k, :], Wk_r[:, 0, k, :], Wk_r[:, 1, k, :]
            if kind == 2:
                return Wv_v[:, k, :], Wv_r[:, 0, k, :], Wv_r[:, 1, k, :]
            t = 0 if kind == 1 else 512
            return ctx_v[:, k, t:t + 512], CT[:, 0, k, t:t + 512], CT[:, 1, k, t:t + 512]

        def f32(ap):
            return ap.bitcast(F32)

        def product(pe, acc, w, m, first, last):
            pe.matmul(acc, w[0], m[0], start=first, stop=False)
            pe.matmul(acc, w[0], m[1], start=False, stop=False)
            return pe.matmul(acc, w[1], m[0], start=False, stop=last)

        def contract(pe, acc, pairs):
            for n, (w, m) in enumerate(pairs):
                mm = product(pe, acc, w, m, n == 0, n == len(pairs) - 1)
            return mm

        def hilo(buf, *at):
            return buf[(slice(None), 0) + at], buf[(slice(None), 1) + at]

        def steps_of(eng, step):
            for c in range(B):
                step(0, c)
            with eng.Fori(0, 3) as i:
                for c in range(B, B + 16):
                    step(i, c)
            for c in range(B, B + 10):
                step(3, c)

        def number(i, c):
            return 16 * i + c if isinstance(i, int) else None

        def step_chunk(c):
            k, at = c % B, (c // B + 1) % 2
            return hilo(Wq_r[:, at], k) if k < KT else hilo(Wo_r[:, at], k - KT)

        def lnbank(t):
            return bank[6 + t % 2] if t < 3 * B else bank[4]

        A = slice(None)
        block = ctx.enter_context(nc.Block())

        @block.sync
        def _(sp):
            def load_first(a):
                if a >= 8:
                    sp.wait_ge(a_lo, a - 7)
                sp.dma_start(work[:, a % 8, :], first_chunk(a)[0]).then_inc(a_loaded[a % 8], 16)

            def load_raw(c, src, dst=None):
                if c >= 4:
                    sp.wait_ge(chunk_split, c - 3)
                sp.dma_start(raw[:, c % 4, :] if dst is None else dst, src).then_inc(raw_loaded[c % 4], 16)

            def load_late(c):
                src, _, _, dst = mlp_chunk(c)
                load_raw(c, src, dst)

            for a in range(8):
                load_first(a)
            for g, src in enumerate((g_xattn, g_ffn)):
                sp.dma_start(graw[:, 2 * g:2 * g + 2], src.rearrange("(a n) -> a n", a=1).broadcast_to([P, 2])
                             ).then_inc(small_loaded, 16)
            sp.dma_start(graww[:, 0], gate0.rearrange("(k p) n -> p k n", p=P)).then_inc(small_loaded, 16)
            sp.dma_start(graww[:, 1], gate1T.rearrange("(k p) n -> p k n", p=P)).then_inc(small_loaded, 16)
            sp.dma_start(gb1[:, :], gate1_b.rearrange("(a n) -> a n", a=1).broadcast_to([P, NE])
                         ).then_inc(small_loaded, 16)
            sp.dma_start(mask8[:, :], mask).then_inc(small_loaded, 16)
            for a in range(8, NA):
                load_first(a)
            load_raw(0, wkT.rearrange("(k p) n -> p k n", p=P), raw_as(0, KT))
            load_raw(1, wvT.rearrange("(k p) n -> p k n", p=P), raw_as(1, KT))
            for k in range(KT):
                load_raw(C_WQ0 + k, Wq_v[k, :, 0:512])
            for n, job in enumerate(JOBS):
                if job[0] not in ("K", "V"):
                    continue
                s = STORE[n]
                sp.wait_ge(kv_lo, LOS[n])
                for part in range(2):
                    if job[0] == "K":
                        _, cl, h, half = job
                        dst = Kscr[h, half * HALF:(half + 1) * HALF, :, part, cl * P:(cl + 1) * P].rearrange("b p t -> p b t")
                        src = stage[:, s % 4, part, :].rearrange("p (b t) -> p b t", b=HALF)
                    else:
                        _, cl, b = job
                        dst = Vscr[:, b, :, part, cl, :].rearrange("h p n -> p h n")
                        src = stage[:, s % 4, part, :].rearrange("p (h n) -> p h n", h=KVH)
                    sp.dma_start(dst, f32(src)).then_inc(kv_stored[s % 4], 16)
            sp.dma_start(gam, ln_gamma.rearrange("(a n) -> a n", a=1).broadcast_to([P, D])).then_inc(gb_loaded, 16)
            sp.dma_start(bet, ln_beta.rearrange("(a n) -> a n", a=1).broadcast_to([P, D])).then_inc(gb_loaded, 16)
            for k in range(QUAD):
                load_raw(C_WO0 + k, Wo_v[k])

            def load_K(i, c):
                src = Kscr[bass.ds(i + c // 16, 1), c % B].rearrange("a p s t -> (a p) s t")
                sp.dma_start(f32(Kb[:, c % 2]), src).then_inc(k_loaded[c % 2], 16)

            def load_V(i, c):
                src = Vscr[bass.ds(i + c // 16, 1), c % B].rearrange("a p s k n -> (a p) s k n")
                sp.dma_start(f32(Vb[:, c % 2]), src).then_inc(v_loaded[c % 2], 16)

            def load_step_chunk(i, c):
                j1, k = c // B + 1, c % B
                if k < KT:
                    src = Wq_v[k, :, bass.ds(1024 * i + 512 * j1, 512)]
                else:
                    src = Wo_v[bass.ds(8 * i + QUAD * j1 + k - KT, 1)].rearrange("a p n -> (a p) n")
                sp.wait_ge(chunk_split, C_STEP + 16 * i + c - 3)
                sp.dma_start(raw[:, (C_STEP + c) % 4, :], src).then_inc(raw_loaded[(C_STEP + c) % 4], 16)

            for s in range(4):
                sp.wait_ge(kv_stored[s], 16 * 2 * 8)
            load_K(0, 0)

            def step(i, c):
                n = number(i, c)
                if n is None or n < STEPS:
                    if n is None or n >= 2:
                        sp.wait_ge(o_mm, 16 * i + c - 1)
                    load_V(i, c)
                if n is None or n + 1 < STEPS:
                    if n is None or n >= 1:
                        sp.wait_ge(s_mm, 2 * (16 * i + c))
                    load_K(i, c + 1)
                if n is None or n < STEPS - B:
                    load_step_chunk(i, c)
                elif n < STEPS:
                    load_late(C_UP + n - (STEPS - B))

            steps_of(sp, step)
            for c in range(C_UP + 8, C_EX):
                load_late(c)

            def load_expert(c):
                e, k = (c - C_EX) // KT, (c - C_EX) % KT
                load_raw(c, ex_v[e, k])

            for k in range(KT):
                load_expert(C_EX + k)
            sp.wait_ge(kb_zero, 1)
            for u in range(B * M1):
                b, m = u // M1, u % M1
                if u >= M1:
                    sp.wait_ge(s1_mm, u - M1 + 1)
                for h in range(HT1):
                    g = (m * HT1 + h) // (H1 // G1)
                    sp.dma_start(f32(KB[D1 * h:D1 * (h + 1), m, :, h, :]), f32(KT1[D1 * g:D1 * (g + 1), :, b * P:(b + 1) * P])
                                 ).then_inc(kb_loaded[m], 16)
                if u == 2 * M1:
                    for k in range(KT):
                        load_expert(C_EX + KT + k)
            sp.wait_ge(s1_exp, B * M1)
            sp.wait_ge(p1_T, B * M1)
            sp.dma_start(work[0:NE, 0, :], expert_b).then_inc(eb_loaded, 16)
            for c in range(C_EX + 2 * KT, C_ALL):
                load_expert(c)
            for b in range(B):
                sp.wait_ge(e_acc, (NE - 1) * B + b + 1)
                sp.dma_start(out[b], X[:, b, :]).then_inc(out_stored, 16)
            sp.wait_ge(out_stored, 16 * B)

        @block.gpsimd
        def _(pool):
            made = [0]

            def link(ins):
                made[0] += 1
                ins.then_inc(consts_made, 1)
                pool.wait_ge(consts_made, made[0])

            link(pool.memset(ident[:, :], 0.0))
            link(pool.affine_select(out=ident[:, :], in_=ident[:, :], compare_op=ALU.not_equal, fill=1.0, base=0,
                                    pattern=[[-1, P]], channel_multiplier=1))
            link(pool.iota(iota8[:, :], pattern=[[1, NE]], base=0, channel_multiplier=0,
                           allow_small_or_imprecise_dtypes=True))
            link(pool.memset(mhalf[:, :], -0.5))
            link(pool.memset(V1[:, :, :, :], 1.0))

            def ln_power(t):
                b = t % B
                pool.wait_ge(ln_stat, t + 1)
                pool.tensor_tensor(rstd[:, b:b + 1], vareps[:, b:b + 1], mhalf[:, :], ALU.pow).then_inc(ln_rstd, 1)

            own = [0]

            def split(src, hi, lo):
                pool.tensor_copy(hi, src).then_inc(chunk_hi, 1)
                own[0] += 1
                pool.wait_ge(chunk_hi, own[0])
                pool.tensor_tensor(lo, src, f32(hi), ALU.subtract).then_inc(chunk_split, 1)

            def split_static(c, src, hi, lo):
                pool.wait_ge(raw_loaded[c % 4], 16 * (c // 4 + 1))
                split(src, hi, lo)

            def split_late(c):
                _, hi, lo, src = mlp_chunk(c)
                split_static(c, src, hi, lo)

            for t in range(4):
                ln_power(t)
            split_static(0, raw_as(0, KT), wk1_r[:, 0], wk1_r[:, 1])
            split_static(1, raw_as(1, KT), wv1_r[:, 0], wv1_r[:, 1])
            for t in range(4, B):
                ln_power(t)
            for k in range(KT):
                c = C_WQ0 + k
                split_static(c, raw[:, c % 4, :], Wq_r[:, 0, 0, k, :], Wq_r[:, 0, 1, k, :])
            pool.wait_ge(kv_mm, len(JOBS))
            for h in range(QUAD):
                c = C_WO0 + h
                split_static(c, raw[:, c % 4, :], Wo_r[:, 0, 0, h, :], Wo_r[:, 0, 1, h, :])

            def step(i, c):
                n = number(i, c)
                if n is not None and n >= STEPS - 5 and n - (STEPS - 5) < B:
                    ln_power(B + n - (STEPS - 5))
                if n is None or n < STEPS:
                    pr = prob[:, c % 2, :].rearrange("p (h t) -> p h t", h=QUAD)
                    pool.wait_ge(s_rcp, 16 * i + c + 1)
                    pool.tensor_tensor(pr, pr, rinv[:, c % 2, :].unsqueeze(2).broadcast_to([P, QUAD, KEYS]), ALU.mult
                                       ).then_inc(p_norm, 1)
                if n is None or n < STEPS - B:
                    hi, lo = step_chunk(c)
                    pool.wait_ge(step_hi, 16 * i + c + 1)
                    pool.tensor_tensor(lo, raw[:, (C_STEP + c) % 4, :], f32(hi), ALU.subtract).then_inc(chunk_split, 1)
                if n is not None and STEPS - 4 <= n < STEPS:
                    pool.wait_ge(q_mm, STEPS)
                    for k in range(2):
                        split_late(C_UP + 2 * (n - (STEPS - 4)) + k)

            steps_of(pool, step)
            ln_power(2 * B - 1)

            pool.wait_ge(o_mm, STEPS)
            split_late(C_FC)
            split_late(C_FC + 1)
            pool.wait_ge(y_mm, STEPS)
            for k in range(2, 5):
                split_late(C_FC + k)

            def act_low(u):
                pool.wait_ge(m_sq_hi, u + 1)
                pool.tensor_tensor(actT[:, 1, u % IT, :], hrow[:, u % 2, :], f32(actT[:, 0, u % IT, :]), ALU.subtract
                                   ).then_inc(m_sq_lo, 1)

            def z_power(b):
                pool.wait_ge(z_stat, b + 1)
                pool.tensor_tensor(zrs[:, b:b + 1], zve[:, b:b + 1], mhalf[:, :], ALU.pow).then_inc(z_rstd, 1)

            split_late(C_DOWN)
            split_late(C_DOWN + 1)
            for u in range(IT):
                act_low(u)
                if u < 6:
                    split_late(C_DOWN + 2 + u)
            pool.wait_ge(gb_made, 2)
            pool.wait_ge(ln_row, 2 * B)
            for b in range(B):
                pool.tensor_tensor(X[:, b, :], X[:, b, :], bet, ALU.add).then_inc(xbeta, 1)
            for b in range(HALF):
                z_power(b)
                ln_power(2 * B + b)
            for u in range(IT, 2 * IT):
                act_low(u)
            pool.wait_ge(m_up, 2 * IT)
            for b in range(HALF, B):
                for k in range(2):
                    split_late(C_WQ1 + 2 * (b - HALF) + k)
                z_power(b)
                ln_power(2 * B + b)
            pool.wait_ge(m_down, B)
            pool.memset(f32(region(RB, 8192)), 0.0).then_inc(kb_zero, 1)

            def split_expert(c):
                e, k = (c - C_EX) // KT, (c - C_EX) % KT
                split_static(c, raw[:, c % 4, :], Ex[e % 2][:, 0, k, :], Ex[e % 2][:, 1, k, :])

            pool.wait_ge(q1_mm, 2 * M1)
            for k in range(KT):
                split_expert(C_EX + k)
            for b in range(B - 1):
                ln_power(3 * B + b)
            pool.wait_ge(s1_mm, B * M1)
            for k in range(KT):
                split_expert(C_EX + KT + k)
            ln_power(4 * B - 1)

            with pool.Fori(1, NE // 2) as i:
                for par in range(2):
                    for k in range(KT):
                        c0 = C_EX + KT * par + k
                        pool.wait_ge(ex_hi, 8 * i + KT * par + k - 7)
                        pool.tensor_tensor(Ex[par][:, 1, k, :], raw[:, c0 % 4, :], f32(Ex[par][:, 0, k, :]), ALU.subtract
                                           ).then_inc(chunk_split, 1)

        @block.scalar
        def _(act):
            for b in range(B):
                act.dma_start(X[:, b, :], x[b]).then_inc(x_loaded[b], 16)
            act.wait_ge(small_loaded, 16 * 6)
            act.activation(gate[:, :], graw[:, :], ACT.Tanh).then_inc(gates_tanh, 1)
            for l in range(2):
                act.copy(gw[:, l, 0], graww[:, l]).then_inc(gatew_hi, 1)

            def first_hi(a):
                act.wait_ge(a_loaded[a % 8], 16 * (a // 8 + 1))
                act.copy(first_chunk(a)[1], work[:, a % 8, :]).then_inc(a_hi, 1)

            def job_hi(n):
                kind = JOBS[n][0]
                act.wait_ge(kv_mm, n + 1)
                if kind in ("K", "V"):
                    s = STORE[n]
                    if s >= 4:
                        act.wait_ge(kv_stored[s % 4], 32 * (s // 4))
                    dst, src = stage[:, s % 4, 0, :], bank[n % 4]
                elif kind == "k1":
                    t = JOBS[n][1] * 512
                    dst, src = KT1[:, 0, t:t + 512], bank[n % 4]
                elif kind == "v1":
                    dst, src = work[:, 6 + JOBS[n][1], :], bank[n % 4]
                else:
                    half = JOBS[n][1]
                    dst = V1[:, half * HALF:(half + 1) * HALF, :, 0:D1]
                    src = bank[n % 4].rearrange("p (b g d) -> p b g d", b=HALF, g=G1)
                    act.wait_ge(consts_made, 5)
                act.copy(dst, src).then_inc(kv_hi, 1)

            def ln_high(t):
                b = t % B
                act.wait_ge(ln_T, t + 1)
                act.copy(HT[:, 0, :, b * P:(b + 1) * P], lnbank(t).rearrange("p (k t) -> p k t", k=KT)).then_inc(ln_hi, 1)

            for a in range(12):
                first_hi(a)
            job_hi(0)
            job_hi(1)
            first_hi(12)
            first_hi(13)
            job_hi(2)
            first_hi(14)
            first_hi(15)
            job_hi(3)
            job_hi(4)
            for b in range(B):
                ln_high(b)
                job_hi(5 + b)
            for n in range(5 + B, len(JOBS)):
                job_hi(n)

            def q_high(index, h, half):
                act.wait_ge(q_mm, index + 1)
                act.activation(qT[:, half, 0, h, :], bank[6 + h % 2], ACT.Copy, scale=SCALE0).then_inc(q_hi, 1)

            for h in range(QUAD):
                q_high(h, h, 0)

            def step(i, c):
                n = number(i, c)
                if n is None or n >= 2:
                    act.wait_ge(o_mm, 16 * i + c - 1)
                    act.copy(OT[:, 0, :], bank[4]).then_inc(o_hi, 1)
                if n is not None and n >= STEPS - 4:
                    ln_high(B + n - (STEPS - 4))
                if n is None or n < STEPS:
                    for h in range(QUAD):
                        if h % 2 == 0:
                            act.wait_ge(s_max, 2 * (16 * i + c) + h // 2 + 1)
                        if h == 0 and (n is None or n >= 2):
                            act.wait_ge(p_T, 2 * (16 * i + c - 1))
                        e = act.activation(prob[:, c % 2, h * KEYS:(h + 1) * KEYS],
                                           bank[h // 2][:, (h % 2) * KEYS:(h % 2 + 1) * KEYS], ACT.Exp,
                                           bias=nmax[:, c % 2, h:h + 1], accum_out=psumr[:, c % 2, h:h + 1])
                        if h % 2:
                            e.then_inc(s_exp, 1)
                if n is None or n < STEPS - QUAD:
                    act.wait_ge(q_mm, 16 * i + c + QUAD + 1)
                    act.activation(qT[:, (c // QUAD + 1) % 2, 0, c % QUAD, :], bank[6 + c % 2], ACT.Copy,
                                   scale=SCALE0).then_inc(q_hi, 1)
                if (n is None or n >= 1) and (n is None or n <= STEPS):
                    for k in range(2):
                        act.wait_ge(p_T, 2 * (16 * i + c - 1) + k + 1)
                        act.copy(PT[:, 0, k, :], bank[2 + k]).then_inc(pt_hi, 1)
                if n is None or n < STEPS - B:
                    if n is None:
                        act.wait_ge(q_mm if c % B < KT else y_mm, 16 * i + B * (c // B))
                    elif c == 0:
                        act.wait_ge(kv_mm, len(JOBS))
                    slot = (C_STEP + c) % 4
                    act.wait_ge(raw_loaded[slot], 64 * i + 16 * ((C_STEP + c) // 4 + 1))
                    act.copy(step_chunk(c)[0], raw[:, slot, :]).then_inc(step_hi, 1)

            steps_of(act, step)
            for t in (2 * B - 2, 2 * B - 1):
                ln_high(t)

            for half in range(2):
                for k in range(LT):
                    act.wait_ge(m_xl, 4 * half + k + 1)
                    act.copy(xlT[:, 0, k, :], bank[k]).then_inc(m_xl_hi, 1)
                if half:
                    ln_high(2 * B + 3)
                for k in range(LT):
                    act.wait_ge(m_xl, 4 * half + LT + k + 1)
                    act.copy(eoT[:, 0, k, :], bank[2 + k]).then_inc(m_xl_hi, 1)

                def act_high(u):
                    act.wait_ge(m_sq, u + 1)
                    act.copy(actT[:, 0, u % IT, :], hrow[:, u % 2, :]).then_inc(m_sq_hi, 1)

                for u in range(IT * half, IT * half + IT):
                    act.wait_ge(m_up, u + 1)
                    if u % IT < 2:
                        act.wait_ge(ln_T, 2 * B + 4 * half)
                    if u >= 2:
                        act.wait_ge(m_sq_lo, u - 1)
                    act.activation(hrow[:, u % 2, :], bank[u % 4], ACT.Relu).then_inc(m_relu, 1)
                    if u % IT:
                        act_high(u - 1)
                act_high(IT * half + IT - 1)
                if not half:
                    for b in range(3):
                        ln_high(2 * B + b)

            def q1_high(n):
                half, m = n // M1, n % M1
                act.wait_ge(q1_mm, n + 1)
                act.activation(qT1[:, 0, m, half * 512:half * 512 + 512], bank[n % 4], ACT.Copy, scale=SCALE1
                               ).then_inc(q1_hi, 1)

            for b in (4, 5):
                ln_high(2 * B + b)
            for n in range(M1):
                q1_high(n)
            for b in (6, 7):
                ln_high(2 * B + b)
            for n in range(M1, 2 * M1):
                q1_high(n)
            for u in range(B * M1 + 8):
                if u < B * M1:
                    act.wait_ge(s1_sub, u + 1)
                    act.activation(prob[:, u % 2, :], prob[:, u % 2, :], ACT.Exp).then_inc(s1_exp, 1)
                if 1 <= u <= B * M1:
                    act.wait_ge(p1_T, u)
                    if u >= 3:
                        act.wait_ge(o1_mm, u - 2)
                    act.copy(probT[:, (u - 1) % 2, :], PS[:, 4:6, :].rearrange("p a c -> p (a c)")).then_inc(p1_copy, 1)
                if u >= 7 and (u - 7) % M1 == 0 and (u - 7) // M1 < B:
                    b = (u - 7) // M1
                    act.wait_ge(o1_T, b + 1)
                    act.copy(OT1[:, b % 2, 0], bank[4].rearrange("p (k t) -> p k t", k=KT)).then_inc(o1_hi, 1)
                if u >= 10 and (u - 10) % M1 == 0 and (u - 10) // M1 < B:
                    ln_high(3 * B + (u - 10) // M1)
            act.wait_ge(g1_T, 1)
            act.wait_ge(eb_loaded, 16)
            act.copy(work[0:NE, 1:3, :], PS[0:NE, 6:8, :]).then_inc(g1_copy, 1)
            with act.Fori(1, NE // 2) as i:
                for par in range(2):
                    act.wait_ge(e_mm, 16 * i + B * par - B)
                    for k in range(KT):
                        c0 = C_EX + KT * par + k
                        act.wait_ge(raw_loaded[c0 % 4], 32 * i + 16 * (c0 // 4 + 1))
                        act.copy(Ex[par][:, 0, k, :], raw[:, c0 % 4, :]).then_inc(ex_hi, 1)

        @block.vector
        def _(dve):
            links = [0]

            def link(ins):
                links[0] += 1
                ins.then_inc(chain, 1)
                dve.wait_ge(chain, links[0])

            def first_lo(a):
                _, hi, lo = first_chunk(a)
                dve.wait_ge(a_hi, a + 1)
                dve.tensor_tensor(lo, work[:, a % 8, :], f32(hi), ALU.subtract).then_inc(a_lo, 1)

            def ln_stats(t):
                b = t % B
                if t < B:
                    dve.wait_ge(x_loaded[b], 16)
                link(dve.bn_stats(stats[:, t % 2, :], X[:, b, :]))
                link(dve.bn_aggr(meanvar[:, b, :], stats[:, t % 2, :]))
                dve.tensor_scalar(vareps[:, b:b + 1], meanvar[:, b, 1:2], LN_EPS, None, ALU.add).then_inc(ln_stat, 1)

            def ln_rows(t):
                b = t % B
                dve.wait_ge(ln_rstd, t + 1)
                if t % B >= 2:
                    dve.wait_ge(ln_T, t - 1)
                dve.tensor_scalar(hrow[:, t % 2, :], X[:, b, :], meanvar[:, b, 0:1], rstd[:, b:b + 1],
                                  ALU.subtract, ALU.mult).then_inc(ln_row, 1)

            def ln_low(t):
                b = t % B
                hi, lo = hilo(HT, A, slice(b * P, (b + 1) * P))
                dve.wait_ge(ln_hi, t + 1)
                dve.tensor_tensor(lo, lnbank(t).rearrange("p (k t) -> p k t", k=KT), f32(hi), ALU.subtract).then_inc(ln_lo, 1)

            def job_lo(n):
                if not HAS_LO[n]:
                    return
                dve.wait_ge(kv_hi, n + 1)
                if JOBS[n][0] == "k1":
                    t = JOBS[n][1] * 512
                    hi, lo = hilo(KT1, slice(t, t + 512))
                else:
                    hi, lo = stage[:, STORE[n] % 4, 0, :], stage[:, STORE[n] % 4, 1, :]
                dve.tensor_tensor(lo, bank[n % 4], f32(hi), ALU.subtract).then_inc(kv_lo, 1)

            dve.wait_ge(consts_made, 2)
            dve.tensor_copy(identr, ident[:, :]).then_inc(identr_made, 1)
            for a in range(8):
                first_lo(a)
            for l in range(2):
                dve.wait_ge(gatew_hi, l + 1)
                dve.tensor_tensor(gw[:, l, 1], graww[:, l], f32(gw[:, l, 0]), ALU.subtract).then_inc(gatew_lo, 1)
            ln_stats(0)
            ln_stats(1)
            for a in range(8, 12):
                first_lo(a)
            ln_rows(0)
            ln_rows(1)
            ln_stats(2)
            ln_stats(3)
            job_lo(0)
            job_lo(1)
            first_lo(12)
            first_lo(13)
            job_lo(2)
            first_lo(14)
            first_lo(15)
            job_lo(3)
            for t in range(4, B):
                ln_stats(t)
            job_lo(4)
            for b in range(B):
                ln_low(b)
                if b + 2 < B:
                    ln_rows(b + 2)
                job_lo(5 + b)
            for n in range(5 + B, len(JOBS)):
                job_lo(n)

            def q_low(index, h, half):
                dve.wait_ge(q_hi, index + 1)
                dve.scalar_tensor_tensor(out=qT[:, half, 1, h, :], in0=bank[6 + h % 2], scalar=SCALE0,
                                         in1=f32(qT[:, half, 0, h, :]), op0=ALU.mult, op1=ALU.subtract).then_inc(q_lo, 1)

            for h in range(QUAD):
                q_low(h, h, 0)
            dve.wait_ge(gates_tanh, 1)
            dve.wait_ge(gb_loaded, 32)
            for v in (gam, bet):
                dve.tensor_scalar(v, v, gate[:, 2:3], None, ALU.mult).then_inc(gb_made, 1)

            def maxima(i, c, k):
                dve.wait_ge(s_mm, 2 * (16 * i + c) + k + 1)
                dve.tensor_reduce(nmax[:, c % 2, 2 * k:2 * k + 2], bank[k].rearrange("p (h t) -> p h t", h=2),
                                  AX_X, ALU.max, negate=True).then_inc(s_max, 1)

            def step(i, c):
                n = number(i, c)
                if n is None or n < STEPS:
                    maxima(i, c, 0)
                if n is None or n >= 2:
                    dve.wait_ge(o_hi, 16 * i + c - 1)
                    dve.tensor_tensor(OT[:, 1, :], bank[4], f32(OT[:, 0, :]), ALU.subtract).then_inc(o_lo, 1)
                if n is not None and n >= STEPS - 4:
                    ln_low(B + n - (STEPS - 4))
                if n is None or n < STEPS:
                    maxima(i, c, 1)
                if n is not None and n >= STEPS - 5:
                    ln_rows(B + n - (STEPS - 5))
                if n is None or n < STEPS:
                    dve.wait_ge(s_exp, 2 * (16 * i + c) + 2)
                    dve.reciprocal(rinv[:, c % 2, :], psumr[:, c % 2, :]).then_inc(s_rcp, 1)
                if n is None or n < STEPS - QUAD:
                    h, at = c % QUAD, (c // QUAD + 1) % 2
                    dve.wait_ge(q_hi, 16 * i + c + QUAD + 1)
                    dve.scalar_tensor_tensor(out=qT[:, at, 1, h, :], in0=bank[6 + c % 2], scalar=SCALE0,
                                             in1=f32(qT[:, at, 0, h, :]), op0=ALU.mult, op1=ALU.subtract).then_inc(q_lo, 1)
                if (n is None or n >= 1) and (n is None or n <= STEPS):
                    for k in range(2):
                        dve.wait_ge(pt_hi, 2 * (16 * i + c - 1) + k + 1)
                        dve.tensor_tensor(PT[:, 1, k, :], bank[2 + k], f32(PT[:, 0, k, :]), ALU.subtract).then_inc(pt_lo, 1)
                if n is None or n >= 2:
                    dve.wait_ge(y_mm, 16 * i + c - 1)
                    b = (c - 2) % B
                    dve.scalar_tensor_tensor(out=X[:, b, :], in0=bank[5], scalar=gate[:, 0:1], in1=X[:, b, :],
                                             op0=ALU.mult, op1=ALU.add).then_inc(y_acc, 1)
                if n is not None and n >= STEPS - 6:
                    dve.wait_ge(y_acc, n - 1)
                    ln_stats(B + n - (STEPS - 6))

            steps_of(dve, step)
            ln_low(2 * B - 2)
            ln_rows(2 * B - 1)
            ln_low(2 * B - 1)

            def z_part(b):
                dve.wait_ge(m_down, b + 1)
                link(dve.tensor_tensor(zrow[:, b % 2, :], bank[4 + b % 2], work[:, b % HALF, :], ALU.add))
                link(dve.bn_stats(stats[:, b % 2, :], zrow[:, b % 2, :]))
                link(dve.bn_aggr(zmv[:, b, :], stats[:, b % 2, :]))
                dve.tensor_scalar(zve[:, b:b + 1], zmv[:, b, 1:2], LN_EPS, None, ALU.add).then_inc(z_stat, 1)

            def z_add(b):
                z = zrow[:, b % 2, :]
                dve.wait_ge(z_rstd, b + 1)
                link(dve.tensor_scalar(z, z, zmv[:, b, 0:1], zrs[:, b:b + 1], ALU.subtract, ALU.mult))
                link(dve.tensor_tensor(z, z, gam, ALU.mult))
                dve.wait_ge(xbeta, b + 1)
                link(dve.tensor_tensor(X[:, b, :], X[:, b, :], z, ALU.add))
                ln_stats(2 * B + b)

            for half in range(2):
                dve.wait_ge(m_gate, half + 1)
                for b in range(HALF):
                    t8 = dve.max(top0[:, b, :], bank[3][:, b * NE:(b + 1) * NE])
                link(t8)
                dve.tensor_tensor(route[:, half * HALF:(half + 1) * HALF].unsqueeze(2), top0[:, :, 0:1], top0[:, :, 1:2],
                                  ALU.add).then_inc(m_route, 1)
                for k in range(LT):
                    dve.wait_ge(m_xl_hi, 4 * half + k + 1)
                    dve.tensor_tensor(xlT[:, 1, k, :], bank[k], f32(xlT[:, 0, k, :]), ALU.subtract).then_inc(m_xl_lo, 1)
                if half:
                    ln_low(2 * B + 3)
                for k in range(LT):
                    dve.wait_ge(m_xl_hi, 4 * half + LT + k + 1)
                    dve.tensor_tensor(eoT[:, 1, k, :], bank[2 + k], f32(eoT[:, 0, k, :]), ALU.subtract).then_inc(m_xl_lo, 1)
                dve.wait_ge(m_route, half + 1)
                for b in range(HALF):
                    r = half * HALF + b
                    dve.wait_ge(m_fc2, r + 1)
                    dve.tensor_scalar(work[:, b, :], bank[4 + b % 2], route[:, r:r + 1], None, ALU.mult).then_inc(m_fc2_out, 1)
                for u in range(IT * half, IT * half + IT):
                    dve.wait_ge(m_relu, u + 1)
                    dve.tensor_tensor(hrow[:, u % 2, :], hrow[:, u % 2, :], hrow[:, u % 2, :], ALU.mult).then_inc(m_sq, 1)
                if half:
                    for h in range(4):
                        dve.tensor_scalar(maskr[:, h * P:(h + 1) * P], mask8[:, :], 1.0, -MASKED, ALU.subtract, ALU.mult
                                          ).then_inc(mask_made, 1)
                    z_part(4)
                    z_add(4)
                    z_part(5)
                    z_add(5)
                    ln_rows(2 * B + 4)
                    z_part(6)
                    z_add(6)
                    ln_rows(2 * B + 5)
                    ln_low(2 * B + 4)
                    z_part(7)
                    z_add(7)
                    ln_low(2 * B + 5)
                    ln_rows(2 * B + 6)
                    ln_rows(2 * B + 7)
                else:
                    for b in range(HALF):
                        z_part(b)
                        z_add(b)
                        if 1 <= b <= 2:
                            ln_rows(2 * B + b - 1)
                    ln_rows(2 * B + 2)
                    ln_low(2 * B)
                    ln_low(2 * B + 1)
                    ln_rows(2 * B + 3)
                    ln_low(2 * B + 2)

            def q1_low(n):
                half, m = n // M1, n % M1
                hi, lo = hilo(qT1, m, slice(half * 512, half * 512 + 512))
                dve.wait_ge(q1_hi, n + 1)
                dve.scalar_tensor_tensor(out=lo, in0=bank[n % 4], scalar=SCALE1, in1=f32(hi),
                                         op0=ALU.mult, op1=ALU.subtract).then_inc(q1_lo, 1)

            for n in range(M1):
                q1_low(n)
            ln_low(2 * B + 6)
            ln_low(2 * B + 7)
            for n in range(M1, 2 * M1):
                q1_low(n)
            for u in range(B * M1 + 8):
                if u < B * M1:
                    sc = PS[:, 2 * (u % 2):2 * (u % 2) + 2, :].rearrange("p a (h t) -> p (a h) t", h=4)
                    dve.wait_ge(s1_mm, u + 1)
                    dve.tensor_reduce(max1[:, u % 2, :], sc, AX_X, ALU.max).then_inc(s1_max, 1)
                    dve.wait_ge(s1_max, u + 1)
                    if u >= 2:
                        dve.wait_ge(p1_T, u - 1)
                    dve.tensor_tensor(prob[:, u % 2, :].rearrange("p (h t) -> p h t", h=HT1), sc,
                                      max1[:, u % 2, :].unsqueeze(2).broadcast_to([P, HT1, P]), ALU.subtract).then_inc(s1_sub, 1)
                v = u - 3
                if 0 <= v < B * M1 and v % 2:
                    b, half = v // M1, v % M1 // 2
                    o = bank[6 + half][:, 0:16 * (D1 + 1)].rearrange("p (h d) -> p h d", h=16)
                    dve.wait_ge(o1_mm, v + 1)
                    link(dve.reciprocal(rsum1[:, half, :].unsqueeze(2), o[:, :, D1:D1 + 1]))
                    if half == 0 and b >= 2:
                        dve.wait_ge(ln_T, 3 * B + b - 1)
                    dve.tensor_tensor(hrow[:, b % 2, half * 256:half * 256 + 256].rearrange("p (h d) -> p h d", h=16),
                                      o[:, :, 0:D1], rsum1[:, half, :].unsqueeze(2).broadcast_to([P, 16, D1]), ALU.mult
                                      ).then_inc(o1_row, 1)
                if u >= 8 and (u - 8) % M1 == 0 and (u - 8) // M1 < B:
                    b = (u - 8) // M1
                    dve.wait_ge(o1_hi, b + 1)
                    dve.tensor_tensor(OT1[:, b % 2, 1], bank[4].rearrange("p (k t) -> p k t", k=KT), f32(OT1[:, b % 2, 0]),
                                      ALU.subtract).then_inc(o1_lo, 1)
                if u >= 9 and (u - 9) % M1 == 0 and (u - 9) // M1 < B:
                    b = (u - 9) // M1
                    dve.wait_ge(y1_mm, b + 1)
                    dve.scalar_tensor_tensor(out=X[:, b, :], in0=bank[5], scalar=gate[:, 1:2], in1=X[:, b, :],
                                             op0=ALU.mult, op1=ALU.add).then_inc(y1_acc, 1)
                    dve.wait_ge(y1_acc, b + 1)
                    ln_stats(3 * B + b)
                if u >= 10 and (u - 10) % M1 == 0 and (u - 10) // M1 < B:
                    b = (u - 10) // M1
                    dve.wait_ge(ln_rstd, 3 * B + b + 1)
                    dve.wait_ge(o1_T, b + 1)
                    dve.tensor_scalar(hrow[:, b % 2, :], X[:, b, :], meanvar[:, b, 0:1], rstd[:, b:b + 1],
                                      ALU.subtract, ALU.mult).then_inc(ln_row, 1)
                if u >= 11 and (u - 11) % M1 == 0 and (u - 11) // M1 < B:
                    ln_low(3 * B + (u - 11) // M1)

            dve.wait_ge(g1_mm, 1)
            link(dve.tensor_tensor(logit1[:, :, :], bank[6][:, 0:B * NE].rearrange("p (b e) -> p b e", b=B),
                                   gb1[:, :].unsqueeze(1).broadcast_to([P, B, NE]), ALU.add))
            for b in range(B):
                t8 = dve.max(top1[:, b, :], logit1[:, b, :])
            link(t8)
            for b in range(B):
                t8 = dve.max_index(idx1[:, b, :], top1[:, b, :], logit1[:, b, :])
            link(t8)
            link(dve.tensor_copy(idxf[:, :].unsqueeze(2), idx1[:, :, 0:1]))
            dve.tensor_tensor(sel[:, :, :], iota8[:, :].unsqueeze(1).broadcast_to([P, B, NE]),
                              idxf[:, :].unsqueeze(2).broadcast_to([P, B, NE]), ALU.is_equal).then_inc(g1_sel, 1)
            dve.wait_ge(g1_sel, 1)
            dve.tensor_scalar(sel[:, :, :], sel[:, :, :], gate[:, 3:4], None, ALU.mult).then_inc(g1_sel, 1)
            dve.wait_ge(g1_sel, 2)

            def add_expert(i, par, b):
                dve.wait_ge(e_mm, 16 * i + B * par + b + 1)
                if not isinstance(i, int):
                    weight = sel[:, b, bass.ds(2 * i + par, 1)]
                else:
                    weight = sel[:, b, 2 * i + par:2 * i + par + 1]
                if not isinstance(i, int) or par:
                    dve.wait_ge(e_acc, 16 * i + B * par + b + 1 - B)
                dve.scalar_tensor_tensor(out=X[:, b, :], in0=bank[b % 4], scalar=weight, in1=X[:, b, :],
                                         op0=ALU.mult, op1=ALU.add).then_inc(e_acc, 1)

            for par in range(2):
                for b in range(B):
                    add_expert(0, par, b)
            for b in range(B):
                dve.wait_ge(b1_mm, b + 1)
                dve.wait_ge(e_acc, B + b + 1)
                dve.tensor_tensor(X[:, b, :], bank[6 + b % 2], X[:, b, :], ALU.add).then_inc(b1_acc, 1)
            dve.wait_ge(b1_acc, B)
            with dve.Fori(1, NE // 2) as i:
                for par in range(2):
                    for b in range(B):
                        add_expert(i, par, b)

        @block.tensor
        def _(pe):
            def ln_transpose(t):
                if t < 3 * B and t % B >= 2:
                    pe.wait_ge(ln_lo, t - 1)
                pe.wait_ge(ln_row, t + 1)
                for k in range(KT):
                    mm = pe.transpose(lnbank(t)[:, k * P:(k + 1) * P], hrow[:, t % 2, k * P:(k + 1) * P], ident[:, :])
                mm.then_inc(ln_T, 1)

            def tokens(buf, k, t0, n):
                return hilo(buf, k, slice(t0, t0 + n))

            def job(n):
                kind = JOBS[n][0]
                if n >= 4:
                    if HAS_LO[n - 4]:
                        pe.wait_ge(kv_lo, LOS[n - 4])
                    else:
                        pe.wait_ge(kv_hi, n - 3)
                acc = bank[n % 4]
                if kind == "K":
                    _, part, h, half = JOBS[n]
                    src = HT if part else CT
                    mm = contract(pe, acc, [(tokens(Wk_r, k, h * P, P), tokens(src, k, half * 512, 512)) for k in range(KT)])
                elif kind == "V":
                    _, part, b = JOBS[n]
                    src = HT if part else CT
                    mm = contract(pe, acc, [(tokens(src, k, b * P, P), tokens(Wv_r, k, 0, 512)) for k in range(KT)])
                elif kind in ("k1", "v1"):
                    w, half = wk1_r if kind == "k1" else wv1_r, JOBS[n][1]
                    mm = contract(pe, acc, [(tokens(w, k, 0, P), tokens(CT, k, half * 512, 512)) for k in range(KT)])
                else:
                    half = JOBS[n][1]
                    for b in range(HALF):
                        mm = pe.transpose(acc[:, b * P:(b + 1) * P], work[:, 6 + half, b * P:(b + 1) * P], ident[:, :])
                mm.then_inc(kv_mm, 1)

            for n in range(NCTX):
                if n == 0:
                    pe.wait_ge(a_lo, 8)
                elif n == 4:
                    pe.wait_ge(a_lo, 12)
                elif n == 8:
                    pe.wait_ge(a_lo, NA)
                job(n)
                if n == 4:
                    pe.wait_ge(consts_made, 2)
                if 4 <= n < 4 + B:
                    ln_transpose(n - 4)
            pe.wait_ge(chunk_split, 2)
            for n in range(NCTX, NCTX + 4):
                job(n)
            for half in range(2):
                pe.wait_ge(kv_hi, NCTX + 3 + half)
                job(NCTX + 4 + half)
            pe.wait_ge(ln_lo, B)
            for n in range(NCTX + 6, len(JOBS)):
                job(n)

            def queries(at, acc, slot, h, half):
                return contract(pe, acc, [(tokens(Wq_r[:, slot], k, h * P, P), tokens(HT, k, half * 512, 512))
                                          for k in range(KT)]).then_inc(q_mm, 1)

            pe.wait_ge(chunk_split, C_WO0)
            for h in range(QUAD):
                if h >= 2:
                    pe.wait_ge(q_lo, h - 1)
                queries(h, bank[6 + h % 2], 0, h, 0)

            def step(i, c):
                n = number(i, c)
                half, bb = c // QUAD % 2, c % QUAD
                if n is None or n < STEPS:
                    pe.wait_ge(q_lo, 16 * i + QUAD * (c // QUAD) + QUAD)
                    pe.wait_ge(k_loaded[c % 2], 128 * i + 16 * (c // 2 + 1))
                    for k in range(2):
                        if n is not None and n == 0:
                            pe.wait_ge(kv_lo, LOS[-1])
                        else:
                            pe.wait_ge(s_exp, 2 * (16 * i + c - 1) + k + 1)
                        for h in (2 * k, 2 * k + 1):
                            w = hilo(qT[:, half], h, slice(bb * P, (bb + 1) * P))
                            mm = product(pe, bank[k][:, (h % 2) * KEYS:(h % 2 + 1) * KEYS], w, hilo(Kb[:, c % 2]), True, True)
                        mm.then_inc(s_mm, 1)
                if n is None or n < STEPS - QUAD:
                    nxt = c // QUAD + 1
                    pe.wait_ge(q_lo, 16 * i + c + QUAD - 1)
                    if n is None or nxt >= 2:
                        pe.wait_ge(chunk_split, C_STEP + 16 * i + B * (nxt // 2 - 1) + KT)
                    queries(n, bank[6 + c % 2], nxt // 2 % 2, c % QUAD, nxt % 2)
                if (n is None or n >= 1) and (n is None or n <= STEPS):
                    pe.wait_ge(p_norm, 16 * i + c)
                    for k in range(2):
                        if n is None or n >= 2:
                            pe.wait_ge(pt_lo, 2 * (16 * i + c - 2) + k + 1)
                        for h in range(QUAD):
                            mm = pe.transpose(bank[2 + k][:, h * P:(h + 1) * P],
                                              prob[:, (c - 1) % 2, h * KEYS + k * P:h * KEYS + (k + 1) * P], ident[:, :])
                        mm.then_inc(p_T, 1)
                if n is None or n >= 2:
                    pe.wait_ge(o_lo, 16 * i + c - 1)
                    pe.wait_ge(chunk_split, C_STEP + 16 * i + B * ((c - 2) // B))
                    if n is None or n >= 3:
                        pe.wait_ge(y_acc, 16 * i + c - 2)
                    mm = contract(pe, bank[5], [(hilo(OT, slice(h * P, (h + 1) * P)), hilo(Wo_r[:, (c - 2) // B % 2], h))
                                                for h in range(QUAD)])
                    mm.then_inc(y_mm, 1)
                if (n is None or n >= 1) and (n is None or n <= STEPS):
                    pe.wait_ge(v_loaded[(c - 1) % 2], 128 * i + 16 * ((c - 1) // 2 + 1))
                    if n is None or n >= 2:
                        pe.wait_ge(o_lo, 16 * i + c - 1)
                    for k in range(2):
                        pe.wait_ge(pt_lo, 2 * (16 * i + c - 1) + k + 1)
                        mm = product(pe, bank[4], hilo(Vb[:, (c - 1) % 2], k), hilo(PT, k), k == 0, k == 1)
                    mm.then_inc(o_mm, 1)
                if n is not None and n >= STEPS - 5:
                    if n < STEPS - 3:
                        pe.wait_ge(q_lo, STEPS)
                    ln_transpose(B + n - (STEPS - 5))

            steps_of(pe, step)
            ln_transpose(2 * B - 1)

            def gate_logits(half):
                t0 = half * 512
                pe.wait_ge(ln_lo, 2 * B)
                pe.wait_ge(gatew_lo, 2)
                for b in range(HALF):
                    mm = contract(pe, bank[3][:, b * NE:(b + 1) * NE],
                                  [(tokens(HT, k, t0 + b * P, P), hilo(gw[:, 0], k)) for k in range(KT)])
                mm.then_inc(m_gate, 1)

            def latent(half):
                pe.wait_ge(chunk_split, C_FC + 2)
                for m in range(LT):
                    mm = contract(pe, bank[m], [(tokens(fc1_r, k, m * P, P), tokens(HT, k, half * 512, 512)) for k in range(KT)])
                    mm.then_inc(m_xl, 1)

            def latent_expert(half):
                pe.wait_ge(chunk_split, C_FC + 3)
                pe.wait_ge(m_xl_lo, 4 * half + LT)
                pe.wait_ge(m_route, half + 1)
                for m in range(LT):
                    mm = contract(pe, bank[2 + m], [(tokens(lat_r, k, m * P, P), hilo(xlT, k)) for k in range(LT)])
                    mm.then_inc(m_xl, 1)

            def latent_out(half):
                pe.wait_ge(chunk_split, C_FC + 5)
                pe.wait_ge(m_xl_lo, 4 * half + 2 * LT)
                for b in range(HALF):
                    r = half * HALF + b
                    if r >= 2:
                        pe.wait_ge(m_fc2_out, r - 1)
                    mm = contract(pe, bank[4 + b % 2], [(tokens(eoT, k, b * P, P), hilo(fc2_r, k)) for k in range(LT)])
                    mm.then_inc(m_fc2, 1)

            def up(half):
                pe.wait_ge(chunk_split, C_UP + 8)
                for u in range(IT * half, IT * half + IT):
                    if u % IT < 4:
                        pe.wait_ge(m_xl_lo, 4 * half + 2 * LT)
                    else:
                        pe.wait_ge(m_relu, u - 3)
                    mm = contract(pe, bank[u % 4], [(tokens(up_r, k, (u % IT) * P, P), tokens(HT, k, half * 512, 512))
                                                    for k in range(KT)])
                    mm.then_inc(m_up, 1)

            def down(b):
                if b % HALF == 0:
                    pe.wait_ge(chunk_split, C_DOWN + IT)
                    pe.wait_ge(m_sq_lo, IT * (b // HALF + 1))
                if b % HALF < 2:
                    pe.wait_ge(m_fc2_out, HALF * (b // HALF + 1))
                else:
                    pe.wait_ge(z_stat, b - 1)
                mm = contract(pe, bank[4 + b % 2], [(tokens(actT, k, (b % HALF) * P, P), hilo(down_r, k)) for k in range(IT)])
                mm.then_inc(m_down, 1)

            pe.wait_ge(s_exp, 2 * STEPS)
            pe.wait_ge(pt_lo, 2 * STEPS)
            pe.wait_ge(o_lo, STEPS)
            pe.wait_ge(y_acc, STEPS)
            gate_logits(0)
            latent(0)
            latent_expert(0)
            latent_out(0)
            up(0)
            for b in range(HALF):
                down(b)
            for b in range(3):
                ln_transpose(2 * B + b)
            pe.wait_ge(m_relu, IT)
            gate_logits(1)
            pe.wait_ge(z_stat, HALF)
            latent(1)
            ln_transpose(2 * B + 3)
            latent_expert(1)
            latent_out(1)
            up(1)
            down(4)
            down(5)
            down(6)
            ln_transpose(2 * B + 4)
            down(7)
            ln_transpose(2 * B + 5)

            def queries1(n):
                half, m = n // M1, n % M1
                if n < 4:
                    pe.wait_ge(m_relu, 2 * IT)
                else:
                    pe.wait_ge(q1_lo, n - 3)
                mm = contract(pe, bank[n % 4], [(tokens(wq1_r, k, m * P, P), tokens(HT, k, half * 512, 512)) for k in range(KT)])
                mm.then_inc(q1_mm, 1)

            pe.wait_ge(chunk_split, C_WOUT)
            pe.wait_ge(ln_lo, 2 * B + HALF)
            for n in range(M1):
                queries1(n)
            ln_transpose(2 * B + 6)
            ln_transpose(2 * B + 7)
            pe.wait_ge(ln_lo, 3 * B)
            for n in range(M1, 2 * M1):
                queries1(n)
            pe.wait_ge(mask_made, 4)
            pe.wait_ge(identr_made, 1)
            pe.wait_ge(z_stat, B)
            for u in range(B * M1 + 8):
                if u < B * M1:
                    b, m = u // M1, u % M1
                    if u == 0:
                        pe.wait_ge(q1_lo, 2 * M1)
                    if u >= 2:
                        pe.wait_ge(s1_sub, u - 1)
                    pe.wait_ge(kb_loaded[m], 16 * HT1 * (b + 1))
                    for k in range(2):
                        acc = bank[2 * (u % 2) + k]
                        pe.matmul(acc, identr, maskr, start=True, stop=False)
                        mm = product(pe, acc, tokens(qT1, m, b * P, P), hilo(KB[:, m], slice(4 * k, 4 * k + 4)), False, True)
                    mm.then_inc(s1_mm, 1)
                if 1 <= u <= B * M1:
                    pe.wait_ge(s1_exp, u)
                    if u >= 2:
                        pe.wait_ge(p1_copy, u - 1)
                    if u >= 8 and (u - 8) % M1 == 0:
                        pe.wait_ge(o1_lo, (u - 8) // M1 + 1)
                    if u >= 9 and (u - 9) % M1 == 0:
                        pe.wait_ge(y1_acc, (u - 9) // M1 + 1)
                    if u >= 11 and (u - 11) % M1 == 0:
                        pe.wait_ge(ln_lo, 3 * B + (u - 11) // M1 + 1)
                    for h in range(HT1):
                        mm = pe.transpose(bank[4 + h // 4][:, (h % 4) * P:(h % 4 + 1) * P],
                                          prob[:, (u - 1) % 2, h * P:(h + 1) * P], ident[:, :])
                    mm.then_inc(p1_T, 1)
                v = u - 2
                if 0 <= v < B * M1:
                    b, m = v // M1, v % M1
                    pe.wait_ge(p1_copy, v + 1)
                    if m % 2 == 0 and b >= 1:
                        pe.wait_ge(o1_row, 2 * b - 1 + m // 2)
                    for h in range(HT1):
                        at = (m % 2 * HT1 + h) * (D1 + 1)
                        mm = pe.matmul(bank[6 + m // 2][:, at:at + D1 + 1], probT[:, v % 2, h * P:(h + 1) * P],
                                       V1[:, b, (m * HT1 + h) // (H1 // G1), :], start=True, stop=True)
                    mm.then_inc(o1_mm, 1)
                if u >= 7 and (u - 7) % M1 == 0 and (u - 7) // M1 < B:
                    b = (u - 7) // M1
                    pe.wait_ge(o1_row, 2 * b + 2)
                    if b:
                        pe.wait_ge(ln_lo, 3 * B + b)
                    pe.wait_ge(p1_copy, min(u, B * M1))
                    for k in range(KT):
                        mm = pe.transpose(bank[4][:, k * P:(k + 1) * P], hrow[:, b % 2, k * P:(k + 1) * P], ident[:, :])
                    mm.then_inc(o1_T, 1)
                if u >= 8 and (u - 8) % M1 == 0 and (u - 8) // M1 < B:
                    b = (u - 8) // M1
                    if b == 0:
                        pe.wait_ge(chunk_split, C_EX)
                    pe.wait_ge(o1_lo, b + 1)
                    pe.wait_ge(p1_copy, min(u, B * M1))
                    mm = contract(pe, bank[5], [(hilo(OT1[:, b % 2], k), hilo(wout_r, k)) for k in range(KT)])
                    mm.then_inc(y1_mm, 1)
                if u >= 10 and (u - 10) % M1 == 0 and (u - 10) // M1 < B:
                    pe.wait_ge(p1_copy, min(u, B * M1))
                    ln_transpose(3 * B + (u - 10) // M1)

            pe.wait_ge(o1_row, 2 * B)
            pe.wait_ge(ln_lo, 4 * B)
            for b in range(B):
                mm = contract(pe, bank[6][:, b * NE:(b + 1) * NE], [(tokens(HT, k, b * P, P), hilo(gw[:, 1], k)) for k in range(KT)])
            mm.then_inc(g1_mm, 1)

            def expert(i, par, b):
                if b == 0:
                    pe.wait_ge(chunk_split, C_EX + 8 * i + KT * par + KT)
                if not (isinstance(i, int) and par == 0 and b < 4):
                    pe.wait_ge(e_acc, 16 * i + 8 * par + b - 3)
                mm = contract(pe, bank[b % 4], [(tokens(HT, k, b * P, P), hilo(Ex[par], k)) for k in range(KT)])
                mm.then_inc(e_mm, 1)

            pe.wait_ge(s1_sub, B * M1)
            for b in range(B):
                expert(0, 0, b)
            pe.wait_ge(g1_sel, 2)
            for b in range(B):
                mm = pe.transpose(PS[0:NE, 6 + b // 4, (b % 4) * P:(b % 4 + 1) * P], sel[:, b, :], ident[:, :])
            mm.then_inc(g1_T, 1)
            for b in range(B):
                expert(0, 1, b)
            pe.wait_ge(g1_copy, 1)
            for b in range(B):
                if b >= 2:
                    pe.wait_ge(b1_acc, b - 1)
                pe.matmul(bank[6 + b % 2], work[0:NE, 1 + b // 4, (b % 4) * P:(b % 4 + 1) * P], work[0:NE, 0, :],
                          start=True, stop=True).then_inc(b1_mm, 1)
            with pe.Fori(1, NE // 2) as i:
                for par in range(2):
                    for b in range(B):
                        expert(i, par, b)


_ORDER = ["x", "ctxT", "mask", "g_xattn", "g_ffn", "Wq", "Wk", "Wv", "Wo", "gate0", "up_w", "down_w", "fc1_w", "fc2_w",
          "latent_w", "ln_gamma", "ln_beta", "wqT", "wkT", "wvT", "woutT", "gate1T", "gate1_b", "expertT", "expert_b"]


def kernel(**inputs):
    import numpy as _np
    import concourse.bacc as _bacc
    from concourse import mybir as _mybir
    from concourse.bass_utils import run_bass_kernel_spmd as _run

    a = {k: _np.asarray(v) for k, v in inputs.items()}
    laid = {
        "x": a["x"],
        "ctxT": a["ctx_4096"].reshape(-1, a["ctx_4096"].shape[-1]).T,
        "mask": a["mask_SxS2_bk0"],
        "g_xattn": a["g_xattn"], "g_ffn": a["g_ffn"],
        "Wq": a["L0_xattn_Wq"], "Wk": a["L0_xattn_Wk"], "Wv": a["L0_xattn_Wv"], "Wo": a["L0_xattn_Wo"],
        "gate0": a["L0_ffn_gate_w"], "up_w": a["L0_ffn_up_w"], "down_w": a["L0_ffn_down_w"],
        "fc1_w": a["L0_ffn_fc1_w"], "fc2_w": a["L0_ffn_fc2_w"], "latent_w": a["L0_ffn_expert_w"],
        "ln_gamma": a["L0_ffn_ln_gamma"], "ln_beta": a["L0_ffn_ln_beta"],
        "wqT": a["L1_xattn_w_q"].T, "wkT": a["L1_xattn_w_k"].T, "wvT": a["L1_xattn_w_v"].T,
        "woutT": a["L1_xattn_w_out"].T,
        "gate1T": a["L1_ffn_gate_w"].T, "gate1_b": a["L1_ffn_gate_b"],
        "expertT": a["L1_ffn_expert_w"].transpose(0, 2, 1), "expert_b": a["L1_ffn_expert_b"],
    }
    nc = _bacc.Bacc("TRN2", target_bir_lowering=False, num_devices=1)
    arrays, args = {}, []
    for name in _ORDER:
        v = _np.ascontiguousarray(laid[name])
        arrays[f"in_{name}"] = v
        args.append(nc.dram_tensor(f"in_{name}", v.shape, _mybir.dt.from_np(v.dtype), kind="ExternalInput").ap())
    shape = a["x"].shape
    args.append(nc.dram_tensor("out_0", shape, _mybir.dt.float32, kind="ExternalOutput").ap())
    program(nc, *args)
    r = _run(nc, [arrays], core_ids=[0])
    return r.results[0]["out_0"]
```

```python
from contextlib import ExitStack

import concourse.bass as bass
from concourse import mybir


ALU = mybir.AluOpType
ACT = mybir.ActivationFunctionType
F32 = mybir.dt.float32
F32R = mybir.dt.float32r
U8 = mybir.dt.uint8
U32 = mybir.dt.uint32
AX_X = mybir.AxisListType.X

P = 128
B = 8
D = 512
KT = D // P
HALF = 4
LN_EPS = 1e-5

KVH = 4
GROUP = 8
QUAD = 4
NQUAD = KVH * GROUP // QUAD
STEPS = NQUAD * B
KEYS = 2 * P
SCALE0 = float(P) ** -0.5

H1 = 32
D1 = D // H1
G1 = 8
HT1 = P // D1
M1 = H1 // HT1
SHARE1 = H1 // G1
UNITS1 = B * G1
SCALE1 = float(D1) ** -0.5
MASKED = -3.0e38

NE = 8
INT = 1024
LAT = 256
IT = INT // P
LT = LAT // P


def program(nc, x, ctxT, mask, g_xattn, g_ffn, Wq, Wk, Wv, Wo, gate0, up_w, down_w, fc1_w, fc2_w,
            latent_w, ln_gamma, ln_beta, wqT, wkT, wvT, woutT, gate1T, gate1_b, expertT, expert_b, out):
    ctx = ExitStack()
    with ctx:
        def sb(name, shape, dt=F32):
            return ctx.enter_context(nc.sbuf_tensor(name, shape, dt))

        def sem(name):
            return ctx.enter_context(nc.semaphore(name))

        PS = ctx.enter_context(nc.psum_tensor("PS", [P, 8, 512], F32))
        bank = [PS[:, k, :] for k in range(8)]

        X = sb("X", [P, B, D])
        work = sb("work", [P, 8, 512])
        prob = work[:, 0:4, :].rearrange("p (s a) c -> p s (a c)", s=2)
        prob1 = work[:, 0:4, :]
        probT1 = work[:, 4:8, :]
        gam = work[:, 4, :]
        bet = work[:, 5, :]
        logitT = work[0:NE, 6, :]
        logitT1 = work[0:NE, 4:6, :]
        zrow = work[:, 6:8, :]
        raw = sb("raw", [P, 4, 512])
        hrow = sb("hrow", [P, 2, 512])
        V1 = sb("V1", [P, B, G1, D1 + 1])
        ident = sb("ident", [P, P])
        iota8 = sb("iota8", [P, NE])
        graw = sb("graw", [P, 4])
        gate = sb("gate", [P, 4])
        stats = sb("stats", [P, 2, 6])
        meanvar = sb("meanvar", [P, B, 2])
        vareps = sb("vareps", [P, B])
        rstd = sb("rstd", [P, B])
        mhalf = sb("mhalf", [P, 1])
        zmv = sb("zmv", [P, B, 2])
        zve = sb("zve", [P, B])
        zrs = sb("zrs", [P, B])
        nmax = sb("nmax", [P, 2, QUAD])
        psumr = sb("psumr", [P, 2, QUAD])
        rinv = sb("rinv", [P, 2, QUAD])
        top0 = sb("top0", [P, HALF, 8])
        route = sb("route", [P, B])
        max1 = sb("max1", [P, 2, SHARE1])
        rsum1 = sb("rsum1", [P, 2, 16])
        gb1 = sb("gb1", [P, NE])
        logit1 = sb("logit1", [P, B, NE])
        top1 = sb("top1", [P, B, 8])
        idx1 = sb("idx1", [P, B, 8], U32)
        idxf = sb("idxf", [P, B])
        sel = sb("sel", [P, B, NE])
        graww = hrow[:, 1, 512 - 2 * KT * NE:512].rearrange("p (l k n) -> p l k n", l=2, k=KT)
        mask8 = sb("mask8", [P, P], U8)

        arena = sb("arena", [P, 40064 + 2 * 2 * KT * NE], F32R)

        def region(at, words):
            return arena[:, at:at + words]

        HT = region(0, 8192).rearrange("p (s k t) -> p s k t", s=2, k=KT)
        RA, RB, RC, RD, RE = 8192, 16384, 24576, 32768, 37888
        Wk_r = region(RB, 4096).rearrange("p (s k n) -> p s k n", s=2, k=KT)
        Wv_r = region(RB + 4096, 4096).rearrange("p (s k n) -> p s k n", s=2, k=KT)
        CT = region(RC, 8192).rearrange("p (s k t) -> p s k t", s=2, k=KT)
        wk1_r = region(RA + 4096, 1024).rearrange("p (s k n) -> p s k n", s=2, k=KT)
        wv1_r = region(RA + 5120, 1024).rearrange("p (s k n) -> p s k n", s=2, k=KT)
        stage = region(RD, 4096).rearrange("p (j s n) -> p j s n", j=4, s=2)
        Wq_r = region(RA, 8192).rearrange("p (j s k n) -> p j s k n", j=2, s=2, k=KT)
        Wo_r = region(RB, 8192).rearrange("p (j s h n) -> p j s h n", j=2, s=2, h=QUAD)
        qT = region(RC, 8192).rearrange("p (j s h t) -> p j s h t", j=2, s=2, h=QUAD)
        Kb = region(RD, 1024).rearrange("p (j s t) -> p j s t", j=2, s=2)
        Vb = region(RD + 1024, 1024).rearrange("p (j s k n) -> p j s k n", j=2, s=2, k=2)
        PT = region(RD + 2048, 2048).rearrange("p (s k n) -> p s k n", s=2, k=2)
        OT = region(RD + 4096, 1024).rearrange("p (s n) -> p s n", s=2)
        up_r = region(RA, 8192).rearrange("p (s k n) -> p s k n", s=2, k=KT)
        down_r = region(RB, 8192).rearrange("p (s k n) -> p s k n", s=2, k=IT)
        actT = region(RC, 8192).rearrange("p (s k t) -> p s k t", s=2, k=IT)
        xlT = region(RC, 2048).rearrange("p (s k t) -> p s k t", s=2, k=LT)
        eoT = region(RC + 2048, 2048).rearrange("p (s k t) -> p s k t", s=2, k=LT)
        fc1_r = region(RD, 2048).rearrange("p (s k n) -> p s k n", s=2, k=KT)
        lat_r = region(RD + 2048, 1024).rearrange("p (s k n) -> p s k n", s=2, k=LT)
        fc2_r = region(RD + 3072, 2048).rearrange("p (s k n) -> p s k n", s=2, k=LT)
        wq1_r = region(RA, 4096).rearrange("p (s k n) -> p s k n", s=2, k=KT)
        wout_r = region(RA + 4096, 4096).rearrange("p (s k n) -> p s k n", s=2, k=KT)
        KB = region(RB, 8192).rearrange("p (m s h t) -> p m s h t", m=M1, s=2, h=HT1)
        qT1 = region(RC, 8192).rearrange("p (s m t) -> p s m t", s=2, m=M1)
        OT1 = region(RD, 2048).rearrange("p (j s k t) -> p j s k t", j=2, s=2, k=KT)
        maskr = region(RD + 2048, 512)
        KT1 = region(RE, 2048).rearrange("p (s t) -> p s t", s=2)
        Ex = [region(RA, 4096).rearrange("p (s k n) -> p s k n", s=2, k=KT),
              region(RB, 4096).rearrange("p (s k n) -> p s k n", s=2, k=KT)]
        gwords = 2 * KT * NE
        gw = region(RE + 2048, 2 * gwords).rearrange("p (l s k n) -> p l s k n", l=2, s=2, k=KT)
        identr = region(RE + 2048 + 2 * gwords, P)

        def gate_wide(l, k):
            at = [RE + 2048 + l * gwords + part * KT * NE + k * NE for part in range(2)]
            return region(at[0], P), region(at[1], P)


        Kscr = nc.dram_tensor("Kscr", [KVH, B, P, 2, KEYS], F32).ap()
        Vscr = nc.dram_tensor("Vscr", [KVH, B, P, 2, 2, P], F32).ap()

        small_loaded = sem("small_loaded")
        gates_tanh = sem("gates_tanh")
        consts_made = sem("consts_made")
        identr_made = sem("identr_made")
        gatew_hi = sem("gatew_hi")
        gatew_lo = sem("gatew_lo")
        x_loaded = [sem(f"x_loaded{b}") for b in range(B)]
        a_loaded = [sem(f"a_loaded{k}") for k in range(8)]
        a_hi = sem("a_hi")
        a_lo = sem("a_lo")
        raw_loaded = [sem(f"raw_loaded{k}") for k in range(4)]
        chunk_hi = sem("chunk_hi")
        late_hi = sem("late_hi")
        step_hi = sem("step_hi")
        ex_hi = sem("ex_hi")
        chunk_split = sem("chunk_split")
        ln_stat = sem("ln_stat")
        ln_rstd = sem("ln_rstd")
        ln_row = sem("ln_row")
        ln_T = sem("ln_T")
        ln_hi = sem("ln_hi")
        ln_lo = sem("ln_lo")
        kv_mm = sem("kv_mm")
        kv_hi = sem("kv_hi")
        kv_lo = sem("kv_lo")
        kv_stored = [sem(f"kv_stored{k}") for k in range(4)]
        k_loaded = [sem(f"k_loaded{k}") for k in range(2)]
        v_loaded = [sem(f"v_loaded{k}") for k in range(2)]
        q_mm = sem("q_mm")
        q_hi = sem("q_hi")
        q_lo = sem("q_lo")
        s_mm = sem("s_mm")
        s_max = sem("s_max")
        s_exp = sem("s_exp")
        s_rcp = sem("s_rcp")
        p_norm = sem("p_norm")
        p_T = sem("p_T")
        pt_hi = sem("pt_hi")
        pt_lo = sem("pt_lo")
        o_mm = sem("o_mm")
        o_hi = sem("o_hi")
        o_lo = sem("o_lo")
        y_mm = sem("y_mm")
        y_acc = sem("y_acc")
        chain = sem("chain")
        gb_loaded = sem("gb_loaded")
        eb_loaded = sem("eb_loaded")
        gb_made = sem("gb_made")
        xbeta = sem("xbeta")
        m_gateT = sem("m_gateT")
        m_gate_row = sem("m_gate_row")
        m_gate = sem("m_gate")
        m_route = sem("m_route")
        m_xl = sem("m_xl")
        m_xl_hi = sem("m_xl_hi")
        m_xl_lo = sem("m_xl_lo")
        m_fc2 = sem("m_fc2")
        m_fc2_out = sem("m_fc2_out")
        m_up = sem("m_up")
        m_relu = sem("m_relu")
        m_sq = sem("m_sq")
        m_sq_hi = sem("m_sq_hi")
        m_sq_lo = sem("m_sq_lo")
        m_down = sem("m_down")
        z_stat = sem("z_stat")
        z_rstd = sem("z_rstd")
        mask_made = sem("mask_made")
        kb_zero = sem("kb_zero")
        kb_loaded = [sem(f"kb_loaded{m}") for m in range(M1)]
        q1_mm = sem("q1_mm")
        q1_hi = sem("q1_hi")
        q1_lo = sem("q1_lo")
        s1_mm = sem("s1_mm")
        s1_max = sem("s1_max")
        s1_sub = sem("s1_sub")
        s1_exp = sem("s1_exp")
        p1_T = sem("p1_T")
        p1_copy = sem("p1_copy")
        o1_mm = sem("o1_mm")
        o1_rcp = sem("o1_rcp")
        o1_row = sem("o1_row")
        o1_T = sem("o1_T")
        o1_hi = sem("o1_hi")
        o1_lo = sem("o1_lo")
        y1_mm = sem("y1_mm")
        y1_acc = sem("y1_acc")
        g1_mmT = sem("g1_mmT")
        g1_row = sem("g1_row")
        g1_mm = sem("g1_mm")
        g1_sel = sem("g1_sel")
        g1_T = sem("g1_T")
        g1_copy = sem("g1_copy")
        b1_mm = sem("b1_mm")
        b1_acc = sem("b1_acc")
        e_mm = sem("e_mm")
        e_acc = sem("e_acc")
        out_stored = sem("out_stored")

        def kv_jobs(part):
            out = []
            for half in range(2):
                out += [("K", part, h, half) for h in range(KVH)]
                out += [("V", part, half * HALF + b) for b in range(HALF)]
            return out

        JOBS = kv_jobs(0) + [("k1", 0), ("k1", 1), ("v1", 0), ("v1", 1), ("v1t", 0), ("v1t", 1)] + kv_jobs(1)
        HAS_LO = [j[0] in ("K", "V", "k1") for j in JOBS]
        LOS = [sum(HAS_LO[:n + 1]) for n in range(len(JOBS))]
        STORE = [sum(j[0] in "KV" for j in JOBS[:n]) for n in range(len(JOBS))]
        NCTX = 16
        NA = 16

        C_WQ0 = 2
        C_WO0 = C_WQ0 + KT
        C_STEP = C_WO0 + QUAD
        C_UP = C_STEP + STEPS - B
        C_FC = C_UP + 8
        C_DOWN = C_FC + 5
        C_WQ1 = C_DOWN + IT
        C_WOUT = C_WQ1 + KT
        C_EX = C_WOUT + KT
        C_ALL = C_EX + NE * KT

        Wq_v = Wq.rearrange("(k p) n -> k p n", p=P)
        Wo_v = Wo.rearrange("(h p) n -> h p n", p=P)
        up_v = up_w.rearrange("(k p) n -> p k n", p=P)
        down_v = down_w.rearrange("(k p) n -> p k n", p=P)
        fc1_v = fc1_w.rearrange("(k p) n -> p k n", p=P)
        fc2_v = fc2_w.rearrange("(k p) n -> p k n", p=P)
        lat_v = latent_w.rearrange("(k p) n -> p k n", p=P)
        wq1_v = wqT.rearrange("(k p) n -> p k n", p=P)
        wout_v = woutT.rearrange("(k p) n -> p k n", p=P)
        ex_v = expertT.rearrange("e (k p) n -> e k p n", p=P)
        ctx_v = ctxT.rearrange("(k p) t -> p k t", p=P)
        Wk_v = Wk.rearrange("(k p) n -> p k n", p=P)
        Wv_v = Wv.rearrange("(k p) n -> p k n", p=P)

        def raw_as(c, parts):
            return raw[:, c % 4, :].rearrange("p (k n) -> p k n", k=parts)

        def mlp_chunk(c):
            if c < C_FC:
                k, n = (c - C_UP) // 2, (c - C_UP) % 2 * 512
                return up_v[:, k, n:n + 512], up_r[:, 0, k, n:n + 512], up_r[:, 1, k, n:n + 512], raw[:, c % 4, :]
            if c < C_FC + 2:
                k = (c - C_FC) * 2
                return fc1_v[:, k:k + 2, :], fc1_r[:, 0, k:k + 2, :], fc1_r[:, 1, k:k + 2, :], raw_as(c, 2)
            if c < C_FC + 3:
                return lat_v, lat_r[:, 0], lat_r[:, 1], raw_as(c, 2)
            if c < C_DOWN:
                k = c - C_FC - 3
                return fc2_v[:, k, :], fc2_r[:, 0, k, :], fc2_r[:, 1, k, :], raw[:, c % 4, :]
            if c < C_WQ1:
                k = c - C_DOWN
                return down_v[:, k, :], down_r[:, 0, k, :], down_r[:, 1, k, :], raw[:, c % 4, :]
            if c < C_WOUT:
                k = c - C_WQ1
                return wq1_v[:, k, :], wq1_r[:, 0, k, :], wq1_r[:, 1, k, :], raw[:, c % 4, :]
            k = c - C_WOUT
            return wout_v[:, k, :], wout_r[:, 0, k, :], wout_r[:, 1, k, :], raw[:, c % 4, :]

        def first_chunk(a):
            k, kind = a % 4, a // 4
            if kind == 0:
                return Wk_v[:, k, :], Wk_r[:, 0, k, :], Wk_r[:, 1, k, :]
            if kind == 2:
                return Wv_v[:, k, :], Wv_r[:, 0, k, :], Wv_r[:, 1, k, :]
            t = 0 if kind == 1 else 512
            return ctx_v[:, k, t:t + 512], CT[:, 0, k, t:t + 512], CT[:, 1, k, t:t + 512]

        def f32(ap):
            return ap.bitcast(F32)

        def product(pe, acc, w, m, first, last):
            pe.matmul(acc, w[0], m[0], start=first, stop=False)
            pe.matmul(acc, w[0], m[1], start=False, stop=False)
            return pe.matmul(acc, w[1], m[0], start=False, stop=last)

        def contract(pe, acc, pairs):
            for n, (w, m) in enumerate(pairs):
                mm = product(pe, acc, w, m, n == 0, n == len(pairs) - 1)
            return mm

        def hilo(buf, *at):
            return buf[(slice(None), 0) + at], buf[(slice(None), 1) + at]

        def steps_of(eng, step):
            for c in range(B):
                step(0, c)
            with eng.Fori(0, 3) as i:
                for c in range(B, B + 16):
                    step(i, c)
            for c in range(B, B + 10):
                step(3, c)

        def number(i, c):
            return 16 * i + c if isinstance(i, int) else None

        def step_chunk(c):
            k, at = c % B, (c // B + 1) % 2
            return hilo(Wq_r[:, at], k) if k < KT else hilo(Wo_r[:, at], k - KT)

        def lnbank(t):
            return bank[6 + t % 2] if t < 3 * B else bank[7]

        def expert_bank(i, par, b):
            return bank[b] if isinstance(i, int) and i == 0 and par == 0 and b < 6 else bank[b % 4]

        A = slice(None)
        block = ctx.enter_context(nc.Block())

        @block.sync
        def _(sp):
            def load_first(a):
                if a >= 8:
                    sp.wait_ge(a_lo, a - 7)
                sp.dma_start(work[:, a % 8, :], first_chunk(a)[0]).then_inc(a_loaded[a % 8], 16)

            def load_raw(c, src, dst=None):
                if c >= 4:
                    sp.wait_ge(chunk_split, c - 3)
                sp.dma_start(raw[:, c % 4, :] if dst is None else dst, src).then_inc(raw_loaded[c % 4], 16)

            def load_late(c):
                src, _, _, dst = mlp_chunk(c)
                load_raw(c, src, dst)

            def load_x(b):
                sp.dma_start(X[:, b, :], x[b]).then_inc(x_loaded[b], 16)

            for a in range(8):
                load_first(a)
            load_x(0)
            load_x(1)
            for g, src in enumerate((g_xattn, g_ffn)):
                sp.dma_start(graw[:, 2 * g:2 * g + 2], src.rearrange("(a n) -> a n", a=1).broadcast_to([P, 2])
                             ).then_inc(small_loaded, 16)
            sp.dma_start(graww[:, 0], gate0.rearrange("(k p) n -> p k n", p=P)).then_inc(small_loaded, 16)
            sp.dma_start(graww[:, 1], gate1T.rearrange("(k p) n -> p k n", p=P)).then_inc(small_loaded, 16)
            sp.dma_start(gb1[:, :], gate1_b.rearrange("(a n) -> a n", a=1).broadcast_to([P, NE])
                         ).then_inc(small_loaded, 16)
            sp.dma_start(mask8[:, :], mask).then_inc(small_loaded, 16)
            for a in range(8, 12):
                load_first(a)
            for b in range(2, B):
                load_x(b)
            for a in range(12, NA):
                load_first(a)
            load_raw(0, wkT.rearrange("(k p) n -> p k n", p=P), raw_as(0, KT))
            load_raw(1, wvT.rearrange("(k p) n -> p k n", p=P), raw_as(1, KT))
            for k in range(KT):
                load_raw(C_WQ0 + k, Wq_v[k, :, 0:512])
            for n, job in enumerate(JOBS):
                if job[0] not in ("K", "V"):
                    continue
                s = STORE[n]
                sp.wait_ge(kv_lo, LOS[n])
                for part in range(2):
                    if job[0] == "K":
                        _, cl, h, half = job
                        dst = Kscr[h, half * HALF:(half + 1) * HALF, :, part, cl * P:(cl + 1) * P].rearrange("b p t -> p b t")
                        src = stage[:, s % 4, part, :].rearrange("p (b t) -> p b t", b=HALF)
                    else:
                        _, cl, b = job
                        dst = Vscr[:, b, :, part, cl, :].rearrange("h p n -> p h n")
                        src = stage[:, s % 4, part, :].rearrange("p (h n) -> p h n", h=KVH)
                    sp.dma_start(dst, f32(src)).then_inc(kv_stored[s % 4], 16)
            sp.dma_start(gam, ln_gamma.rearrange("(a n) -> a n", a=1).broadcast_to([P, D])).then_inc(gb_loaded, 16)
            sp.dma_start(bet, ln_beta.rearrange("(a n) -> a n", a=1).broadcast_to([P, D])).then_inc(gb_loaded, 16)
            for k in range(QUAD):
                load_raw(C_WO0 + k, Wo_v[k])

            def load_K(i, c):
                src = Kscr[bass.ds(i + c // 16, 1), c % B].rearrange("a p s t -> (a p) s t")
                sp.dma_start(f32(Kb[:, c % 2]), src).then_inc(k_loaded[c % 2], 16)

            def load_V(i, c):
                src = Vscr[bass.ds(i + c // 16, 1), c % B].rearrange("a p s k n -> (a p) s k n")
                sp.dma_start(f32(Vb[:, c % 2]), src).then_inc(v_loaded[c % 2], 16)

            def load_step_chunk(i, c):
                j1, k = c // B + 1, c % B
                if k < KT:
                    src = Wq_v[k, :, bass.ds(1024 * i + 512 * j1, 512)]
                else:
                    src = Wo_v[bass.ds(8 * i + QUAD * j1 + k - KT, 1)].rearrange("a p n -> (a p) n")
                sp.wait_ge(chunk_split, C_STEP + 16 * i + c - 3)
                sp.dma_start(raw[:, (C_STEP + c) % 4, :], src).then_inc(raw_loaded[(C_STEP + c) % 4], 16)

            for s in range(4):
                sp.wait_ge(kv_stored[s], 16 * 2 * 8)
            load_K(0, 0)

            def step(i, c):
                n = number(i, c)
                if n is None or n < STEPS:
                    if n is None or n >= 2:
                        sp.wait_ge(o_mm, 16 * i + c - 1)
                    load_V(i, c)
                if n is None or n + 1 < STEPS:
                    if n is None or n >= 1:
                        sp.wait_ge(s_mm, 2 * (16 * i + c))
                    load_K(i, c + 1)
                if n is None or n < STEPS - B:
                    load_step_chunk(i, c)
                elif n < STEPS:
                    load_late(C_UP + n - (STEPS - B))

            steps_of(sp, step)
            for c in range(C_UP + 8, C_EX):
                load_late(c)

            def load_expert(c):
                e, k = (c - C_EX) // KT, (c - C_EX) % KT
                load_raw(c, ex_v[e, k])

            for k in range(KT):
                load_expert(C_EX + k)
            sp.wait_ge(kb_zero, 1)
            for u in range(B * M1):
                b, m = u // M1, u % M1
                if u >= M1:
                    sp.wait_ge(s1_mm, 2 * (u - M1) + 2)
                for h in range(HT1):
                    g = (m * HT1 + h) // (H1 // G1)
                    sp.dma_start(f32(KB[D1 * h:D1 * (h + 1), m, :, h, :]), f32(KT1[D1 * g:D1 * (g + 1), :, b * P:(b + 1) * P])
                                 ).then_inc(kb_loaded[m], 16)
                if u == 2 * M1:
                    for k in range(KT):
                        load_expert(C_EX + KT + k)
            sp.wait_ge(s1_exp, UNITS1)
            sp.wait_ge(p1_T, UNITS1)
            sp.dma_start(work[0:NE, 0, :], expert_b).then_inc(eb_loaded, 16)
            for c in range(C_EX + 2 * KT, C_ALL):
                load_expert(c)
            for b in range(B):
                sp.wait_ge(e_acc, (NE - 1) * B + b + 1)
                sp.dma_start(out[b], X[:, b, :]).then_inc(out_stored, 16)
            sp.wait_ge(out_stored, 16 * B)

        @block.gpsimd
        def _(pool):
            made = [0]

            def link(ins):
                made[0] += 1
                ins.then_inc(consts_made, 1)
                pool.wait_ge(consts_made, made[0])

            link(pool.memset(ident[:, :], 0.0))
            link(pool.affine_select(out=ident[:, :], in_=ident[:, :], compare_op=ALU.not_equal, fill=1.0, base=0,
                                    pattern=[[-1, P]], channel_multiplier=1))
            link(pool.iota(iota8[:, :], pattern=[[1, NE]], base=0, channel_multiplier=0,
                           allow_small_or_imprecise_dtypes=True))
            link(pool.memset(mhalf[:, :], -0.5))
            link(pool.memset(V1[:, :, :, :], 1.0))

            def ln_power(t):
                b = t % B
                pool.wait_ge(ln_stat, t + 1)
                pool.tensor_tensor(rstd[:, b:b + 1], vareps[:, b:b + 1], mhalf[:, :], ALU.pow).then_inc(ln_rstd, 1)

            own = [0]

            def split(src, hi, lo):
                pool.tensor_copy(hi, src).then_inc(chunk_hi, 1)
                own[0] += 1
                pool.wait_ge(chunk_hi, own[0])
                pool.tensor_tensor(lo, src, f32(hi), ALU.subtract).then_inc(chunk_split, 1)

            def split_static(c, src, hi, lo):
                pool.wait_ge(raw_loaded[c % 4], 16 * (c // 4 + 1))
                split(src, hi, lo)

            def split_late(c):
                _, hi, lo, src = mlp_chunk(c)
                split_static(c, src, hi, lo)

            for t in range(4):
                ln_power(t)
            split_static(0, raw_as(0, KT), wk1_r[:, 0], wk1_r[:, 1])
            split_static(1, raw_as(1, KT), wv1_r[:, 0], wv1_r[:, 1])
            for t in range(4, B):
                ln_power(t)
            for k in range(KT):
                c = C_WQ0 + k
                split_static(c, raw[:, c % 4, :], Wq_r[:, 0, 0, k, :], Wq_r[:, 0, 1, k, :])
            pool.wait_ge(kv_mm, len(JOBS))
            for h in range(QUAD):
                c = C_WO0 + h
                split_static(c, raw[:, c % 4, :], Wo_r[:, 0, 0, h, :], Wo_r[:, 0, 1, h, :])

            def step(i, c):
                n = number(i, c)
                if n is not None and n >= STEPS - 5 and n - (STEPS - 5) < B:
                    ln_power(B + n - (STEPS - 5))
                if n is None or n < STEPS:
                    pr = prob[:, c % 2, :].rearrange("p (h t) -> p h t", h=QUAD)
                    pool.wait_ge(s_rcp, 16 * i + c + 1)
                    pool.tensor_tensor(pr, pr, rinv[:, c % 2, :].unsqueeze(2).broadcast_to([P, QUAD, KEYS]), ALU.mult
                                       ).then_inc(p_norm, 1)
                if n is None or n < STEPS - B:
                    hi, lo = step_chunk(c)
                    pool.wait_ge(step_hi, 16 * i + c + 1)
                    pool.tensor_tensor(lo, raw[:, (C_STEP + c) % 4, :], f32(hi), ALU.subtract).then_inc(chunk_split, 1)
                if n is not None and STEPS - 4 <= n < STEPS:
                    pool.wait_ge(q_mm, STEPS)
                    for k in range(2):
                        split_late(C_UP + 2 * (n - (STEPS - 4)) + k)

            steps_of(pool, step)
            ln_power(2 * B - 1)

            def late_low(c):
                _, hi, lo, src = mlp_chunk(c)
                pool.wait_ge(late_hi, c - C_FC + 1)
                pool.tensor_tensor(lo, src, f32(hi), ALU.subtract).then_inc(chunk_split, 1)

            for c in range(C_FC, C_DOWN):
                late_low(c)

            def act_low(u):
                pool.wait_ge(m_sq_hi, u + 1)
                pool.tensor_tensor(actT[:, 1, u % IT, :], hrow[:, u % 2, :], f32(actT[:, 0, u % IT, :]), ALU.subtract
                                   ).then_inc(m_sq_lo, 1)

            def z_power(b):
                pool.wait_ge(z_stat, b + 1)
                pool.tensor_tensor(zrs[:, b:b + 1], zve[:, b:b + 1], mhalf[:, :], ALU.pow).then_inc(z_rstd, 1)

            for u in range(IT):
                late_low(C_DOWN + u)
                act_low(u)
            pool.wait_ge(gb_made, 2)
            pool.wait_ge(ln_row, 2 * B)
            for b in range(B):
                pool.tensor_tensor(X[:, b, :], X[:, b, :], bet, ALU.add).then_inc(xbeta, 1)
            for b in range(HALF):
                z_power(b)
                ln_power(2 * B + b)
            for u in range(IT, 2 * IT):
                act_low(u)
            for k in range(KT):
                late_low(C_WQ1 + k)
            for b in range(HALF, B):
                z_power(b)
                ln_power(2 * B + b)
            pool.wait_ge(m_down, B)
            pool.memset(f32(region(RB, 8192)), 0.0).then_inc(kb_zero, 1)
            for k in range(KT):
                late_low(C_WOUT + k)

            def split_expert(c):
                e, k = (c - C_EX) // KT, (c - C_EX) % KT
                split_static(c, raw[:, c % 4, :], Ex[e % 2][:, 0, k, :], Ex[e % 2][:, 1, k, :])

            pool.wait_ge(q1_mm, 2 * M1)
            for k in range(KT):
                split_expert(C_EX + k)
            for b in range(B - 1):
                ln_power(3 * B + b)
            pool.wait_ge(s1_mm, UNITS1)
            for k in range(KT):
                split_expert(C_EX + KT + k)
            ln_power(4 * B - 1)

            with pool.Fori(1, NE // 2) as i:
                for par in range(2):
                    for k in range(KT):
                        c0 = C_EX + KT * par + k
                        pool.wait_ge(ex_hi, 8 * i + KT * par + k - 7)
                        pool.tensor_tensor(Ex[par][:, 1, k, :], raw[:, c0 % 4, :], f32(Ex[par][:, 0, k, :]), ALU.subtract
                                           ).then_inc(chunk_split, 1)

        @block.scalar
        def _(act):
            def first_hi(a):
                act.wait_ge(a_loaded[a % 8], 16 * (a // 8 + 1))
                act.copy(first_chunk(a)[1], work[:, a % 8, :]).then_inc(a_hi, 1)

            def job_hi(n):
                kind = JOBS[n][0]
                act.wait_ge(kv_mm, n + 1)
                if kind in ("K", "V"):
                    s = STORE[n]
                    if s >= 4:
                        act.wait_ge(kv_stored[s % 4], 32 * (s // 4))
                    dst, src = stage[:, s % 4, 0, :], bank[n % 4]
                elif kind == "k1":
                    t = JOBS[n][1] * 512
                    dst, src = KT1[:, 0, t:t + 512], bank[n % 4]
                elif kind == "v1":
                    dst, src = work[:, 6 + JOBS[n][1], :], bank[n % 4]
                else:
                    half = JOBS[n][1]
                    dst = V1[:, half * HALF:(half + 1) * HALF, :, 0:D1]
                    src = bank[n % 4].rearrange("p (b g d) -> p b g d", b=HALF, g=G1)
                    act.wait_ge(consts_made, 5)
                act.copy(dst, src).then_inc(kv_hi, 1)

            def ln_high(t):
                b = t % B
                act.wait_ge(ln_T, t + 1)
                act.copy(HT[:, 0, :, b * P:(b + 1) * P], lnbank(t).rearrange("p (k t) -> p k t", k=KT)).then_inc(ln_hi, 1)

            for a in range(8):
                first_hi(a)
            act.wait_ge(small_loaded, 16 * 6)
            act.activation(gate[:, :], graw[:, :], ACT.Tanh).then_inc(gates_tanh, 1)
            for l in range(2):
                act.copy(gw[:, l, 0], graww[:, l]).then_inc(gatew_hi, 1)
            for a in range(8, 12):
                first_hi(a)
            job_hi(0)
            job_hi(1)
            first_hi(12)
            first_hi(13)
            job_hi(2)
            first_hi(14)
            first_hi(15)
            job_hi(3)
            job_hi(4)
            for b in range(B):
                ln_high(b)
                job_hi(5 + b)
            for n in range(5 + B, len(JOBS)):
                job_hi(n)

            def q_high(index, h, half):
                act.wait_ge(q_mm, index + 1)
                act.activation(qT[:, half, 0, h, :], bank[6 + h % 2], ACT.Copy, scale=SCALE0).then_inc(q_hi, 1)

            for h in range(QUAD):
                q_high(h, h, 0)

            def step(i, c):
                n = number(i, c)
                if n is None or n >= 2:
                    act.wait_ge(o_mm, 16 * i + c - 1)
                    act.copy(OT[:, 0, :], bank[4]).then_inc(o_hi, 1)
                if n is not None and n >= STEPS - 4:
                    ln_high(B + n - (STEPS - 4))
                if n is None or n < STEPS:
                    for h in range(QUAD):
                        if h % 2 == 0:
                            act.wait_ge(s_max, 2 * (16 * i + c) + h // 2 + 1)
                        if h == 0 and (n is None or n >= 2):
                            act.wait_ge(p_T, 2 * (16 * i + c - 1))
                        e = act.activation(prob[:, c % 2, h * KEYS:(h + 1) * KEYS],
                                           bank[h // 2][:, (h % 2) * KEYS:(h % 2 + 1) * KEYS], ACT.Exp,
                                           bias=nmax[:, c % 2, h:h + 1], accum_out=psumr[:, c % 2, h:h + 1])
                        if h % 2:
                            e.then_inc(s_exp, 1)
                if n is None or n < STEPS - QUAD:
                    act.wait_ge(q_mm, 16 * i + c + QUAD + 1)
                    act.activation(qT[:, (c // QUAD + 1) % 2, 0, c % QUAD, :], bank[6 + c % 2], ACT.Copy,
                                   scale=SCALE0).then_inc(q_hi, 1)
                if (n is None or n >= 1) and (n is None or n <= STEPS):
                    for k in range(2):
                        act.wait_ge(p_T, 2 * (16 * i + c - 1) + k + 1)
                        act.copy(PT[:, 0, k, :], bank[2 + k]).then_inc(pt_hi, 1)
                if n is None or n < STEPS - B:
                    if n is None:
                        act.wait_ge(q_mm if c % B < KT else y_mm, 16 * i + B * (c // B))
                    elif c == 0:
                        act.wait_ge(kv_mm, len(JOBS))
                    slot = (C_STEP + c) % 4
                    act.wait_ge(raw_loaded[slot], 64 * i + 16 * ((C_STEP + c) // 4 + 1))
                    act.copy(step_chunk(c)[0], raw[:, slot, :]).then_inc(step_hi, 1)

            steps_of(act, step)
            ln_high(2 * B - 2)

            def late_high(c):
                _, hi, _, src = mlp_chunk(c)
                act.wait_ge(raw_loaded[c % 4], 16 * (c // 4 + 1))
                act.copy(hi, src).then_inc(late_hi, 1)

            act.wait_ge(o_mm, STEPS)
            late_high(C_FC)
            late_high(C_FC + 1)
            for half in range(2):
                if half:
                    act.wait_ge(ln_stat, 2 * B + 3)
                act.wait_ge(m_gateT, half + 1)
                act.copy(logitT, bank[3][0:NE, :]).then_inc(m_gate_row, 1)
                if not half:
                    ln_high(2 * B - 1)
                    act.wait_ge(y_mm, STEPS)
                    late_high(C_FC + 2)
                for k in range(LT):
                    act.wait_ge(m_xl, 4 * half + k + 1)
                    act.copy(xlT[:, 0, k, :], bank[k]).then_inc(m_xl_hi, 1)
                    if not half:
                        late_high(C_FC + 3 + k)
                if half:
                    ln_high(2 * B + 3)
                for k in range(LT):
                    act.wait_ge(m_xl, 4 * half + LT + k + 1)
                    act.copy(eoT[:, 0, k, :], bank[2 + k]).then_inc(m_xl_hi, 1)

                def act_high(u):
                    act.wait_ge(m_sq, u + 1)
                    act.copy(actT[:, 0, u % IT, :], hrow[:, u % 2, :]).then_inc(m_sq_hi, 1)

                for u in range(IT * half, IT * half + IT):
                    if not half:
                        late_high(C_DOWN + u)
                    act.wait_ge(m_up, u + 1)
                    if u % IT < 2:
                        act.wait_ge(ln_T, 2 * B + 4 * half)
                    if u >= 2:
                        act.wait_ge(m_sq_lo, u - 1)
                    act.activation(hrow[:, u % 2, :], bank[u % 4], ACT.Relu).then_inc(m_relu, 1)
                    if u % IT:
                        act_high(u - 1)
                act_high(IT * half + IT - 1)
                if not half:
                    for b in range(3):
                        ln_high(2 * B + b)
            act.wait_ge(m_up, 2 * IT)
            for k in range(KT):
                late_high(C_WQ1 + k)

            def q1_high(n):
                half, m = n // M1, n % M1
                act.wait_ge(q1_mm, n + 1)
                act.activation(qT1[:, 0, m, half * 512:half * 512 + 512], bank[n % 4], ACT.Copy, scale=SCALE1
                               ).then_inc(q1_hi, 1)

            for b in (4, 5):
                ln_high(2 * B + b)
            for k in range(KT):
                late_high(C_WOUT + k)
            for n in range(M1):
                q1_high(n)
            for b in (6, 7):
                ln_high(2 * B + b)
            for n in range(M1, 2 * M1):
                q1_high(n)
            for w in range(UNITS1 + 10):
                if w >= 12 and (w - 12) % G1 == 0 and (w - 12) // G1 < B:
                    b = (w - 12) // G1
                    act.wait_ge(o1_T, b + 1)
                    act.copy(OT1[:, b % 2, 0], bank[7].rearrange("p (k t) -> p k t", k=KT)).then_inc(o1_hi, 1)
                if w >= 17 and (w - 17) % G1 == 0:
                    ln_high(3 * B + (w - 17) // G1)
                if 2 <= w < UNITS1 + 2:
                    v = w - 2
                    act.wait_ge(p1_T, v + 1)
                    if v >= 4:
                        act.wait_ge(o1_mm, v - 3)
                    act.copy(probT1[:, v % 4, :], bank[3 + v % 2]).then_inc(p1_copy, 1)
                if w < UNITS1:
                    act.wait_ge(s1_sub, w + 1)
                    act.activation(prob1[:, w % 4, :], prob1[:, w % 4, :], ACT.Exp).then_inc(s1_exp, 1)
            act.wait_ge(g1_mmT, 2)
            act.copy(logitT1, PS[0:NE, 6:8, :]).then_inc(g1_row, 1)
            act.wait_ge(g1_T, 1)
            act.wait_ge(eb_loaded, 16)
            act.copy(work[0:NE, 1:3, :], PS[0:NE, 6:8, :]).then_inc(g1_copy, 1)
            with act.Fori(1, NE // 2) as i:
                for par in range(2):
                    act.wait_ge(e_mm, 16 * i + B * par - B)
                    for k in range(KT):
                        c0 = C_EX + KT * par + k
                        act.wait_ge(raw_loaded[c0 % 4], 32 * i + 16 * (c0 // 4 + 1))
                        act.copy(Ex[par][:, 0, k, :], raw[:, c0 % 4, :]).then_inc(ex_hi, 1)

        @block.vector
        def _(dve):
            links = [0]

            def link(ins):
                links[0] += 1
                ins.then_inc(chain, 1)
                dve.wait_ge(chain, links[0])

            def first_lo(a):
                _, hi, lo = first_chunk(a)
                dve.wait_ge(a_hi, a + 1)
                dve.tensor_tensor(lo, work[:, a % 8, :], f32(hi), ALU.subtract).then_inc(a_lo, 1)

            def ln_stats(t):
                b = t % B
                if t < B:
                    dve.wait_ge(x_loaded[b], 16)
                link(dve.bn_stats(stats[:, t % 2, :], X[:, b, :]))
                link(dve.bn_aggr(meanvar[:, b, :], stats[:, t % 2, :]))
                dve.tensor_scalar(vareps[:, b:b + 1], meanvar[:, b, 1:2], LN_EPS, None, ALU.add).then_inc(ln_stat, 1)

            def ln_rows(t):
                b = t % B
                dve.wait_ge(ln_rstd, t + 1)
                if t % B >= 2:
                    dve.wait_ge(ln_T, t - 1)
                dve.tensor_scalar(hrow[:, t % 2, :], X[:, b, :], meanvar[:, b, 0:1], rstd[:, b:b + 1],
                                  ALU.subtract, ALU.mult).then_inc(ln_row, 1)

            def ln_low(t):
                b = t % B
                hi, lo = hilo(HT, A, slice(b * P, (b + 1) * P))
                dve.wait_ge(ln_hi, t + 1)
                dve.tensor_tensor(lo, lnbank(t).rearrange("p (k t) -> p k t", k=KT), f32(hi), ALU.subtract).then_inc(ln_lo, 1)

            def job_lo(n):
                if not HAS_LO[n]:
                    return
                dve.wait_ge(kv_hi, n + 1)
                if JOBS[n][0] == "k1":
                    t = JOBS[n][1] * 512
                    hi, lo = hilo(KT1, slice(t, t + 512))
                else:
                    hi, lo = stage[:, STORE[n] % 4, 0, :], stage[:, STORE[n] % 4, 1, :]
                dve.tensor_tensor(lo, bank[n % 4], f32(hi), ALU.subtract).then_inc(kv_lo, 1)

            dve.wait_ge(consts_made, 2)
            dve.tensor_copy(identr, ident[:, :]).then_inc(identr_made, 1)
            for a in range(8):
                first_lo(a)
            for l in range(2):
                dve.wait_ge(gatew_hi, l + 1)
                dve.tensor_tensor(gw[:, l, 1], graww[:, l], f32(gw[:, l, 0]), ALU.subtract).then_inc(gatew_lo, 1)
            ln_stats(0)
            ln_stats(1)
            for a in range(8, 12):
                first_lo(a)
            ln_rows(0)
            ln_rows(1)
            ln_stats(2)
            ln_stats(3)
            job_lo(0)
            job_lo(1)
            first_lo(12)
            first_lo(13)
            job_lo(2)
            first_lo(14)
            first_lo(15)
            job_lo(3)
            for t in range(4, B):
                ln_stats(t)
            job_lo(4)
            for b in range(B):
                ln_low(b)
                if b + 2 < B:
                    ln_rows(b + 2)
                job_lo(5 + b)
            for n in range(5 + B, len(JOBS)):
                job_lo(n)

            def q_low(index, h, half):
                dve.wait_ge(q_hi, index + 1)
                dve.scalar_tensor_tensor(out=qT[:, half, 1, h, :], in0=bank[6 + h % 2], scalar=SCALE0,
                                         in1=f32(qT[:, half, 0, h, :]), op0=ALU.mult, op1=ALU.subtract).then_inc(q_lo, 1)

            for h in range(QUAD):
                q_low(h, h, 0)
            dve.wait_ge(gates_tanh, 1)
            dve.wait_ge(gb_loaded, 32)
            for v in (gam, bet):
                dve.tensor_scalar(v, v, gate[:, 2:3], None, ALU.mult).then_inc(gb_made, 1)

            def maxima(i, c, k):
                dve.wait_ge(s_mm, 2 * (16 * i + c) + k + 1)
                dve.tensor_reduce(nmax[:, c % 2, 2 * k:2 * k + 2], bank[k].rearrange("p (h t) -> p h t", h=2),
                                  AX_X, ALU.max, negate=True).then_inc(s_max, 1)

            def step(i, c):
                n = number(i, c)
                if n is None or n < STEPS:
                    maxima(i, c, 0)
                if n is None or n >= 2:
                    dve.wait_ge(o_hi, 16 * i + c - 1)
                    dve.tensor_tensor(OT[:, 1, :], bank[4], f32(OT[:, 0, :]), ALU.subtract).then_inc(o_lo, 1)
                if n is not None and n >= STEPS - 4:
                    ln_low(B + n - (STEPS - 4))
                if n is None or n < STEPS:
                    maxima(i, c, 1)
                if n is not None and n >= STEPS - 5:
                    ln_rows(B + n - (STEPS - 5))
                if n is None or n < STEPS:
                    dve.wait_ge(s_exp, 2 * (16 * i + c) + 2)
                    dve.reciprocal(rinv[:, c % 2, :], psumr[:, c % 2, :]).then_inc(s_rcp, 1)
                if n is None or n < STEPS - QUAD:
                    h, at = c % QUAD, (c // QUAD + 1) % 2
                    dve.wait_ge(q_hi, 16 * i + c + QUAD + 1)
                    dve.scalar_tensor_tensor(out=qT[:, at, 1, h, :], in0=bank[6 + c % 2], scalar=SCALE0,
                                             in1=f32(qT[:, at, 0, h, :]), op0=ALU.mult, op1=ALU.subtract).then_inc(q_lo, 1)
                if (n is None or n >= 1) and (n is None or n <= STEPS):
                    for k in range(2):
                        dve.wait_ge(pt_hi, 2 * (16 * i + c - 1) + k + 1)
                        dve.tensor_tensor(PT[:, 1, k, :], bank[2 + k], f32(PT[:, 0, k, :]), ALU.subtract).then_inc(pt_lo, 1)
                if n is None or n >= 2:
                    dve.wait_ge(y_mm, 16 * i + c - 1)
                    b = (c - 2) % B
                    dve.scalar_tensor_tensor(out=X[:, b, :], in0=bank[5], scalar=gate[:, 0:1], in1=X[:, b, :],
                                             op0=ALU.mult, op1=ALU.add).then_inc(y_acc, 1)
                if n is not None and n >= STEPS - 6:
                    dve.wait_ge(y_acc, n - 1)
                    ln_stats(B + n - (STEPS - 6))

            steps_of(dve, step)
            ln_rows(2 * B - 1)
            ln_low(2 * B - 2)
            ln_low(2 * B - 1)

            def z_part(b):
                dve.wait_ge(m_down, b + 1)
                link(dve.tensor_tensor(zrow[:, b % 2, :], bank[4 + b % 2], work[:, b % HALF, :], ALU.add))
                link(dve.bn_stats(stats[:, b % 2, :], zrow[:, b % 2, :]))
                link(dve.bn_aggr(zmv[:, b, :], stats[:, b % 2, :]))
                dve.tensor_scalar(zve[:, b:b + 1], zmv[:, b, 1:2], LN_EPS, None, ALU.add).then_inc(z_stat, 1)

            def z_add(b):
                z = zrow[:, b % 2, :]
                dve.wait_ge(z_rstd, b + 1)
                link(dve.tensor_scalar(z, z, zmv[:, b, 0:1], zrs[:, b:b + 1], ALU.subtract, ALU.mult))
                link(dve.tensor_tensor(z, z, gam, ALU.mult))
                dve.wait_ge(xbeta, b + 1)
                link(dve.tensor_tensor(X[:, b, :], X[:, b, :], z, ALU.add))
                ln_stats(2 * B + b)

            for half in range(2):
                for k in range(LT):
                    dve.wait_ge(m_xl_hi, 4 * half + k + 1)
                    dve.tensor_tensor(xlT[:, 1, k, :], bank[k], f32(xlT[:, 0, k, :]), ALU.subtract).then_inc(m_xl_lo, 1)
                dve.wait_ge(m_gate, half + 1)
                for b in range(HALF):
                    t8 = dve.max(top0[:, b, :], bank[3][:, b * NE:(b + 1) * NE])
                link(t8)
                dve.tensor_tensor(route[:, half * HALF:(half + 1) * HALF].unsqueeze(2), top0[:, :, 0:1], top0[:, :, 1:2],
                                  ALU.add).then_inc(m_route, 1)
                if half:
                    ln_low(2 * B + 3)
                for k in range(LT):
                    dve.wait_ge(m_xl_hi, 4 * half + LT + k + 1)
                    dve.tensor_tensor(eoT[:, 1, k, :], bank[2 + k], f32(eoT[:, 0, k, :]), ALU.subtract).then_inc(m_xl_lo, 1)
                dve.wait_ge(m_route, half + 1)
                for b in range(HALF):
                    r = half * HALF + b
                    dve.wait_ge(m_fc2, r + 1)
                    dve.tensor_scalar(work[:, b, :], bank[4 + b % 2], route[:, r:r + 1], None, ALU.mult).then_inc(m_fc2_out, 1)
                for u in range(IT * half, IT * half + IT):
                    dve.wait_ge(m_relu, u + 1)
                    dve.tensor_tensor(hrow[:, u % 2, :], hrow[:, u % 2, :], hrow[:, u % 2, :], ALU.mult).then_inc(m_sq, 1)
                if half:
                    for h in range(4):
                        dve.tensor_scalar(maskr[:, h * P:(h + 1) * P], mask8[:, :], 1.0, -MASKED, ALU.subtract, ALU.mult
                                          ).then_inc(mask_made, 1)
                    z_part(4)
                    z_add(4)
                    z_part(5)
                    z_add(5)
                    ln_rows(2 * B + 4)
                    z_part(6)
                    z_add(6)
                    ln_rows(2 * B + 5)
                    ln_low(2 * B + 4)
                    z_part(7)
                    z_add(7)
                    ln_low(2 * B + 5)
                    ln_rows(2 * B + 6)
                    ln_rows(2 * B + 7)
                else:
                    for b in range(HALF):
                        z_part(b)
                        z_add(b)
                        if 1 <= b <= 2:
                            ln_rows(2 * B + b - 1)
                    ln_rows(2 * B + 2)
                    ln_low(2 * B)
                    ln_low(2 * B + 1)
                    ln_rows(2 * B + 3)
                    ln_low(2 * B + 2)

            def q1_low(n):
                half, m = n // M1, n % M1
                hi, lo = hilo(qT1, m, slice(half * 512, half * 512 + 512))
                dve.wait_ge(q1_hi, n + 1)
                dve.scalar_tensor_tensor(out=lo, in0=bank[n % 4], scalar=SCALE1, in1=f32(hi),
                                         op0=ALU.mult, op1=ALU.subtract).then_inc(q1_lo, 1)

            for n in range(M1):
                q1_low(n)
            ln_low(2 * B + 6)
            ln_low(2 * B + 7)
            for n in range(M1, 2 * M1):
                q1_low(n)
            for w in range(UNITS1 + 10):
                v = w - 4
                if 0 <= v < UNITS1 and v % 4 == 3:
                    b, half = v // G1, v % G1 // 4
                    o = bank[5 + half][:, 0:16 * (D1 + 1)].rearrange("p (h d) -> p h d", h=16)
                    dve.wait_ge(o1_mm, v + 1)
                    link(dve.reciprocal(rsum1[:, half, :].unsqueeze(2), o[:, :, D1:D1 + 1]))
                    if half == 0 and b >= 2:
                        dve.wait_ge(ln_T, 3 * B + b - 1)
                    dve.tensor_tensor(hrow[:, b % 2, half * 256:half * 256 + 256].rearrange("p (h d) -> p h d", h=16),
                                      o[:, :, 0:D1], rsum1[:, half, :].unsqueeze(2).broadcast_to([P, 16, D1]), ALU.mult
                                      ).then_inc(o1_row, 1)
                if w >= 14 and (w - 14) % G1 == 0 and (w - 14) // G1 < B:
                    b = (w - 14) // G1
                    dve.wait_ge(y1_mm, b + 1)
                    dve.scalar_tensor_tensor(out=X[:, b, :], in0=bank[7], scalar=gate[:, 1:2], in1=X[:, b, :],
                                             op0=ALU.mult, op1=ALU.add).then_inc(y1_acc, 1)
                if w < UNITS1:
                    sc = bank[w % 3].rearrange("p (h t) -> p h t", h=SHARE1)
                    dve.wait_ge(s1_mm, w + 1)
                    dve.tensor_reduce(max1[:, w % 2, :], sc, AX_X, ALU.max).then_inc(s1_max, 1)
                    dve.wait_ge(s1_max, w + 1)
                    if w >= 4:
                        dve.wait_ge(p1_T, w - 3)
                    dve.tensor_tensor(prob1[:, w % 4, :].rearrange("p (h t) -> p h t", h=SHARE1), sc,
                                      max1[:, w % 2, :].unsqueeze(2).broadcast_to([P, SHARE1, P]), ALU.subtract
                                      ).then_inc(s1_sub, 1)
                if w >= 12 and (w - 12) % G1 == 0 and (w - 12) // G1 < B:
                    b = (w - 12) // G1
                    dve.wait_ge(o1_hi, b + 1)
                    dve.tensor_tensor(OT1[:, b % 2, 1], bank[7].rearrange("p (k t) -> p k t", k=KT), f32(OT1[:, b % 2, 0]),
                                      ALU.subtract).then_inc(o1_lo, 1)
                if w >= 14 and (w - 14) % G1 == 0 and (w - 14) // G1 < B:
                    b = (w - 14) // G1
                    dve.wait_ge(y1_acc, b + 1)
                    ln_stats(3 * B + b)
                if w >= 15 and (w - 15) % G1 == 0 and (w - 15) // G1 < B:
                    b = (w - 15) // G1
                    dve.wait_ge(ln_rstd, 3 * B + b + 1)
                    dve.wait_ge(o1_T, b + 1)
                    dve.tensor_scalar(hrow[:, b % 2, :], X[:, b, :], meanvar[:, b, 0:1], rstd[:, b:b + 1],
                                      ALU.subtract, ALU.mult).then_inc(ln_row, 1)
                if w >= 17 and (w - 17) % G1 == 0:
                    ln_low(3 * B + (w - 17) // G1)

            dve.wait_ge(g1_mm, 1)
            link(dve.tensor_tensor(logit1[:, :, :], bank[6][:, 0:B * NE].rearrange("p (b e) -> p b e", b=B),
                                   gb1[:, :].unsqueeze(1).broadcast_to([P, B, NE]), ALU.add))
            for b in range(B):
                t8 = dve.max(top1[:, b, :], logit1[:, b, :])
            link(t8)
            for b in range(B):
                t8 = dve.max_index(idx1[:, b, :], top1[:, b, :], logit1[:, b, :])
            link(t8)
            link(dve.tensor_copy(idxf[:, :].unsqueeze(2), idx1[:, :, 0:1]))
            dve.tensor_tensor(sel[:, :, :], iota8[:, :].unsqueeze(1).broadcast_to([P, B, NE]),
                              idxf[:, :].unsqueeze(2).broadcast_to([P, B, NE]), ALU.is_equal).then_inc(g1_sel, 1)
            dve.wait_ge(g1_sel, 1)
            dve.tensor_scalar(sel[:, :, :], sel[:, :, :], gate[:, 3:4], None, ALU.mult).then_inc(g1_sel, 1)
            dve.wait_ge(g1_sel, 2)

            def add_expert(i, par, b):
                dve.wait_ge(e_mm, 16 * i + B * par + b + 1)
                if not isinstance(i, int):
                    weight = sel[:, b, bass.ds(2 * i + par, 1)]
                else:
                    weight = sel[:, b, 2 * i + par:2 * i + par + 1]
                if not isinstance(i, int) or par:
                    dve.wait_ge(e_acc, 16 * i + B * par + b + 1 - B)
                dve.scalar_tensor_tensor(out=X[:, b, :], in0=expert_bank(i, par, b), scalar=weight, in1=X[:, b, :],
                                         op0=ALU.mult, op1=ALU.add).then_inc(e_acc, 1)

            for par in range(2):
                for b in range(B):
                    add_expert(0, par, b)
            for b in range(B):
                dve.wait_ge(b1_mm, b + 1)
                dve.wait_ge(e_acc, B + b + 1)
                dve.tensor_tensor(X[:, b, :], bank[6 + b % 2], X[:, b, :], ALU.add).then_inc(b1_acc, 1)
            dve.wait_ge(b1_acc, B)
            with dve.Fori(1, NE // 2) as i:
                for par in range(2):
                    for b in range(B):
                        add_expert(i, par, b)

        @block.tensor
        def _(pe):
            def ln_transpose(t):
                if t < 3 * B and t % B >= 2:
                    pe.wait_ge(ln_lo, t - 1)
                pe.wait_ge(ln_row, t + 1)
                for k in range(KT):
                    mm = pe.transpose(lnbank(t)[:, k * P:(k + 1) * P], hrow[:, t % 2, k * P:(k + 1) * P], ident[:, :])
                mm.then_inc(ln_T, 1)

            def tokens(buf, k, t0, n):
                return hilo(buf, k, slice(t0, t0 + n))

            def job(n):
                kind = JOBS[n][0]
                if n >= 4:
                    if HAS_LO[n - 4]:
                        pe.wait_ge(kv_lo, LOS[n - 4])
                    else:
                        pe.wait_ge(kv_hi, n - 3)
                acc = bank[n % 4]
                if kind == "K":
                    _, part, h, half = JOBS[n]
                    src = HT if part else CT
                    mm = contract(pe, acc, [(tokens(Wk_r, k, h * P, P), tokens(src, k, half * 512, 512)) for k in range(KT)])
                elif kind == "V":
                    _, part, b = JOBS[n]
                    src = HT if part else CT
                    mm = contract(pe, acc, [(tokens(src, k, b * P, P), tokens(Wv_r, k, 0, 512)) for k in range(KT)])
                elif kind in ("k1", "v1"):
                    w, half = wk1_r if kind == "k1" else wv1_r, JOBS[n][1]
                    mm = contract(pe, acc, [(tokens(w, k, 0, P), tokens(CT, k, half * 512, 512)) for k in range(KT)])
                else:
                    half = JOBS[n][1]
                    for b in range(HALF):
                        mm = pe.transpose(acc[:, b * P:(b + 1) * P], work[:, 6 + half, b * P:(b + 1) * P], ident[:, :])
                mm.then_inc(kv_mm, 1)

            for n in range(NCTX):
                if n == 0:
                    pe.wait_ge(a_lo, 8)
                elif n == 4:
                    pe.wait_ge(a_lo, 12)
                elif n == 8:
                    pe.wait_ge(a_lo, NA)
                job(n)
                if n == 4:
                    pe.wait_ge(consts_made, 2)
                if 4 <= n < 4 + B:
                    ln_transpose(n - 4)
            pe.wait_ge(chunk_split, 2)
            for n in range(NCTX, NCTX + 4):
                job(n)
            for half in range(2):
                pe.wait_ge(kv_hi, NCTX + 3 + half)
                job(NCTX + 4 + half)
            pe.wait_ge(ln_lo, B)
            for n in range(NCTX + 6, len(JOBS)):
                job(n)

            def queries(at, acc, slot, h, half):
                return contract(pe, acc, [(tokens(Wq_r[:, slot], k, h * P, P), tokens(HT, k, half * 512, 512))
                                          for k in range(KT)]).then_inc(q_mm, 1)

            pe.wait_ge(chunk_split, C_WO0)
            for h in range(QUAD):
                if h >= 2:
                    pe.wait_ge(q_lo, h - 1)
                queries(h, bank[6 + h % 2], 0, h, 0)

            def step(i, c):
                n = number(i, c)
                half, bb = c // QUAD % 2, c % QUAD
                if n is None or n < STEPS:
                    pe.wait_ge(q_lo, 16 * i + QUAD * (c // QUAD) + QUAD)
                    pe.wait_ge(k_loaded[c % 2], 128 * i + 16 * (c // 2 + 1))
                    for k in range(2):
                        if n is not None and n == 0:
                            pe.wait_ge(kv_lo, LOS[-1])
                        else:
                            pe.wait_ge(s_exp, 2 * (16 * i + c - 1) + k + 1)
                        for h in (2 * k, 2 * k + 1):
                            w = hilo(qT[:, half], h, slice(bb * P, (bb + 1) * P))
                            mm = product(pe, bank[k][:, (h % 2) * KEYS:(h % 2 + 1) * KEYS], w, hilo(Kb[:, c % 2]), True, True)
                        mm.then_inc(s_mm, 1)
                if n is None or n < STEPS - QUAD:
                    nxt = c // QUAD + 1
                    pe.wait_ge(q_lo, 16 * i + c + QUAD - 1)
                    if n is None or nxt >= 2:
                        pe.wait_ge(chunk_split, C_STEP + 16 * i + B * (nxt // 2 - 1) + KT)
                    queries(n, bank[6 + c % 2], nxt // 2 % 2, c % QUAD, nxt % 2)
                if (n is None or n >= 1) and (n is None or n <= STEPS):
                    pe.wait_ge(p_norm, 16 * i + c)
                    for k in range(2):
                        if n is None or n >= 2:
                            pe.wait_ge(pt_lo, 2 * (16 * i + c - 2) + k + 1)
                        for h in range(QUAD):
                            mm = pe.transpose(bank[2 + k][:, h * P:(h + 1) * P],
                                              prob[:, (c - 1) % 2, h * KEYS + k * P:h * KEYS + (k + 1) * P], ident[:, :])
                        mm.then_inc(p_T, 1)
                if n is None or n >= 2:
                    pe.wait_ge(o_lo, 16 * i + c - 1)
                    pe.wait_ge(chunk_split, C_STEP + 16 * i + B * ((c - 2) // B))
                    if n is None or n >= 3:
                        pe.wait_ge(y_acc, 16 * i + c - 2)
                    mm = contract(pe, bank[5], [(hilo(OT, slice(h * P, (h + 1) * P)), hilo(Wo_r[:, (c - 2) // B % 2], h))
                                                for h in range(QUAD)])
                    mm.then_inc(y_mm, 1)
                if (n is None or n >= 1) and (n is None or n <= STEPS):
                    pe.wait_ge(v_loaded[(c - 1) % 2], 128 * i + 16 * ((c - 1) // 2 + 1))
                    if n is None or n >= 2:
                        pe.wait_ge(o_lo, 16 * i + c - 1)
                    for k in range(2):
                        pe.wait_ge(pt_lo, 2 * (16 * i + c - 1) + k + 1)
                        mm = product(pe, bank[4], hilo(Vb[:, (c - 1) % 2], k), hilo(PT, k), k == 0, k == 1)
                    mm.then_inc(o_mm, 1)
                if n is not None and n >= STEPS - 5:
                    if n < STEPS - 3:
                        pe.wait_ge(q_lo, STEPS)
                    ln_transpose(B + n - (STEPS - 5))

            steps_of(pe, step)

            def gate_logits(half):
                pe.wait_ge(gatew_lo, 2)
                pe.wait_ge(identr_made, 1)
                contract(pe, bank[3], [(gate_wide(0, k), tokens(HT, k, half * 512, 512)) for k in range(KT)]).then_inc(m_gateT, 1)

            def gate_rows(half):
                pe.wait_ge(m_gate_row, half + 1)
                for b in range(HALF):
                    mm = pe.transpose(bank[3][:, b * NE:(b + 1) * NE], logitT[:, b * P:(b + 1) * P], ident[0:NE, 0:NE])
                mm.then_inc(m_gate, 1)

            def latent(half):
                pe.wait_ge(chunk_split, C_FC + 2)
                for m in range(LT):
                    mm = contract(pe, bank[m], [(tokens(fc1_r, k, m * P, P), tokens(HT, k, half * 512, 512)) for k in range(KT)])
                    mm.then_inc(m_xl, 1)

            def latent_expert(half):
                pe.wait_ge(chunk_split, C_FC + 3)
                pe.wait_ge(m_xl_lo, 4 * half + LT)
                pe.wait_ge(m_route, half + 1)
                for m in range(LT):
                    mm = contract(pe, bank[2 + m], [(tokens(lat_r, k, m * P, P), hilo(xlT, k)) for k in range(LT)])
                    mm.then_inc(m_xl, 1)

            def latent_out(half):
                pe.wait_ge(chunk_split, C_FC + 5)
                pe.wait_ge(m_xl_lo, 4 * half + 2 * LT)
                for b in range(HALF):
                    r = half * HALF + b
                    if r >= 2:
                        pe.wait_ge(m_fc2_out, r - 1)
                    mm = contract(pe, bank[4 + b % 2], [(tokens(eoT, k, b * P, P), hilo(fc2_r, k)) for k in range(LT)])
                    mm.then_inc(m_fc2, 1)

            def up(half):
                pe.wait_ge(chunk_split, C_UP + 8)
                for u in range(IT * half, IT * half + IT):
                    if u % IT < 4:
                        pe.wait_ge(m_xl_lo, 4 * half + 2 * LT)
                    else:
                        pe.wait_ge(m_relu, u - 3)
                    mm = contract(pe, bank[u % 4], [(tokens(up_r, k, (u % IT) * P, P), tokens(HT, k, half * 512, 512))
                                                    for k in range(KT)])
                    mm.then_inc(m_up, 1)

            def down(b):
                if b % HALF == 0:
                    pe.wait_ge(chunk_split, C_DOWN + IT)
                    pe.wait_ge(m_sq_lo, IT * (b // HALF + 1))
                if b % HALF < 2:
                    pe.wait_ge(m_fc2_out, HALF * (b // HALF + 1))
                else:
                    pe.wait_ge(z_stat, b - 1)
                mm = contract(pe, bank[4 + b % 2], [(tokens(actT, k, (b % HALF) * P, P), hilo(down_r, k)) for k in range(IT)])
                mm.then_inc(m_down, 1)

            pe.wait_ge(s_exp, 2 * STEPS)
            pe.wait_ge(pt_lo, 2 * STEPS)
            pe.wait_ge(o_lo, STEPS)
            pe.wait_ge(y_acc, STEPS)
            pe.wait_ge(ln_lo, B + HALF)
            gate_logits(0)
            ln_transpose(2 * B - 1)
            latent(0)
            gate_rows(0)
            latent_expert(0)
            latent_out(0)
            up(0)
            for b in range(HALF):
                down(b)
            for b in range(3):
                ln_transpose(2 * B + b)
            pe.wait_ge(m_relu, IT)
            pe.wait_ge(ln_lo, 2 * B)
            gate_logits(1)
            latent(1)
            gate_rows(1)
            ln_transpose(2 * B + 3)
            latent_expert(1)
            latent_out(1)
            up(1)
            down(4)
            down(5)
            down(6)
            ln_transpose(2 * B + 4)
            down(7)
            ln_transpose(2 * B + 5)

            def queries1(n):
                half, m = n // M1, n % M1
                if n < 4:
                    pe.wait_ge(m_relu, 2 * IT)
                else:
                    pe.wait_ge(q1_lo, n - 3)
                mm = contract(pe, bank[n % 4], [(tokens(wq1_r, k, m * P, P), tokens(HT, k, half * 512, 512)) for k in range(KT)])
                mm.then_inc(q1_mm, 1)

            pe.wait_ge(chunk_split, C_WOUT)
            pe.wait_ge(ln_lo, 2 * B + HALF)
            for n in range(M1):
                queries1(n)
            ln_transpose(2 * B + 6)
            ln_transpose(2 * B + 7)
            pe.wait_ge(ln_lo, 3 * B)
            for n in range(M1, 2 * M1):
                queries1(n)
            pe.wait_ge(mask_made, 4)
            pe.wait_ge(identr_made, 1)
            pe.wait_ge(z_stat, B)
            def expert(i, par, b):
                if b == 0:
                    pe.wait_ge(chunk_split, C_EX + 8 * i + KT * par + KT)
                if not (isinstance(i, int) and par == 0 and b < 6):
                    pe.wait_ge(e_acc, 16 * i + 8 * par + b - 3)
                mm = contract(pe, expert_bank(i, par, b), [(tokens(HT, k, b * P, P), hilo(Ex[par], k)) for k in range(KT)])
                mm.then_inc(e_mm, 1)

            def gate_logits1(half):
                return contract(pe, bank[6 + half], [(gate_wide(1, k), tokens(HT, k, half * 512, 512)) for k in range(KT)]
                                ).then_inc(g1_mmT, 1)

            for w in range(UNITS1 + 9):
                if w < UNITS1:
                    b, m, acc = w // G1, w % G1 // 2, bank[w % 3]
                    if w == 0:
                        pe.wait_ge(q1_lo, 2 * M1)
                    if w >= 3:
                        pe.wait_ge(s1_sub, w - 2)
                    if w % 2 == 0:
                        pe.wait_ge(kb_loaded[m], 16 * HT1 * (b + 1))
                    pe.matmul(acc, identr, maskr, start=True, stop=False)
                    first = SHARE1 * (w % 2)
                    product(pe, acc, tokens(qT1, m, b * P, P), hilo(KB[:, m], slice(first, first + SHARE1)), False, True
                            ).then_inc(s1_mm, 1)
                if 2 <= w < UNITS1 + 2:
                    v = w - 2
                    pe.wait_ge(s1_exp, v + 1)
                    if v >= 2:
                        pe.wait_ge(p1_copy, v - 1)
                    for h in range(SHARE1):
                        mm = pe.transpose(bank[3 + v % 2][:, h * P:(h + 1) * P], prob1[:, v % 4, h * P:(h + 1) * P], ident[:, :])
                    mm.then_inc(p1_T, 1)
                v = w - 3
                if 0 <= v < UNITS1:
                    b, g = v // G1, v % G1
                    pe.wait_ge(p1_copy, v + 1)
                    if g % 4 == 0 and b >= 1:
                        pe.wait_ge(o1_row, 2 * b - 1 + g // 4)
                    for h in range(SHARE1):
                        at = (g % 4 * SHARE1 + h) * (D1 + 1)
                        mm = pe.matmul(bank[5 + g // 4][:, at:at + D1 + 1], probT1[:, v % 4, h * P:(h + 1) * P],
                                       V1[:, b, g, :], start=True, stop=True)
                    mm.then_inc(o1_mm, 1)
                if w >= 11 and (w - 11) % G1 == 0 and (w - 11) // G1 < B:
                    b = (w - 11) // G1
                    pe.wait_ge(o1_row, 2 * b + 2)
                    if b:
                        pe.wait_ge(ln_lo, 3 * B + b)
                    for k in range(KT):
                        mm = pe.transpose(bank[7][:, k * P:(k + 1) * P], hrow[:, b % 2, k * P:(k + 1) * P], ident[:, :])
                    mm.then_inc(o1_T, 1)
                if w >= 13 and (w - 13) % G1 == 0 and (w - 13) // G1 < B:
                    b = (w - 13) // G1
                    if b == 0:
                        pe.wait_ge(chunk_split, C_EX)
                    pe.wait_ge(o1_lo, b + 1)
                    mm = contract(pe, bank[7], [(hilo(OT1[:, b % 2], k), hilo(wout_r, k)) for k in range(KT)])
                    mm.then_inc(y1_mm, 1)
                if w >= 16 and (w - 16) % G1 == 0:
                    b = (w - 16) // G1
                    pe.wait_ge(y1_acc, b + 1)
                    ln_transpose(3 * B + b)
                if w == UNITS1 + 3:
                    pe.wait_ge(s1_sub, UNITS1)
                    pe.wait_ge(p1_copy, UNITS1)
                    expert(0, 0, 0)
                    expert(0, 0, 1)
                if w == UNITS1 + 5:
                    pe.wait_ge(o1_row, 2 * B)
                    expert(0, 0, 2)
                    gate_logits1(0)
                    expert(0, 0, 3)
                    expert(0, 0, 4)

            expert(0, 0, 5)
            pe.wait_ge(ln_lo, 4 * B)
            gate_logits1(1)
            pe.wait_ge(g1_row, 1)
            for t in range(B):
                mm = pe.transpose(bank[6][:, t * NE:(t + 1) * NE], logitT1[:, t // HALF, t % HALF * P:(t % HALF + 1) * P],
                                  ident[0:NE, 0:NE])
            mm.then_inc(g1_mm, 1)
            expert(0, 0, 6)
            expert(0, 0, 7)
            pe.wait_ge(g1_sel, 2)
            for b in range(B):
                mm = pe.transpose(PS[0:NE, 6 + b // 4, (b % 4) * P:(b % 4 + 1) * P], sel[:, b, :], ident[:, :])
            mm.then_inc(g1_T, 1)
            for b in range(B):
                expert(0, 1, b)
            pe.wait_ge(g1_copy, 1)
            for b in range(B):
                if b >= 2:
                    pe.wait_ge(b1_acc, b - 1)
                pe.matmul(bank[6 + b % 2], work[0:NE, 1 + b // 4, (b % 4) * P:(b % 4 + 1) * P], work[0:NE, 0, :],
                          start=True, stop=True).then_inc(b1_mm, 1)
            with pe.Fori(1, NE // 2) as i:
                for par in range(2):
                    for b in range(B):
                        expert(i, par, b)


_ORDER = ["x", "ctxT", "mask", "g_xattn", "g_ffn", "Wq", "Wk", "Wv", "Wo", "gate0", "up_w", "down_w", "fc1_w", "fc2_w",
          "latent_w", "ln_gamma", "ln_beta", "wqT", "wkT", "wvT", "woutT", "gate1T", "gate1_b", "expertT", "expert_b"]


def kernel(**inputs):
    import numpy as _np
    import concourse.bacc as _bacc
    from concourse import mybir as _mybir
    from concourse.bass_utils import run_bass_kernel_spmd as _run

    a = {k: _np.asarray(v) for k, v in inputs.items()}
    laid = {
        "x": a["x"],
        "ctxT": a["ctx_4096"].reshape(-1, a["ctx_4096"].shape[-1]).T,
        "mask": a["mask_SxS2_bk0"],
        "g_xattn": a["g_xattn"], "g_ffn": a["g_ffn"],
        "Wq": a["L0_xattn_Wq"], "Wk": a["L0_xattn_Wk"], "Wv": a["L0_xattn_Wv"], "Wo": a["L0_xattn_Wo"],
        "gate0": a["L0_ffn_gate_w"], "up_w": a["L0_ffn_up_w"], "down_w": a["L0_ffn_down_w"],
        "fc1_w": a["L0_ffn_fc1_w"], "fc2_w": a["L0_ffn_fc2_w"], "latent_w": a["L0_ffn_expert_w"],
        "ln_gamma": a["L0_ffn_ln_gamma"], "ln_beta": a["L0_ffn_ln_beta"],
        "wqT": a["L1_xattn_w_q"].T, "wkT": a["L1_xattn_w_k"].T, "wvT": a["L1_xattn_w_v"].T,
        "woutT": a["L1_xattn_w_out"].T,
        "gate1T": a["L1_ffn_gate_w"].T, "gate1_b": a["L1_ffn_gate_b"],
        "expertT": a["L1_ffn_expert_w"].transpose(0, 2, 1), "expert_b": a["L1_ffn_expert_b"],
    }
    nc = _bacc.Bacc("TRN2", target_bir_lowering=False, num_devices=1)
    arrays, args = {}, []
    for name in _ORDER:
        v = _np.ascontiguousarray(laid[name])
        arrays[f"in_{name}"] = v
        args.append(nc.dram_tensor(f"in_{name}", v.shape, _mybir.dt.from_np(v.dtype), kind="ExternalInput").ap())
    shape = a["x"].shape
    args.append(nc.dram_tensor("out_0", shape, _mybir.dt.float32, kind="ExternalOutput").ap())
    program(nc, *args)
    r = _run(nc, [arrays], core_ids=[0])
    return r.results[0]["out_0"]
```

```python
from contextlib import ExitStack

import concourse.bass as bass
from concourse import mybir


ALU = mybir.AluOpType
ACT = mybir.ActivationFunctionType
F32 = mybir.dt.float32
F32R = mybir.dt.float32r
U8 = mybir.dt.uint8
U32 = mybir.dt.uint32
I32 = mybir.dt.int32
AX_X = mybir.AxisListType.X

P = 128
B = 8
D = 512
KT = D // P
HALF = 4
LN_EPS = 1e-5

KVH = 4
GROUP = 8
QUAD = 4
NQUAD = KVH * GROUP // QUAD
STEPS = NQUAD * B
KEYS = 2 * P
SCALE0 = float(P) ** -0.5

H1 = 32
D1 = D // H1
G1 = 8
HT1 = P // D1
M1 = H1 // HT1
SHARE1 = H1 // G1
UNITS1 = B * G1
SCALE1 = float(D1) ** -0.5
MASKED = -3.0e38

NE = 8
TILES = B + NE - 1
CHOICE = 6
INT = 1024
LAT = 256
IT = INT // P
LT = LAT // P


def program(nc, x, ctxT, mask, g_xattn, g_ffn, Wq, Wk, Wv, Wo, gate0, up_w, down_w, fc1_w, fc2_w,
            latent_w, ln_gamma, ln_beta, wqT, wkT, wvT, woutT, gate1T, gate1_b, expertT, expert_b, out):
    ctx = ExitStack()
    with ctx:
        def sb(name, shape, dt=F32):
            return ctx.enter_context(nc.sbuf_tensor(name, shape, dt))

        def sem(name):
            return ctx.enter_context(nc.semaphore(name))

        PS = ctx.enter_context(nc.psum_tensor("PS", [P, 8, 512], F32))
        bank = [PS[:, k, :] for k in range(8)]

        X = sb("X", [P, B, D])
        work = sb("work", [P, 8, 512])
        prob = work[:, 0:4, :].rearrange("p (s a) c -> p s (a c)", s=2)
        prob1 = work[:, 0:4, :]
        probT1 = work[:, 4:8, :]
        gam = work[:, 4, :]
        bet = work[:, 5, :]
        logitT = work[0:NE, 6, :]
        zrow = work[:, 6:8, :]
        raw = sb("raw", [P, 4, 512])
        hrow = sb("hrow", [P, 2, 512])
        V1 = sb("V1", [P, B, G1, D1 + 1])
        ident = sb("ident", [P, P])
        iota8 = sb("iota8", [P, NE])
        graw = sb("graw", [P, 4])
        gate = sb("gate", [P, 4])
        stats = sb("stats", [P, 2, 6])
        meanvar = sb("meanvar", [P, B, 2])
        vareps = sb("vareps", [P, B])
        rstd = sb("rstd", [P, B])
        mhalf = sb("mhalf", [P, 1])
        zmv = sb("zmv", [P, B, 2])
        zve = sb("zve", [P, B])
        zrs = sb("zrs", [P, B])
        nmax = sb("nmax", [P, 2, QUAD])
        psumr = sb("psumr", [P, 2, QUAD])
        rinv = sb("rinv", [P, 2, QUAD])
        top0 = sb("top0", [P, HALF, 8])
        route = sb("route", [P, B])
        max1 = sb("max1", [P, 2, SHARE1])
        rsum1 = sb("rsum1", [P, 2, 16])
        gb1 = sb("gb1", [P, NE])
        gw1 = sb("gw1", [P, KT, NE])
        logit1 = sb("logit1", [P, NE])
        top1 = sb("top1", [P, 8])
        idx1 = sb("idx1", [P, 8], U32)
        idxf = sb("idxf", [P, 1])
        oneh = sb("oneh", [P, B, NE])
        chosen = sb("chosen", [P, B + 1, NE])
        slot = sb("slot", [P, B], U32)
        graww = hrow[:, 1, 512 - KT * NE:512].rearrange("p (k n) -> p k n", k=KT)
        mask8 = sb("mask8", [P, P], U8)
        tile_block = sb("tile_block", [1, 16], I32)

        END = (NE + 1) * 4096
        arena = sb("arena", [P, END], F32R)
        arena_end = sb("arena_end", [P, 1024 + P + 2 * KT * NE], F32R)
        late = sb("late", [P, 2048])

        def region(at, words):
            return arena[:, at:at + words] if at < END else arena_end[:, at - END:at - END + words]

        HT = region(0, 8192).rearrange("p (s k t) -> p s k t", s=2, k=KT)
        RA, RB, RC, RD, RE = 8192, 16384, 24576, 32768, 37888
        Wk_r = region(RB, 4096).rearrange("p (s k n) -> p s k n", s=2, k=KT)
        Wv_r = region(RB + 4096, 4096).rearrange("p (s k n) -> p s k n", s=2, k=KT)
        CT = region(RC, 8192).rearrange("p (s k t) -> p s k t", s=2, k=KT)
        wk1_r = region(RA + 4096, 1024).rearrange("p (s k n) -> p s k n", s=2, k=KT)
        wv1_r = region(RA + 5120, 1024).rearrange("p (s k n) -> p s k n", s=2, k=KT)
        stage = region(RD, 4096).rearrange("p (j s n) -> p j s n", j=4, s=2)
        Wq_r = region(RA, 8192).rearrange("p (j s k n) -> p j s k n", j=2, s=2, k=KT)
        Wo_r = region(RB, 8192).rearrange("p (j s h n) -> p j s h n", j=2, s=2, h=QUAD)
        qT = region(RC, 8192).rearrange("p (j s h t) -> p j s h t", j=2, s=2, h=QUAD)
        Kb = region(RD, 1024).rearrange("p (j s t) -> p j s t", j=2, s=2)
        Vb = region(RD + 1024, 1024).rearrange("p (j s k n) -> p j s k n", j=2, s=2, k=2)
        PT = region(RD + 2048, 2048).rearrange("p (s k n) -> p s k n", s=2, k=2)
        OT = region(RD + 4096, 1024).rearrange("p (s n) -> p s n", s=2)
        up_r = region(RA, 8192).rearrange("p (s k n) -> p s k n", s=2, k=KT)
        down_r = region(RB, 8192).rearrange("p (s k n) -> p s k n", s=2, k=IT)
        actT = region(RC, 8192).rearrange("p (s k t) -> p s k t", s=2, k=IT)
        xlT = actT[:, :, IT - 2 * LT:IT - LT]
        eoT = actT[:, :, IT - LT:IT]
        fc1_r = region(RD, 2048).rearrange("p (s k n) -> p s k n", s=2, k=KT)
        lat_r = region(RD + 2048, 1024).rearrange("p (s k n) -> p s k n", s=2, k=LT)
        fc2_r = [region(RD + 3072 + part * 1024, 1024).rearrange("p (k n) -> p k n", k=LT) for part in range(2)]
        wq1_r = region(RA, 4096).rearrange("p (s k n) -> p s k n", s=2, k=KT)
        wout_r = region(0, 4096).rearrange("p (s k n) -> p s k n", s=2, k=KT)
        KB = region(RB, 8192).rearrange("p (m s h t) -> p m s h t", m=M1, s=2, h=HT1)
        qT1 = region(RC, 8192).rearrange("p (f s m t) -> p f s m t", f=2, s=2, m=M1)
        OT1 = region(RD, 2048).rearrange("p (j s k t) -> p j s k t", j=2, s=2, k=KT)
        maskr = region(RD + 2048, 512)
        KT1 = late.bitcast(F32R).rearrange("p (s t) -> p s t", s=2)
        blocks = region(0, (NE + 1) * 4096).rearrange("p (q s k n) -> p q s k n", q=NE + 1, s=2, k=KT)
        Ex = [blocks[:, NE - e] for e in range(NE)]
        xs_raw = work[:, 0:4, :]
        XST = region(0, 2048).rearrange("p (j s k t) -> p j s k t", j=2, s=2, k=KT)
        ys = late.rearrange("p (j n) -> p j n", j=4)
        onehT = region(2048, B * P)[0:NE, :]
        ebias_r = region(RD + 4096, 1024).rearrange("p (s n) -> p s n", s=2)[0:NE]
        zeros = region(RD + 4096, 512).bitcast(F32)
        ebias = V1.rearrange("p b g d -> p (b g d)")[0:NE, 0:D]
        table = late[:, 1024:1536]
        before = table[:, 0:P]
        ones = table[:, P:2 * P]
        starts = table[:, 256:264]
        earlier = table[:, 264:328].rearrange("p (e f) -> p e f", e=NE)
        iota_tiles = table[:, 328:328 + TILES]
        tiles_of = table[:, 416:424]
        first_of = table[:, 424:432]
        slotf = table[:, 432:440]
        blockf = table[:, 440:440 + TILES]
        routing = late[:, 1536:1536 + P]
        gwords = 2 * KT * NE
        gw = region(RE, gwords).rearrange("p (s k n) -> p s k n", s=2, k=KT)
        identr = region(RE + gwords, P)

        def gate_wide(k):
            at = [RE + part * KT * NE + k * NE for part in range(2)]
            return region(at[0], P), region(at[1], P)


        Kscr = nc.dram_tensor("Kscr", [KVH, B, P, 2, KEYS], F32).ap()
        Vscr = nc.dram_tensor("Vscr", [KVH, B, P, 2, 2, P], F32).ap()

        Xscr = nc.dram_tensor("Xscr", [TILES * P, D], F32).ap()
        Yscr = nc.dram_tensor("Yscr", [TILES * P, D], F32).ap()

        small_loaded = sem("small_loaded")
        gates_tanh = sem("gates_tanh")
        consts_made = sem("consts_made")
        identr_made = sem("identr_made")
        gatew_hi = sem("gatew_hi")
        gatew_lo = sem("gatew_lo")
        x_loaded = [sem(f"x_loaded{b}") for b in range(B)]
        a_loaded = [sem(f"a_loaded{k}") for k in range(8)]
        a_hi = sem("a_hi")
        a_lo = sem("a_lo")
        raw_loaded = [sem(f"raw_loaded{k}") for k in range(4)]
        chunk_hi = sem("chunk_hi")
        late_hi = sem("late_hi")
        step_hi = sem("step_hi")
        ex_hi = sem("ex_hi")
        chunk_split = sem("chunk_split")
        ln_stat = sem("ln_stat")
        ln_rstd = sem("ln_rstd")
        ln_row = sem("ln_row")
        ln_T = sem("ln_T")
        ln_hi = sem("ln_hi")
        ln_lo = sem("ln_lo")
        kv_mm = sem("kv_mm")
        kv_hi = sem("kv_hi")
        kv_lo = sem("kv_lo")
        kv_stored = [sem(f"kv_stored{k}") for k in range(4)]
        k_loaded = [sem(f"k_loaded{k}") for k in range(2)]
        v_loaded = [sem(f"v_loaded{k}") for k in range(2)]
        q_mm = sem("q_mm")
        q_hi = sem("q_hi")
        q_lo = sem("q_lo")
        s_mm = sem("s_mm")
        s_max = sem("s_max")
        s_exp = sem("s_exp")
        s_rcp = sem("s_rcp")
        p_norm = sem("p_norm")
        p_T = sem("p_T")
        pt_hi = sem("pt_hi")
        pt_lo = sem("pt_lo")
        o_mm = sem("o_mm")
        o_hi = sem("o_hi")
        o_lo = sem("o_lo")
        y_mm = sem("y_mm")
        y_acc = sem("y_acc")
        chain = sem("chain")
        gb_loaded = sem("gb_loaded")
        eb_loaded = sem("eb_loaded")
        eb_hi = sem("eb_hi")
        eb_lo = sem("eb_lo")
        gb_made = sem("gb_made")
        xbeta = sem("xbeta")
        m_gateT = sem("m_gateT")
        m_gate_row = sem("m_gate_row")
        m_gate = sem("m_gate")
        m_route = sem("m_route")
        m_xl = sem("m_xl")
        m_xl_hi = sem("m_xl_hi")
        m_xl_lo = sem("m_xl_lo")
        m_fc2 = sem("m_fc2")
        m_fc2_out = sem("m_fc2_out")
        m_up = sem("m_up")
        m_relu = sem("m_relu")
        m_sq = sem("m_sq")
        m_sq_hi = sem("m_sq_hi")
        m_sq_lo = sem("m_sq_lo")
        m_down = sem("m_down")
        z_stat = sem("z_stat")
        z_rstd = sem("z_rstd")
        mask_made = sem("mask_made")
        kb_zero = sem("kb_zero")
        kb_loaded = [sem(f"kb_loaded{m}") for m in range(M1)]
        q1_mm = sem("q1_mm")
        q1_hi = sem("q1_hi")
        q1_lo = sem("q1_lo")
        s1_mm = sem("s1_mm")
        s1_max = sem("s1_max")
        s1_sub = sem("s1_sub")
        s1_exp = sem("s1_exp")
        p1_T = sem("p1_T")
        p1_copy = sem("p1_copy")
        o1_mm = sem("o1_mm")
        o1_rcp = sem("o1_rcp")
        o1_row = sem("o1_row")
        o1_T = sem("o1_T")
        o1_hi = sem("o1_hi")
        o1_lo = sem("o1_lo")
        y1_mm = sem("y1_mm")
        y1_acc = sem("y1_acc")
        tables_made = sem("tables_made")
        xscr_zero = sem("xscr_zero")
        ex_lo = sem("ex_lo")
        g1_rank = sem("g1_rank")
        slots_made = sem("slots_made")
        blocks_made = sem("blocks_made")
        xn_rows = sem("xn_rows")
        scattered = sem("scattered")
        xs_loaded = [sem(f"xs_loaded{k}") for k in range(4)]
        xs_T = sem("xs_T")
        xs_hi = sem("xs_hi")
        xs_lo = sem("xs_lo")
        y_copied = sem("y_copied")
        y_stored = [sem(f"y_stored{k}") for k in range(4)]
        yrow_loaded = [sem(f"yrow_loaded{b}") for b in range(B)]
        g1_xt = sem("g1_xt")
        g1_mm = sem("g1_mm")
        g1_part = sem("g1_part")
        g1_T = sem("g1_T")
        g1_copy = sem("g1_copy")
        b1_mm = sem("b1_mm")
        b1_acc = sem("b1_acc")
        e_mm = sem("e_mm")
        e_acc = sem("e_acc")
        out_stored = sem("out_stored")

        def kv_jobs(part):
            out = []
            for half in range(2):
                out += [("K", part, h, half) for h in range(KVH)]
                out += [("V", part, half * HALF + b) for b in range(HALF)]
            return out

        JOBS = kv_jobs(0) + [("k1", 0), ("k1", 1), ("v1", 0), ("v1", 1), ("v1t", 0), ("v1t", 1)] + kv_jobs(1)
        HAS_LO = [j[0] in ("K", "V", "k1") for j in JOBS]
        LOS = [sum(HAS_LO[:n + 1]) for n in range(len(JOBS))]
        STORE = [sum(j[0] in "KV" for j in JOBS[:n]) for n in range(len(JOBS))]
        NCTX = 16
        NA = 16

        C_WQ0 = 2
        C_WO0 = C_WQ0 + KT
        C_STEP = C_WO0 + QUAD
        C_UP = C_STEP + STEPS - B
        C_FC = C_UP + 8
        C_DOWN = C_FC + 5
        C_WQ1 = C_DOWN + IT
        C_WOUT = C_WQ1 + KT
        C_EX = C_WOUT + KT
        C_POOL = C_EX + 7 * KT
        C_ALL = C_EX + NE * KT
        ORDER = [6, 5, 7, 2, 1, 3, 4, 0]

        Wq_v = Wq.rearrange("(k p) n -> k p n", p=P)
        Wo_v = Wo.rearrange("(h p) n -> h p n", p=P)
        up_v = up_w.rearrange("(k p) n -> p k n", p=P)
        down_v = down_w.rearrange("(k p) n -> p k n", p=P)
        fc1_v = fc1_w.rearrange("(k p) n -> p k n", p=P)
        fc2_v = fc2_w.rearrange("(k p) n -> p k n", p=P)
        lat_v = latent_w.rearrange("(k p) n -> p k n", p=P)
        wq1_v = wqT.rearrange("(k p) n -> p k n", p=P)
        wout_v = woutT.rearrange("(k p) n -> p k n", p=P)
        ex_v = expertT.rearrange("e (k p) n -> e k p n", p=P)
        ctx_v = ctxT.rearrange("(k p) t -> p k t", p=P)
        Wk_v = Wk.rearrange("(k p) n -> p k n", p=P)
        Wv_v = Wv.rearrange("(k p) n -> p k n", p=P)

        def raw_as(c, parts):
            return raw[:, c % 4, :].rearrange("p (k n) -> p k n", k=parts)

        def mlp_chunk(c):
            if c < C_FC:
                k, n = (c - C_UP) // 2, (c - C_UP) % 2 * 512
                return up_v[:, k, n:n + 512], up_r[:, 0, k, n:n + 512], up_r[:, 1, k, n:n + 512], raw[:, c % 4, :]
            if c < C_FC + 2:
                k = (c - C_FC) * 2
                return fc1_v[:, k:k + 2, :], fc1_r[:, 0, k:k + 2, :], fc1_r[:, 1, k:k + 2, :], raw_as(c, 2)
            if c < C_FC + 3:
                return lat_v, lat_r[:, 0], lat_r[:, 1], raw_as(c, 2)
            if c < C_DOWN:
                k = c - C_FC - 3
                return fc2_v[:, k, :], fc2_r[0][:, k, :], fc2_r[1][:, k, :], raw[:, c % 4, :]
            if c < C_WQ1:
                k = c - C_DOWN
                return down_v[:, k, :], down_r[:, 0, k, :], down_r[:, 1, k, :], raw[:, c % 4, :]
            if c < C_WOUT:
                k = c - C_WQ1
                return wq1_v[:, k, :], wq1_r[:, 0, k, :], wq1_r[:, 1, k, :], raw[:, c % 4, :]
            k = c - C_WOUT
            return wout_v[:, k, :], wout_r[:, 0, k, :], wout_r[:, 1, k, :], raw[:, c % 4, :]

        def first_chunk(a):
            k, kind = a % 4, a // 4
            if a < 2 * KT:
                k, kind = a // 2, a % 2
            if kind == 0:
                return Wk_v[:, k, :], Wk_r[:, 0, k, :], Wk_r[:, 1, k, :]
            if kind == 2:
                return Wv_v[:, k, :], Wv_r[:, 0, k, :], Wv_r[:, 1, k, :]
            t = 0 if kind == 1 else 512
            return ctx_v[:, k, t:t + 512], CT[:, 0, k, t:t + 512], CT[:, 1, k, t:t + 512]

        def f32(ap):
            return ap.bitcast(F32)

        def product(pe, acc, w, m, first, last):
            pe.matmul(acc, w[0], m[0], start=first, stop=False)
            pe.matmul(acc, w[0], m[1], start=False, stop=False)
            return pe.matmul(acc, w[1], m[0], start=False, stop=last)

        def contract(pe, acc, pairs):
            for n, (w, m) in enumerate(pairs):
                mm = product(pe, acc, w, m, n == 0, n == len(pairs) - 1)
            return mm

        def hilo(buf, *at):
            return buf[(slice(None), 0) + at], buf[(slice(None), 1) + at]

        def steps_of(eng, step):
            for c in range(B):
                step(0, c)
            with eng.Fori(0, 3) as i:
                for c in range(B, B + 16):
                    step(i, c)
            for c in range(B, B + 10):
                step(3, c)

        def number(i, c):
            return 16 * i + c if isinstance(i, int) else None

        def step_chunk(c):
            k, at = c % B, (c // B + 1) % 2
            return hilo(Wq_r[:, at], k) if k < KT else hilo(Wo_r[:, at], k - KT)

        def lnbank(t):
            return bank[6 + t % 2] if t < 3 * B else bank[7]

        def expert_chunk(c):
            e, k = ORDER[(c - C_EX) // KT], (c - C_EX) % KT
            return ex_v[e, k], Ex[e][:, 0, k, :], Ex[e][:, 1, k, :]

        def expert_block_free(eng, c):
            e, k = ORDER[(c - C_EX) // KT], (c - C_EX) % KT
            if k == 0 and e == 1:
                eng.wait_ge(s1_mm, UNITS1)
            if k == 0 and e == 0:
                eng.wait_ge(y1_mm, B)

        def act_rows(u):
            return work[:, u % 2, :] if u % IT < 2 else hrow[:, u % 2, :]

        def up_bank(u):
            return bank[(2, 3, 2, 3, 0, 1, 2, 3)[u % IT]]

        A = slice(None)
        block = ctx.enter_context(nc.Block())

        @block.sync
        def _(sp):
            def load_first(a):
                if a >= 8:
                    sp.wait_ge(a_lo, a - 7)
                sp.dma_start(work[:, a % 8, :], first_chunk(a)[0]).then_inc(a_loaded[a % 8], 16)

            def load_raw(c, src, dst=None):
                if c >= 4:
                    sp.wait_ge(chunk_split, c - 3)
                sp.dma_start(raw[:, c % 4, :] if dst is None else dst, src).then_inc(raw_loaded[c % 4], 16)

            def load_late(c):
                src, _, _, dst = mlp_chunk(c)
                load_raw(c, src, dst)

            def load_x(b):
                sp.dma_start(X[:, b, :], x[b]).then_inc(x_loaded[b], 16)

            for a in range(8):
                load_first(a)
            load_x(0)
            load_x(1)
            for g, src in enumerate((g_xattn, g_ffn)):
                sp.dma_start(graw[:, 2 * g:2 * g + 2], src.rearrange("(a n) -> a n", a=1).broadcast_to([P, 2])
                             ).then_inc(small_loaded, 16)
            sp.dma_start(graww, gate0.rearrange("(k p) n -> p k n", p=P)).then_inc(small_loaded, 16)
            sp.dma_start(gw1[:, :, :], gate1T.rearrange("(k p) n -> p k n", p=P)).then_inc(small_loaded, 16)
            sp.dma_start(gb1[:, :], gate1_b.rearrange("(a n) -> a n", a=1).broadcast_to([P, NE])
                         ).then_inc(small_loaded, 16)
            sp.dma_start(mask8[:, :], mask).then_inc(small_loaded, 16)
            for a in range(8, 12):
                load_first(a)
            for b in range(2, B):
                load_x(b)
            for a in range(12, NA):
                load_first(a)
            load_raw(0, wkT.rearrange("(k p) n -> p k n", p=P), raw_as(0, KT))
            load_raw(1, wvT.rearrange("(k p) n -> p k n", p=P), raw_as(1, KT))
            for k in range(2):
                load_raw(C_WQ0 + k, Wq_v[k, :, 0:512])
            for n, job in enumerate(JOBS):
                if job[0] not in ("K", "V"):
                    continue
                s = STORE[n]
                sp.wait_ge(kv_lo, LOS[n])
                for part in range(2):
                    if job[0] == "K":
                        _, cl, h, half = job
                        dst = Kscr[h, half * HALF:(half + 1) * HALF, :, part, cl * P:(cl + 1) * P].rearrange("b p t -> p b t")
                        src = stage[:, s % 4, part, :].rearrange("p (b t) -> p b t", b=HALF)
                    else:
                        _, cl, b = job
                        dst = Vscr[:, b, :, part, cl, :].rearrange("h p n -> p h n")
                        src = stage[:, s % 4, part, :].rearrange("p (h n) -> p h n", h=KVH)
                    sp.dma_start(dst, f32(src)).then_inc(kv_stored[s % 4], 16)
                if s in (5, 6):
                    load_raw(C_WQ0 + s - 3, Wq_v[s - 3, :, 0:512])
            sp.dma_start(gam, ln_gamma.rearrange("(a n) -> a n", a=1).broadcast_to([P, D])).then_inc(gb_loaded, 16)
            sp.dma_start(bet, ln_beta.rearrange("(a n) -> a n", a=1).broadcast_to([P, D])).then_inc(gb_loaded, 16)
            for k in range(QUAD):
                load_raw(C_WO0 + k, Wo_v[k])

            def load_K(i, c):
                src = Kscr[bass.ds(i + c // 16, 1), c % B].rearrange("a p s t -> (a p) s t")
                sp.dma_start(f32(Kb[:, c % 2]), src).then_inc(k_loaded[c % 2], 16)

            def load_V(i, c):
                src = Vscr[bass.ds(i + c // 16, 1), c % B].rearrange("a p s k n -> (a p) s k n")
                sp.dma_start(f32(Vb[:, c % 2]), src).then_inc(v_loaded[c % 2], 16)

            def load_step_chunk(i, c):
                j1, k = c // B + 1, c % B
                if k < KT:
                    src = Wq_v[k, :, bass.ds(1024 * i + 512 * j1, 512)]
                else:
                    src = Wo_v[bass.ds(8 * i + QUAD * j1 + k - KT, 1)].rearrange("a p n -> (a p) n")
                sp.wait_ge(chunk_split, C_STEP + 16 * i + c - 3)
                sp.dma_start(raw[:, (C_STEP + c) % 4, :], src).then_inc(raw_loaded[(C_STEP + c) % 4], 16)

            for s in range(4):
                sp.wait_ge(kv_stored[s], 16 * 2 * 8)
            load_K(0, 0)

            def step(i, c):
                n = number(i, c)
                if n is None or n < STEPS:
                    if n is None or n >= 2:
                        sp.wait_ge(o_mm, 16 * i + c - 1)
                    load_V(i, c)
                if n is None or n + 1 < STEPS:
                    if n is None or n >= 1:
                        sp.wait_ge(s_mm, 2 * (16 * i + c))
                    load_K(i, c + 1)
                if n is None or n < STEPS - B:
                    load_step_chunk(i, c)
                elif n < STEPS:
                    load_late(C_UP + n - (STEPS - B))

            steps_of(sp, step)
            for c in range(C_UP + 8, C_EX):
                load_late(c)

            def load_expert(c):
                if c - 4 >= C_POOL:
                    sp.wait_ge(ex_lo, c - 3 - C_POOL)
                    sp.dma_start(raw[:, c % 4, :], expert_chunk(c)[0]).then_inc(raw_loaded[c % 4], 16)
                else:
                    load_raw(c, expert_chunk(c)[0])

            for u in range(B * M1):
                b, m = u // M1, u % M1
                if u < M1:
                    sp.wait_ge(kb_zero, u + 1)
                else:
                    sp.wait_ge(s1_mm, 2 * (u - M1) + 2)
                for h in range(HT1):
                    g = (m * HT1 + h) // (H1 // G1)
                    sp.dma_start(f32(KB[D1 * h:D1 * (h + 1), m, :, h, :]), f32(KT1[D1 * g:D1 * (g + 1), :, b * P:(b + 1) * P])
                                 ).then_inc(kb_loaded[m], 16)
                if u in (6, 13, 18, 23, 28):
                    for k in range(KT):
                        load_expert(C_EX + KT * (6, 13, 18, 23, 28).index(u) + k)
            for c in range(C_EX + 5 * KT, C_ALL):
                load_expert(c)
                if c == C_EX + 6 * KT:
                    sp.wait_ge(o1_mm, UNITS1)
                    sp.dma_start(ebias, expert_b).then_inc(eb_loaded, 16)

            def load_tile(j):
                sp.dma_start(xs_raw[:, j % 4, :], Xscr[j * P:(j + 1) * P]).then_inc(xs_loaded[j % 4], 16)

            sp.wait_ge(scattered, 16 * B)
            for j in range(4):
                load_tile(j)
            for j in range(TILES):
                if j + 4 < TILES:
                    sp.wait_ge(xs_T, j + 1)
                    load_tile(j + 4)
                sp.wait_ge(y_copied, j + 1)
                sp.dma_start(Yscr[j * P:(j + 1) * P], ys[:, j % 4, :]).then_inc(y_stored[j % 4], 16)
            for b in range(B):
                sp.wait_ge(e_acc, b + 1)
                sp.dma_start(out[b], X[:, b, :]).then_inc(out_stored, 16)
            sp.wait_ge(out_stored, 16 * B)

        @block.gpsimd
        def _(pool):
            made = [0]

            def link(ins):
                made[0] += 1
                ins.then_inc(consts_made, 1)
                pool.wait_ge(consts_made, made[0])

            link(pool.memset(ident[:, :], 0.0))
            link(pool.affine_select(out=ident[:, :], in_=ident[:, :], compare_op=ALU.not_equal, fill=1.0, base=0,
                                    pattern=[[-1, P]], channel_multiplier=1))
            link(pool.iota(iota8[:, :], pattern=[[1, NE]], base=0, channel_multiplier=0,
                           allow_small_or_imprecise_dtypes=True))
            link(pool.memset(mhalf[:, :], -0.5))
            link(pool.memset(V1[:, :, :, :], 1.0))

            def ln_power(t):
                b = t % B
                pool.wait_ge(ln_stat, t + 1)
                pool.tensor_tensor(rstd[:, b:b + 1], vareps[:, b:b + 1], mhalf[:, :], ALU.pow).then_inc(ln_rstd, 1)

            own = [0]

            def split(src, hi, lo):
                pool.tensor_copy(hi, src).then_inc(chunk_hi, 1)
                own[0] += 1
                pool.wait_ge(chunk_hi, own[0])
                pool.tensor_tensor(lo, src, f32(hi), ALU.subtract).then_inc(chunk_split, 1)

            def split_static(c, src, hi, lo):
                pool.wait_ge(raw_loaded[c % 4], 16 * (c // 4 + 1))
                split(src, hi, lo)

            def late_low(c):
                _, hi, lo, src = mlp_chunk(c)
                pool.wait_ge(late_hi, c - C_UP + 1)
                pool.tensor_tensor(lo, src, f32(hi), ALU.subtract).then_inc(chunk_split, 1)

            for t in range(4):
                ln_power(t)
            split_static(0, raw_as(0, KT), wk1_r[:, 0], wk1_r[:, 1])
            split_static(1, raw_as(1, KT), wv1_r[:, 0], wv1_r[:, 1])
            for t in range(4, B):
                ln_power(t)
            for k in range(KT):
                c = C_WQ0 + k
                split_static(c, raw[:, c % 4, :], Wq_r[:, 0, 0, k, :], Wq_r[:, 0, 1, k, :])
            pool.wait_ge(kv_mm, len(JOBS))
            for h in range(QUAD):
                c = C_WO0 + h
                split_static(c, raw[:, c % 4, :], Wo_r[:, 0, 0, h, :], Wo_r[:, 0, 1, h, :])

            def step(i, c):
                n = number(i, c)
                if n is not None and n >= STEPS - 5 and n - (STEPS - 5) < B:
                    ln_power(B + n - (STEPS - 5))
                if n is None or n < STEPS:
                    pr = prob[:, c % 2, :].rearrange("p (h t) -> p h t", h=QUAD)
                    pool.wait_ge(s_rcp, 16 * i + c + 1)
                    pool.tensor_tensor(pr, pr, rinv[:, c % 2, :].unsqueeze(2).broadcast_to([P, QUAD, KEYS]), ALU.mult
                                       ).then_inc(p_norm, 1)
                if n is None or n < STEPS - B:
                    hi, lo = step_chunk(c)
                    pool.wait_ge(step_hi, 16 * i + c + 1)
                    pool.tensor_tensor(lo, raw[:, (C_STEP + c) % 4, :], f32(hi), ALU.subtract).then_inc(chunk_split, 1)
                if n is not None and STEPS - 4 <= n < STEPS:
                    for k in range(2):
                        late_low(C_UP + 2 * (n - (STEPS - 4)) + k)

            steps_of(pool, step)
            ln_power(2 * B - 1)

            for c in range(C_FC, C_DOWN):
                late_low(c)

            def z_power(b):
                pool.wait_ge(z_stat, b + 1)
                pool.tensor_tensor(zrs[:, b:b + 1], zve[:, b:b + 1], mhalf[:, :], ALU.pow).then_inc(z_rstd, 1)

            for u in range(IT):
                late_low(C_DOWN + u)
            pool.wait_ge(gb_made, 2)
            pool.wait_ge(ln_row, 2 * B)
            for b in range(B):
                pool.tensor_tensor(X[:, b, :], X[:, b, :], bet, ALU.add).then_inc(xbeta, 1)
            for b in range(HALF):
                z_power(b)
                ln_power(2 * B + b)
            for k in range(KT):
                late_low(C_WQ1 + k)
            for b in range(HALF, B):
                z_power(b)
                ln_power(2 * B + b)
            pool.wait_ge(m_down, B)
            for m in range(M1):
                pool.memset(f32(region(RB + 2048 * m, 2048)), 0.0).then_inc(kb_zero, 1)
            pool.memset(zeros, 0.0).then_inc(tables_made, 1)
            pool.wait_ge(tables_made, 1)
            for j in range(TILES):
                pool.dma_start(Xscr[j * P:(j + 1) * P], zeros).then_inc(xscr_zero, 16)
                if j == TILES // 2:
                    for k in range(KT):
                        late_low(C_WOUT + k)

            pool.wait_ge(q1_mm, 2 * M1)

            def split_expert(c):
                split_static(c, raw[:, c % 4, :], *expert_chunk(c)[1:])

            for c in range(C_EX, C_EX + 2):
                split_expert(c)
            steps_made = [1]

            def table_link(ins):
                steps_made[0] += 1
                ins.then_inc(tables_made, 1)
                pool.wait_ge(tables_made, steps_made[0])

            for b in range(B - 1):
                ln_power(3 * B + b)
                if b == 4:
                    pool.wait_ge(s1_mm, UNITS1 // 2)
                for c in {0: (2, 3), 1: range(4, 8), 2: range(8, 12), 4: range(12, 16)}.get(b, ()):
                    split_expert(C_EX + c)
            for m in range(M1):
                pool.wait_ge(kb_loaded[m], 16 * HT1 * B)
            table_link(pool.memset(table[:, :], 1.0))
            table_link(pool.affine_select(out=before, in_=ones, compare_op=ALU.is_gt, fill=0.0, base=0,
                                          pattern=[[1, P]], channel_multiplier=-1))
            table_link(pool.affine_select(out=earlier, in_=earlier, compare_op=ALU.is_gt, fill=0.0, base=0,
                                          pattern=[[1, NE], [-1, NE]], channel_multiplier=0))
            table_link(pool.iota(starts, pattern=[[P, NE]], base=0, channel_multiplier=0,
                                 allow_small_or_imprecise_dtypes=True))
            table_link(pool.iota(iota_tiles, pattern=[[1, TILES]], base=0, channel_multiplier=0,
                                 allow_small_or_imprecise_dtypes=True))
            for c in range(C_EX + 4 * KT, C_POOL):
                if c == C_EX + 6 * KT:
                    ln_power(4 * B - 1)
                _, hi, lo = expert_chunk(c)
                pool.wait_ge(ex_hi, c - C_EX - 4 * KT + 1)
                pool.tensor_tensor(lo, raw[:, c % 4, :], f32(hi), ALU.subtract).then_inc(chunk_split, 1)
            pool.wait_ge(slots_made, 1)
            pool.wait_ge(xscr_zero, 16 * TILES)
            for b in range(B):
                pool.wait_ge(xn_rows, b + 1)
                pool.indirect_dma_start(Xscr, bass.IndirectOffsetOnAxis(slot[:, b:b + 1], 0), work[:, b, :], None
                                        ).then_inc(scattered, 16)
            for k in range(4):
                pool.wait_ge(y_stored[k], 16 * len(range(k, TILES, 4)))
            pool.wait_ge(scattered, 16 * B)
            for b in range(B):
                pool.indirect_dma_start(work[:, b, :], None, Yscr, bass.IndirectOffsetOnAxis(slot[:, b:b + 1], 0)
                                        ).then_inc(yrow_loaded[b], 16)

        @block.scalar
        def _(act):
            def first_hi(a):
                act.wait_ge(a_loaded[a % 8], 16 * (a // 8 + 1))
                act.copy(first_chunk(a)[1], work[:, a % 8, :]).then_inc(a_hi, 1)

            def job_hi(n):
                kind = JOBS[n][0]
                act.wait_ge(kv_mm, n + 1)
                if kind in ("K", "V"):
                    s = STORE[n]
                    if s >= 4:
                        act.wait_ge(kv_stored[s % 4], 32 * (s // 4))
                    dst, src = stage[:, s % 4, 0, :], bank[n % 4]
                elif kind == "k1":
                    t = JOBS[n][1] * 512
                    dst, src = KT1[:, 0, t:t + 512], bank[n % 4]
                elif kind == "v1":
                    dst, src = work[:, 6 + JOBS[n][1], :], bank[n % 4]
                else:
                    half = JOBS[n][1]
                    dst = V1[:, half * HALF:(half + 1) * HALF, :, 0:D1]
                    src = bank[n % 4].rearrange("p (b g d) -> p b g d", b=HALF, g=G1)
                    act.wait_ge(consts_made, 5)
                act.copy(dst, src).then_inc(kv_hi, 1)

            def ln_high(t):
                b = t % B
                act.wait_ge(ln_T, t + 1)
                act.copy(HT[:, 0, :, b * P:(b + 1) * P], lnbank(t).rearrange("p (k t) -> p k t", k=KT)).then_inc(ln_hi, 1)

            for a in range(8):
                first_hi(a)
            act.wait_ge(small_loaded, 16 * 6)
            act.activation(gate[:, :], graw[:, :], ACT.Tanh).then_inc(gates_tanh, 1)
            act.copy(gw[:, 0], graww).then_inc(gatew_hi, 1)
            for a in range(8, 12):
                first_hi(a)
            job_hi(0)
            job_hi(1)
            first_hi(12)
            first_hi(13)
            job_hi(2)
            first_hi(14)
            first_hi(15)
            job_hi(3)
            job_hi(4)
            for b in range(B):
                ln_high(b)
                job_hi(5 + b)
            for n in range(5 + B, len(JOBS)):
                job_hi(n)

            def late_high(c):
                _, hi, _, src = mlp_chunk(c)
                act.wait_ge(raw_loaded[c % 4], 16 * (c // 4 + 1))
                act.copy(hi, src).then_inc(late_hi, 1)

            def q_high(index, h, half):
                act.wait_ge(q_mm, index + 1)
                act.activation(qT[:, half, 0, h, :], bank[6 + h % 2], ACT.Copy, scale=SCALE0).then_inc(q_hi, 1)

            for h in range(QUAD):
                q_high(h, h, 0)

            def step(i, c):
                n = number(i, c)
                if n is None or n >= 2:
                    act.wait_ge(o_mm, 16 * i + c - 1)
                    act.copy(OT[:, 0, :], bank[4]).then_inc(o_hi, 1)
                if n is None or n < STEPS:
                    for h in range(QUAD):
                        if h % 2 == 0:
                            act.wait_ge(s_max, 2 * (16 * i + c) + h // 2 + 1)
                        if h == 0 and (n is None or n >= 2):
                            act.wait_ge(p_T, 2 * (16 * i + c - 1))
                        e = act.activation(prob[:, c % 2, h * KEYS:(h + 1) * KEYS],
                                           bank[h // 2][:, (h % 2) * KEYS:(h % 2 + 1) * KEYS], ACT.Exp,
                                           bias=nmax[:, c % 2, h:h + 1], accum_out=psumr[:, c % 2, h:h + 1])
                        if h % 2:
                            e.then_inc(s_exp, 1)
                if n is None or n < STEPS - QUAD:
                    act.wait_ge(q_mm, 16 * i + c + QUAD + 1)
                    act.activation(qT[:, (c // QUAD + 1) % 2, 0, c % QUAD, :], bank[6 + c % 2], ACT.Copy,
                                   scale=SCALE0).then_inc(q_hi, 1)
                if (n is None or n >= 1) and (n is None or n <= STEPS):
                    for k in range(2):
                        act.wait_ge(p_T, 2 * (16 * i + c - 1) + k + 1)
                        act.copy(PT[:, 0, k, :], bank[2 + k]).then_inc(pt_hi, 1)
                if n is not None and n >= STEPS - 4:
                    ln_high(B + n - (STEPS - 4))
                if n is None or n < STEPS - B:
                    if n is None:
                        act.wait_ge(q_mm if c % B < KT else y_mm, 16 * i + B * (c // B))
                    elif c == 0:
                        act.wait_ge(kv_mm, len(JOBS))
                    slot = (C_STEP + c) % 4
                    act.wait_ge(raw_loaded[slot], 64 * i + 16 * ((C_STEP + c) // 4 + 1))
                    act.copy(step_chunk(c)[0], raw[:, slot, :]).then_inc(step_hi, 1)
                if n is not None and STEPS - 4 <= n < STEPS:
                    act.wait_ge(q_mm, STEPS)
                    for k in range(2):
                        late_high(C_UP + 2 * (n - (STEPS - 4)) + k)

            steps_of(act, step)
            ln_high(2 * B - 2)

            act.wait_ge(o_mm, STEPS)
            late_high(C_FC)
            late_high(C_FC + 1)
            act.wait_ge(y_mm, STEPS)
            late_high(C_FC + 2)
            late_high(C_FC + 3)
            for half in range(2):
                if half:
                    act.wait_ge(ln_stat, 2 * B + 3)
                act.wait_ge(m_gateT, half + 1)
                act.copy(logitT, bank[3][0:NE, :]).then_inc(m_gate_row, 1)
                if not half:
                    ln_high(2 * B - 1)
                    late_high(C_FC + 4)
                for k in range(LT):
                    act.wait_ge(m_xl, 4 * half + k + 1)
                    act.copy(xlT[:, 0, k, :], bank[k]).then_inc(m_xl_hi, 1)
                if half:
                    ln_high(2 * B)
                    ln_high(2 * B + 1)

                def act_high(u):
                    act.wait_ge(m_sq, u + 1)
                    act.copy(actT[:, 0, u % IT, :], act_rows(u)).then_inc(m_sq_hi, 1)

                def act_relu(u):
                    if not half:
                        late_high(C_DOWN + u)
                    act.wait_ge(m_up, u + 1)
                    if 2 <= u % IT < 4:
                        act.wait_ge(ln_T, 2 * B + 4 * half)
                    if u % IT >= 4:
                        act.wait_ge(m_sq_lo, u - 1)
                    act.activation(act_rows(u), up_bank(u), ACT.Relu).then_inc(m_relu, 1)

                u0 = IT * half
                act_relu(u0)
                act_relu(u0 + 1)
                act_high(u0)
                act_high(u0 + 1)
                for k in range(LT):
                    act.wait_ge(m_xl, 4 * half + LT + k + 1)
                    act.copy(eoT[:, 0, k, :], bank[k]).then_inc(m_xl_hi, 1)
                if half:
                    ln_high(2 * B + 2)
                    ln_high(2 * B + 3)
                for u in range(u0 + 2, u0 + IT):
                    act_relu(u)
                    if u > u0 + 2:
                        act_high(u - 1)
                act_high(u0 + IT - 1)
            act.wait_ge(m_up, 2 * IT)
            for k in range(KT):
                late_high(C_WQ1 + k)

            def q1_high(n):
                half, m = n // M1, n % M1
                act.wait_ge(q1_mm, n + 1)
                act.activation(qT1[:, half, 0, m, :], bank[n % 4], ACT.Copy, scale=SCALE1
                               ).then_inc(q1_hi, 1)

            for b in (4, 5):
                ln_high(2 * B + b)
            for n in range(2 * M1):
                q1_high(n)
                if n in (1, 2):
                    ln_high(2 * B + 5 + n)
            for k in range(KT):
                late_high(C_WOUT + k)
            expert_highs = [C_EX + 4 * KT]

            def expert_high(n):
                for c in range(expert_highs[0], expert_highs[0] + n):
                    expert_block_free(act, c)
                    act.wait_ge(raw_loaded[c % 4], 16 * (c // 4 + 1))
                    act.copy(expert_chunk(c)[1], raw[:, c % 4, :]).then_inc(ex_hi, 1)
                expert_highs[0] += n

            for w in range(UNITS1 + 10):
                if w >= 12 and (w - 12) % G1 == 0 and (w - 12) // G1 < B:
                    b = (w - 12) // G1
                    act.wait_ge(o1_T, b + 1)
                    act.copy(OT1[:, b % 2, 0], bank[7].rearrange("p (k t) -> p k t", k=KT)).then_inc(o1_hi, 1)
                if w >= 17 and (w - 17) % G1 == 0:
                    b = (w - 17) // G1
                    act.wait_ge(ln_T, 3 * B + b + 1)
                    act.copy(hrow[:, b % 2, :], bank[7]).then_inc(g1_xt, 1)
                if 2 <= w < UNITS1 + 2:
                    v = w - 2
                    act.wait_ge(p1_T, v + 1)
                    if v >= 4:
                        act.wait_ge(o1_mm, v - 3)
                    act.copy(probT1[:, v % 4, :], bank[3 + v % 2]).then_inc(p1_copy, 1)
                if w < UNITS1:
                    act.wait_ge(s1_sub, w + 1)
                    act.activation(prob1[:, w % 4, :], prob1[:, w % 4, :], ACT.Exp).then_inc(s1_exp, 1)
                if w == UNITS1 + 8:
                    act.wait_ge(eb_loaded, 16)
                    act.wait_ge(xscr_zero, 16 * TILES)
                    act.copy(ebias_r[:, 0], ebias).then_inc(eb_hi, 1)
                if w >= UNITS1:
                    expert_high((1, 1, 2, 1, 1, 1, 1, 1, 1, 2)[w - UNITS1])
            act.wait_ge(g1_T, 1)
            act.copy(onehT, PS[0:NE, 6:8, :].rearrange("p a n -> p (a n)")).then_inc(g1_copy, 1)
            expert_high(C_ALL - expert_highs[0])

            def tile_high(j):
                act.wait_ge(xs_T, j + 1)
                if j >= 2:
                    act.wait_ge(e_mm, j - 1)
                act.copy(XST[:, j % 2, 0], bank[4 + j % 2].rearrange("p (k t) -> p k t", k=KT)).then_inc(xs_hi, 1)

            act.wait_ge(b1_mm, B)
            tile_high(0)
            for j in range(TILES):
                if j + 1 < TILES:
                    tile_high(j + 1)
                act.wait_ge(e_mm, j + 1)
                if j >= 4:
                    act.wait_ge(y_stored[j % 4], 16 * (j // 4))
                act.copy(ys[:, j % 4, :], bank[j % 4]).then_inc(y_copied, 1)

        @block.vector
        def _(dve):
            links = [0]

            def link(ins):
                links[0] += 1
                ins.then_inc(chain, 1)
                dve.wait_ge(chain, links[0])

            def first_lo(a):
                _, hi, lo = first_chunk(a)
                dve.wait_ge(a_hi, a + 1)
                dve.tensor_tensor(lo, work[:, a % 8, :], f32(hi), ALU.subtract).then_inc(a_lo, 1)

            def ln_stats(t):
                b = t % B
                if t < B:
                    dve.wait_ge(x_loaded[b], 16)
                link(dve.bn_stats(stats[:, t % 2, :], X[:, b, :]))
                link(dve.bn_aggr(meanvar[:, b, :], stats[:, t % 2, :]))
                dve.tensor_scalar(vareps[:, b:b + 1], meanvar[:, b, 1:2], LN_EPS, None, ALU.add).then_inc(ln_stat, 1)

            def ln_rows(t):
                b = t % B
                dve.wait_ge(ln_rstd, t + 1)
                if t % B >= 2:
                    dve.wait_ge(ln_T, t - 1)
                dve.tensor_scalar(hrow[:, t % 2, :], X[:, b, :], meanvar[:, b, 0:1], rstd[:, b:b + 1],
                                  ALU.subtract, ALU.mult).then_inc(ln_row, 1)

            def ln_low(t):
                b = t % B
                hi, lo = hilo(HT, A, slice(b * P, (b + 1) * P))
                dve.wait_ge(ln_hi, t + 1)
                dve.tensor_tensor(lo, lnbank(t).rearrange("p (k t) -> p k t", k=KT), f32(hi), ALU.subtract).then_inc(ln_lo, 1)

            def job_lo(n):
                if not HAS_LO[n]:
                    return
                dve.wait_ge(kv_hi, n + 1)
                if JOBS[n][0] == "k1":
                    t = JOBS[n][1] * 512
                    hi, lo = hilo(KT1, slice(t, t + 512))
                else:
                    hi, lo = stage[:, STORE[n] % 4, 0, :], stage[:, STORE[n] % 4, 1, :]
                dve.tensor_tensor(lo, bank[n % 4], f32(hi), ALU.subtract).then_inc(kv_lo, 1)

            dve.wait_ge(consts_made, 2)
            dve.tensor_copy(identr, ident[:, :]).then_inc(identr_made, 1)
            for a in range(8):
                first_lo(a)
            dve.wait_ge(gatew_hi, 1)
            dve.tensor_tensor(gw[:, 1], graww, f32(gw[:, 0]), ALU.subtract).then_inc(gatew_lo, 1)
            ln_stats(0)
            ln_stats(1)
            for a in range(8, 12):
                first_lo(a)
            ln_rows(0)
            ln_rows(1)
            ln_stats(2)
            ln_stats(3)
            job_lo(0)
            job_lo(1)
            first_lo(12)
            first_lo(13)
            job_lo(2)
            first_lo(14)
            first_lo(15)
            job_lo(3)
            for t in range(4, B):
                ln_stats(t)
            job_lo(4)
            for b in range(B):
                ln_low(b)
                if b + 2 < B:
                    ln_rows(b + 2)
                job_lo(5 + b)
            for n in range(5 + B, len(JOBS)):
                job_lo(n)

            def q_low(index, h, half):
                dve.wait_ge(q_hi, index + 1)
                dve.scalar_tensor_tensor(out=qT[:, half, 1, h, :], in0=bank[6 + h % 2], scalar=SCALE0,
                                         in1=f32(qT[:, half, 0, h, :]), op0=ALU.mult, op1=ALU.subtract).then_inc(q_lo, 1)

            for h in range(QUAD):
                q_low(h, h, 0)
            dve.wait_ge(gates_tanh, 1)
            dve.wait_ge(gb_loaded, 32)
            for v in (gam, bet):
                dve.tensor_scalar(v, v, gate[:, 2:3], None, ALU.mult).then_inc(gb_made, 1)

            def maxima(i, c, k):
                dve.wait_ge(s_mm, 2 * (16 * i + c) + k + 1)
                dve.tensor_reduce(nmax[:, c % 2, 2 * k:2 * k + 2], bank[k].rearrange("p (h t) -> p h t", h=2),
                                  AX_X, ALU.max, negate=True).then_inc(s_max, 1)

            def step(i, c):
                n = number(i, c)
                if n is None or n < STEPS:
                    maxima(i, c, 0)
                if n is None or n >= 2:
                    dve.wait_ge(o_hi, 16 * i + c - 1)
                    dve.tensor_tensor(OT[:, 1, :], bank[4], f32(OT[:, 0, :]), ALU.subtract).then_inc(o_lo, 1)
                if n is None or n < STEPS:
                    maxima(i, c, 1)
                if n is not None and n >= STEPS - 5:
                    ln_rows(B + n - (STEPS - 5))
                if n is None or n < STEPS:
                    dve.wait_ge(s_exp, 2 * (16 * i + c) + 2)
                    dve.reciprocal(rinv[:, c % 2, :], psumr[:, c % 2, :]).then_inc(s_rcp, 1)
                if n is None or n < STEPS - QUAD:
                    h, at = c % QUAD, (c // QUAD + 1) % 2
                    dve.wait_ge(q_hi, 16 * i + c + QUAD + 1)
                    dve.scalar_tensor_tensor(out=qT[:, at, 1, h, :], in0=bank[6 + c % 2], scalar=SCALE0,
                                             in1=f32(qT[:, at, 0, h, :]), op0=ALU.mult, op1=ALU.subtract).then_inc(q_lo, 1)
                if (n is None or n >= 1) and (n is None or n <= STEPS):
                    for k in range(2):
                        dve.wait_ge(pt_hi, 2 * (16 * i + c - 1) + k + 1)
                        dve.tensor_tensor(PT[:, 1, k, :], bank[2 + k], f32(PT[:, 0, k, :]), ALU.subtract).then_inc(pt_lo, 1)
                if n is not None and n >= STEPS - 4:
                    ln_low(B + n - (STEPS - 4))
                if n is None or n >= 2:
                    dve.wait_ge(y_mm, 16 * i + c - 1)
                    b = (c - 2) % B
                    dve.scalar_tensor_tensor(out=X[:, b, :], in0=bank[5], scalar=gate[:, 0:1], in1=X[:, b, :],
                                             op0=ALU.mult, op1=ALU.add).then_inc(y_acc, 1)
                if n is not None and n >= STEPS - 6:
                    dve.wait_ge(y_acc, n - 1)
                    ln_stats(B + n - (STEPS - 6))

            steps_of(dve, step)
            ln_rows(2 * B - 1)
            ln_low(2 * B - 2)
            ln_low(2 * B - 1)

            def act_low(u):
                dve.wait_ge(m_sq_hi, u + 1)
                dve.tensor_tensor(actT[:, 1, u % IT, :], act_rows(u), f32(actT[:, 0, u % IT, :]), ALU.subtract
                                  ).then_inc(m_sq_lo, 1)

            def z_part(b):
                dve.wait_ge(m_down, b + 1)
                link(dve.tensor_tensor(zrow[:, b % 2, :], bank[4 + b % 2], work[:, b % HALF, :], ALU.add))
                link(dve.bn_stats(stats[:, b % 2, :], zrow[:, b % 2, :]))
                link(dve.bn_aggr(zmv[:, b, :], stats[:, b % 2, :]))
                dve.tensor_scalar(zve[:, b:b + 1], zmv[:, b, 1:2], LN_EPS, None, ALU.add).then_inc(z_stat, 1)

            def z_add(b):
                z = zrow[:, b % 2, :]
                link(dve.scalar_tensor_tensor(out=z, in0=z, scalar=zmv[:, b, 0:1], in1=gam, op0=ALU.subtract, op1=ALU.mult))
                dve.wait_ge(z_rstd, b + 1)
                dve.wait_ge(xbeta, b + 1)
                link(dve.scalar_tensor_tensor(out=X[:, b, :], in0=z, scalar=zrs[:, b:b + 1], in1=X[:, b, :],
                                              op0=ALU.mult, op1=ALU.add))
                ln_stats(2 * B + b)

            for half in range(2):
                for k in range(LT):
                    dve.wait_ge(m_xl_hi, 4 * half + k + 1)
                    dve.tensor_tensor(xlT[:, 1, k, :], bank[k], f32(xlT[:, 0, k, :]), ALU.subtract).then_inc(m_xl_lo, 1)
                dve.wait_ge(m_gate, half + 1)
                for b in range(HALF):
                    t8 = dve.max(top0[:, b, :], bank[3][:, b * NE:(b + 1) * NE])
                link(t8)
                dve.tensor_tensor(route[:, half * HALF:(half + 1) * HALF].unsqueeze(2), top0[:, :, 0:1], top0[:, :, 1:2],
                                  ALU.add).then_inc(m_route, 1)
                if half:
                    z_add(3)
                    ln_low(2 * B)
                    ln_rows(2 * B + 2)
                    ln_low(2 * B + 1)

                def act_square(u):
                    dve.wait_ge(m_relu, u + 1)
                    dve.tensor_tensor(act_rows(u), act_rows(u), act_rows(u), ALU.mult).then_inc(m_sq, 1)

                u0 = IT * half
                act_square(u0)
                act_square(u0 + 1)
                for k in range(LT):
                    dve.wait_ge(m_xl_hi, 4 * half + LT + k + 1)
                    dve.tensor_tensor(eoT[:, 1, k, :], bank[k], f32(eoT[:, 0, k, :]), ALU.subtract).then_inc(m_xl_lo, 1)
                act_low(u0)
                act_low(u0 + 1)
                if half:
                    ln_rows(2 * B + 3)
                    ln_low(2 * B + 2)
                dve.wait_ge(m_route, half + 1)
                dve.wait_ge(m_sq_lo, u0 + 2)
                for b in range(HALF):
                    r = half * HALF + b
                    dve.wait_ge(m_fc2, r + 1)
                    dve.tensor_scalar(work[:, b, :], bank[4 + b % 2], route[:, r:r + 1], None, ALU.mult).then_inc(m_fc2_out, 1)
                if half:
                    ln_low(2 * B + 3)
                for u in range(u0 + 2, u0 + IT):
                    act_square(u)
                    if u > u0 + 2:
                        act_low(u - 1)
                act_low(u0 + IT - 1)
                if half:
                    for h in range(4):
                        dve.tensor_scalar(maskr[:, h * P:(h + 1) * P], mask8[:, :], 1.0, -MASKED, ALU.subtract, ALU.mult
                                          ).then_inc(mask_made, 1)
                    z_part(4)
                    z_add(4)
                    z_part(5)
                    z_add(5)
                    ln_rows(2 * B + 4)
                    z_part(6)
                    z_add(6)
                    ln_rows(2 * B + 5)
                    ln_low(2 * B + 4)
                    z_part(7)
                    z_add(7)
                    ln_low(2 * B + 5)
                    ln_rows(2 * B + 6)
                    ln_rows(2 * B + 7)
                else:
                    for b in range(HALF):
                        z_part(b)
                        if b < 3:
                            z_add(b)
                        if 1 <= b <= 2:
                            ln_rows(2 * B + b - 1)

            def q1_low(n):
                half, m = n // M1, n % M1
                hi, lo = hilo(qT1[:, half], m)
                dve.wait_ge(q1_hi, n + 1)
                dve.scalar_tensor_tensor(out=lo, in0=bank[n % 4], scalar=SCALE1, in1=f32(hi),
                                         op0=ALU.mult, op1=ALU.subtract).then_inc(q1_lo, 1)

            for n in range(2 * M1):
                q1_low(n)
                if n in (1, 2):
                    ln_low(2 * B + 5 + n)
            def choose(b, part):
                if part == 0:
                    dve.wait_ge(g1_mm, b + 1)
                else:
                    dve.wait_ge(g1_part, CHOICE * b + part)
                if part == 0:
                    done = dve.tensor_tensor(logit1[:, :], bank[7][:, 0:NE], gb1[:, :], ALU.add)
                elif part == 1:
                    done = dve.max(top1[:, :], logit1[:, :])
                elif part == 2:
                    done = dve.max_index(idx1[:, :], top1[:, :], logit1[:, :])
                elif part == 3:
                    done = dve.tensor_copy(idxf[:, :], idx1[:, 0:1])
                elif part == 4:
                    done = dve.tensor_scalar(oneh[:, b, :], iota8[:, :], idxf[:, :], None, ALU.is_equal)
                else:
                    done = dve.tensor_tensor(chosen[:, b + 1, :], chosen[:, b, :], oneh[:, b, :], ALU.add)
                done.then_inc(g1_part, 1)

            def slot_rows(b):
                if b == 0:
                    dve.wait_ge(p1_T, UNITS1)
                    dve.wait_ge(o1_mm, UNITS1)
                dve.tensor_scalar(work[:, b, :], X[:, b, :], meanvar[:, b, 0:1], rstd[:, b:b + 1],
                                  ALU.subtract, ALU.mult).then_inc(xn_rows, 1)

            link(dve.memset(chosen[:, 0, :], 0.0))
            for w in range(UNITS1 + 11):
                v = w - 4
                if 0 <= v < UNITS1 and v % 4 == 3:
                    b, half = v // G1, v % G1 // 4
                    o = bank[5 + half][:, 0:16 * (D1 + 1)].rearrange("p (h d) -> p h d", h=16)
                    dve.wait_ge(o1_mm, v + 1)
                    link(dve.reciprocal(rsum1[:, half, :].unsqueeze(2), o[:, :, D1:D1 + 1]))
                    if half == 0 and b >= 2:
                        dve.wait_ge(g1_mm, b - 1)
                    dve.tensor_tensor(hrow[:, b % 2, half * 256:half * 256 + 256].rearrange("p (h d) -> p h d", h=16),
                                      o[:, :, 0:D1], rsum1[:, half, :].unsqueeze(2).broadcast_to([P, 16, D1]), ALU.mult
                                      ).then_inc(o1_row, 1)
                if w >= 14 and (w - 14) % G1 == 0 and (w - 14) // G1 < B:
                    b = (w - 14) // G1
                    dve.wait_ge(y1_mm, b + 1)
                    dve.scalar_tensor_tensor(out=X[:, b, :], in0=bank[7], scalar=gate[:, 1:2], in1=X[:, b, :],
                                             op0=ALU.mult, op1=ALU.add).then_inc(y1_acc, 1)
                if w < UNITS1:
                    sc = bank[w % 3].rearrange("p (h t) -> p h t", h=SHARE1)
                    dve.wait_ge(s1_mm, w + 1)
                    dve.tensor_reduce(max1[:, w % 2, :], sc, AX_X, ALU.max).then_inc(s1_max, 1)
                    dve.wait_ge(s1_max, w + 1)
                    if w >= 4:
                        dve.wait_ge(p1_T, w - 3)
                    dve.tensor_tensor(prob1[:, w % 4, :].rearrange("p (h t) -> p h t", h=SHARE1), sc,
                                      max1[:, w % 2, :].unsqueeze(2).broadcast_to([P, SHARE1, P]), ALU.subtract
                                      ).then_inc(s1_sub, 1)
                if w >= 12 and (w - 12) % G1 == 0 and (w - 12) // G1 < B:
                    b = (w - 12) // G1
                    dve.wait_ge(o1_hi, b + 1)
                    dve.tensor_tensor(OT1[:, b % 2, 1], bank[7].rearrange("p (k t) -> p k t", k=KT), f32(OT1[:, b % 2, 0]),
                                      ALU.subtract).then_inc(o1_lo, 1)
                if w >= 14 and (w - 14) % G1 == 0 and (w - 14) // G1 < B:
                    b = (w - 14) // G1
                    dve.wait_ge(y1_acc, b + 1)
                    ln_stats(3 * B + b)
                if w >= 15 and (w - 15) % G1 == 0 and (w - 15) // G1 < B:
                    b = (w - 15) // G1
                    dve.wait_ge(ln_rstd, 3 * B + b + 1)
                    dve.wait_ge(o1_T, b + 1)
                    dve.tensor_scalar(hrow[:, b % 2, :], X[:, b, :], meanvar[:, b, 0:1], rstd[:, b:b + 1],
                                      ALU.subtract, ALU.mult).then_inc(ln_row, 1)
                if w >= 18 and (w - 18) % G1 < CHOICE:
                    choose((w - 18) // G1, (w - 18) % G1)
                if w == UNITS1 + 9:
                    dve.wait_ge(eb_hi, 1)
                    dve.tensor_tensor(ebias_r[:, 1], ebias, f32(ebias_r[:, 0]), ALU.subtract).then_inc(eb_lo, 1)
                if w >= UNITS1 + 3 and w < UNITS1 + 10:
                    slot_rows(w - UNITS1 - 3)

            for part in range(1, CHOICE):
                choose(B - 1, part)
            dve.wait_ge(tables_made, 6)
            sq = routing[:, 0:NE * NE].rearrange("p (e f) -> p e f", e=NE)
            dve.wait_ge(g1_rank, 1)
            link(dve.tensor_tensor(sq, bank[2][:, B * NE:B * NE + NE].unsqueeze(2).broadcast_to([P, NE, NE]),
                                   starts.unsqueeze(1).broadcast_to([P, NE, NE]), ALU.is_gt))
            link(dve.tensor_reduce(tiles_of, sq, AX_X, ALU.add))
            link(dve.tensor_tensor(sq, tiles_of.unsqueeze(1).broadcast_to([P, NE, NE]), earlier, ALU.mult))
            link(dve.tensor_reduce(first_of, sq, AX_X, ALU.add))
            link(dve.scalar_tensor_tensor(out=sq, in0=first_of.unsqueeze(1).broadcast_to([P, B, NE]), scalar=float(P),
                                          in1=bank[2][:, 0:B * NE].rearrange("p (b e) -> p b e", b=B),
                                          op0=ALU.mult, op1=ALU.add))
            link(dve.tensor_tensor(sq, sq, oneh[:, :, :], ALU.mult))
            link(dve.tensor_reduce(slotf, sq, AX_X, ALU.add))
            dve.tensor_copy(slot[:, :], slotf).then_inc(slots_made, 1)
            slot_rows(B - 1)
            tl = routing[:, 0:TILES * NE].rearrange("p (j e) -> p j e", j=TILES)
            link(dve.tensor_tensor(tl, first_of.unsqueeze(1).broadcast_to([P, TILES, NE]),
                                   iota_tiles.unsqueeze(2).broadcast_to([P, TILES, NE]), ALU.is_le))
            link(dve.tensor_reduce(blockf, tl, AX_X, ALU.add))
            link(dve.tensor_scalar(blockf, blockf, -1.0, float(NE + 1), ALU.mult, ALU.add))
            dve.tensor_copy(tile_block[0:1, 0:TILES], blockf[0:1, :]).then_inc(blocks_made, 1)

            for b in range(B):
                if b < KT:
                    c = C_POOL + b
                    _, hi, lo = expert_chunk(c)
                    dve.wait_ge(ex_hi, c - C_EX - 4 * KT + 1)
                    dve.tensor_tensor(lo, raw[:, c % 4, :], f32(hi), ALU.subtract).then_inc(ex_lo, 1)
                dve.wait_ge(b1_mm, b + 1)
                dve.scalar_tensor_tensor(out=X[:, b, :], in0=bank[6 + b % 2], scalar=gate[:, 3:4], in1=X[:, b, :],
                                         op0=ALU.mult, op1=ALU.add).then_inc(b1_acc, 1)
            for j in range(TILES):
                dve.wait_ge(xs_hi, j + 1)
                dve.tensor_tensor(XST[:, j % 2, 1], bank[4 + j % 2].rearrange("p (k t) -> p k t", k=KT),
                                  f32(XST[:, j % 2, 0]), ALU.subtract).then_inc(xs_lo, 1)
            dve.wait_ge(b1_acc, B)
            for b in range(B):
                dve.wait_ge(yrow_loaded[b], 16)
                dve.scalar_tensor_tensor(out=X[:, b, :], in0=work[:, b, :], scalar=gate[:, 3:4], in1=X[:, b, :],
                                         op0=ALU.mult, op1=ALU.add).then_inc(e_acc, 1)

        @block.tensor
        def _(pe):
            def ln_transpose(t):
                if t < 3 * B and t % B >= 2:
                    pe.wait_ge(ln_lo, t - 1)
                pe.wait_ge(ln_row, t + 1)
                for k in range(KT):
                    mm = pe.transpose(lnbank(t)[:, k * P:(k + 1) * P], hrow[:, t % 2, k * P:(k + 1) * P], ident[:, :])
                mm.then_inc(ln_T, 1)

            def tokens(buf, k, t0, n):
                return hilo(buf, k, slice(t0, t0 + n))

            def job(n):
                kind = JOBS[n][0]
                if n >= 4:
                    if HAS_LO[n - 4]:
                        pe.wait_ge(kv_lo, LOS[n - 4])
                    else:
                        pe.wait_ge(kv_hi, n - 3)
                acc = bank[n % 4]
                if kind == "K":
                    _, part, h, half = JOBS[n]
                    src = HT if part else CT
                    for k in range(KT):
                        if n == 0:
                            pe.wait_ge(a_lo, 2 * k + 2)
                        mm = product(pe, acc, tokens(Wk_r, k, h * P, P), tokens(src, k, half * 512, 512), k == 0, k == KT - 1)
                elif kind == "V":
                    _, part, b = JOBS[n]
                    src = HT if part else CT
                    mm = contract(pe, acc, [(tokens(src, k, b * P, P), tokens(Wv_r, k, 0, 512)) for k in range(KT)])
                elif kind in ("k1", "v1"):
                    w, half = wk1_r if kind == "k1" else wv1_r, JOBS[n][1]
                    mm = contract(pe, acc, [(tokens(w, k, 0, P), tokens(CT, k, half * 512, 512)) for k in range(KT)])
                else:
                    half = JOBS[n][1]
                    for b in range(HALF):
                        mm = pe.transpose(acc[:, b * P:(b + 1) * P], work[:, 6 + half, b * P:(b + 1) * P], ident[:, :])
                mm.then_inc(kv_mm, 1)

            for n in range(NCTX):
                if n == 4:
                    pe.wait_ge(a_lo, 12)
                elif n == 8:
                    pe.wait_ge(a_lo, NA)
                job(n)
                if n == 4:
                    pe.wait_ge(consts_made, 2)
                if 4 <= n < 4 + B:
                    ln_transpose(n - 4)
            pe.wait_ge(chunk_split, 2)
            for n in range(NCTX, NCTX + 4):
                job(n)
            for half in range(2):
                pe.wait_ge(kv_hi, NCTX + 3 + half)
                job(NCTX + 4 + half)
            pe.wait_ge(ln_lo, B)
            for n in range(NCTX + 6, len(JOBS)):
                job(n)

            def queries(at, acc, slot, h, half):
                return contract(pe, acc, [(tokens(Wq_r[:, slot], k, h * P, P), tokens(HT, k, half * 512, 512))
                                          for k in range(KT)]).then_inc(q_mm, 1)

            pe.wait_ge(chunk_split, C_WO0)
            for h in range(QUAD):
                if h >= 2:
                    pe.wait_ge(q_lo, h - 1)
                queries(h, bank[6 + h % 2], 0, h, 0)

            def step(i, c):
                n = number(i, c)
                half, bb = c // QUAD % 2, c % QUAD
                if n is None or n < STEPS:
                    pe.wait_ge(q_lo, 16 * i + QUAD * (c // QUAD) + QUAD)
                    pe.wait_ge(k_loaded[c % 2], 128 * i + 16 * (c // 2 + 1))
                    for k in range(2):
                        if n is not None and n == 0:
                            pe.wait_ge(kv_lo, LOS[-1])
                        else:
                            pe.wait_ge(s_exp, 2 * (16 * i + c - 1) + k + 1)
                        for h in (2 * k, 2 * k + 1):
                            w = hilo(qT[:, half], h, slice(bb * P, (bb + 1) * P))
                            mm = product(pe, bank[k][:, (h % 2) * KEYS:(h % 2 + 1) * KEYS], w, hilo(Kb[:, c % 2]), True, True)
                        mm.then_inc(s_mm, 1)
                if n is None or n < STEPS - QUAD:
                    nxt = c // QUAD + 1
                    pe.wait_ge(q_lo, 16 * i + c + QUAD - 1)
                    if n is None or nxt >= 2:
                        pe.wait_ge(chunk_split, C_STEP + 16 * i + B * (nxt // 2 - 1) + KT)
                    queries(n, bank[6 + c % 2], nxt // 2 % 2, c % QUAD, nxt % 2)
                if (n is None or n >= 1) and (n is None or n <= STEPS):
                    pe.wait_ge(p_norm, 16 * i + c)
                    for k in range(2):
                        if n is None or n >= 2:
                            pe.wait_ge(pt_lo, 2 * (16 * i + c - 2) + k + 1)
                        for h in range(QUAD):
                            mm = pe.transpose(bank[2 + k][:, h * P:(h + 1) * P],
                                              prob[:, (c - 1) % 2, h * KEYS + k * P:h * KEYS + (k + 1) * P], ident[:, :])
                        mm.then_inc(p_T, 1)
                if n is None or n >= 2:
                    pe.wait_ge(o_lo, 16 * i + c - 1)
                    pe.wait_ge(chunk_split, C_STEP + 16 * i + B * ((c - 2) // B))
                    if n is None or n >= 3:
                        pe.wait_ge(y_acc, 16 * i + c - 2)
                    mm = contract(pe, bank[5], [(hilo(OT, slice(h * P, (h + 1) * P)), hilo(Wo_r[:, (c - 2) // B % 2], h))
                                                for h in range(QUAD)])
                    mm.then_inc(y_mm, 1)
                if (n is None or n >= 1) and (n is None or n <= STEPS):
                    pe.wait_ge(v_loaded[(c - 1) % 2], 128 * i + 16 * ((c - 1) // 2 + 1))
                    if n is None or n >= 2:
                        pe.wait_ge(o_lo, 16 * i + c - 1)
                    for k in range(2):
                        pe.wait_ge(pt_lo, 2 * (16 * i + c - 1) + k + 1)
                        mm = product(pe, bank[4], hilo(Vb[:, (c - 1) % 2], k), hilo(PT, k), k == 0, k == 1)
                    mm.then_inc(o_mm, 1)
                if n is not None and n >= STEPS - 5:
                    if n < STEPS - 3:
                        pe.wait_ge(q_lo, STEPS)
                    ln_transpose(B + n - (STEPS - 5))

            steps_of(pe, step)

            def gate_logits(half):
                pe.wait_ge(gatew_lo, 1)
                pe.wait_ge(identr_made, 1)
                contract(pe, bank[3], [(gate_wide(k), tokens(HT, k, half * 512, 512)) for k in range(KT)]).then_inc(m_gateT, 1)

            def gate_rows(half):
                pe.wait_ge(m_gate_row, half + 1)
                for b in range(HALF):
                    mm = pe.transpose(bank[3][:, b * NE:(b + 1) * NE], logitT[:, b * P:(b + 1) * P], ident[0:NE, 0:NE])
                mm.then_inc(m_gate, 1)

            def latent(half):
                pe.wait_ge(chunk_split, C_FC + 2)
                for m in range(LT):
                    mm = contract(pe, bank[m], [(tokens(fc1_r, k, m * P, P), tokens(HT, k, half * 512, 512)) for k in range(KT)])
                    mm.then_inc(m_xl, 1)

            def latent_expert(half):
                pe.wait_ge(chunk_split, C_FC + 3)
                pe.wait_ge(m_xl_lo, 4 * half + LT)
                for m in range(LT):
                    mm = contract(pe, bank[m], [(tokens(lat_r, k, m * P, P), hilo(xlT, k)) for k in range(LT)])
                    mm.then_inc(m_xl, 1)

            def latent_out(half):
                pe.wait_ge(chunk_split, C_FC + 5)
                pe.wait_ge(m_xl_lo, 4 * half + 2 * LT)
                for b in range(HALF):
                    r = half * HALF + b
                    if r >= 2:
                        pe.wait_ge(m_fc2_out, r - 1)
                    mm = contract(pe, bank[4 + b % 2], [(tokens(eoT, k, b * P, P), (fc2_r[0][:, k, :], fc2_r[1][:, k, :])) for k in range(LT)])
                    mm.then_inc(m_fc2, 1)

            def up(half, first, last):
                pe.wait_ge(chunk_split, C_UP + 8)
                for v in range(first, last):
                    u = IT * half + v
                    if v == 1:
                        pe.wait_ge(m_route, half + 1)
                    if v in (2, 3):
                        pe.wait_ge(m_relu, u - 1)
                    if v in (4, 5):
                        pe.wait_ge(m_xl_lo, 4 * half + 2 * LT)
                    if v in (6, 7):
                        pe.wait_ge(m_relu, u - 3)
                    mm = contract(pe, up_bank(u), [(tokens(up_r, k, v * P, P), tokens(HT, k, half * 512, 512))
                                                   for k in range(KT)])
                    mm.then_inc(m_up, 1)

            def down(b):
                if b % HALF < 2:
                    pe.wait_ge(m_fc2_out, HALF * (b // HALF + 1))
                else:
                    pe.wait_ge(z_stat, b - 1)
                for k in range(IT):
                    if b % HALF == 0:
                        pe.wait_ge(chunk_split, C_DOWN + k + 1)
                        pe.wait_ge(m_sq_lo, IT * (b // HALF) + k + 1)
                    mm = product(pe, bank[4 + b % 2], tokens(actT, k, (b % HALF) * P, P), hilo(down_r, k), k == 0, k == IT - 1)
                mm.then_inc(m_down, 1)

            pe.wait_ge(s_exp, 2 * STEPS)
            pe.wait_ge(pt_lo, 2 * STEPS)
            pe.wait_ge(o_lo, STEPS)
            pe.wait_ge(y_acc, STEPS)
            pe.wait_ge(ln_lo, B + HALF)
            gate_logits(0)
            ln_transpose(2 * B - 1)
            latent(0)
            gate_rows(0)
            up(0, 0, 2)
            latent_expert(0)
            latent_out(0)
            up(0, 2, IT)
            for b in range(HALF):
                down(b)
            pe.wait_ge(m_relu, IT)
            pe.wait_ge(ln_lo, 2 * B)
            gate_logits(1)
            latent(1)
            gate_rows(1)
            ln_transpose(2 * B)
            ln_transpose(2 * B + 1)
            up(1, 0, 2)
            latent_expert(1)
            ln_transpose(2 * B + 2)
            latent_out(1)
            ln_transpose(2 * B + 3)
            up(1, 2, IT)
            down(4)
            down(5)
            down(6)
            ln_transpose(2 * B + 4)
            down(7)
            ln_transpose(2 * B + 5)

            def queries1(n):
                half, m = n // M1, n % M1
                if n < 4:
                    pe.wait_ge(m_relu, 2 * IT)
                else:
                    pe.wait_ge(q1_lo, n - 3)
                mm = contract(pe, bank[n % 4], [(tokens(wq1_r, k, m * P, P), tokens(HT, k, half * 512, 512)) for k in range(KT)])
                mm.then_inc(q1_mm, 1)

            pe.wait_ge(chunk_split, C_WOUT)
            pe.wait_ge(ln_lo, 2 * B + HALF)
            for n in range(2 * M1):
                if n == M1:
                    pe.wait_ge(ln_lo, 3 * B)
                queries1(n)
                if n in (1, 2):
                    ln_transpose(2 * B + 5 + n)
            pe.wait_ge(mask_made, 4)
            pe.wait_ge(identr_made, 1)
            pe.wait_ge(z_stat, B)
            for w in range(UNITS1 + 10):
                if w < UNITS1:
                    b, m, acc = w // G1, w % G1 // 2, bank[w % 3]
                    if w < 3:
                        pe.wait_ge(q1_lo, M1 + w + 1)
                    if w >= 3:
                        pe.wait_ge(s1_sub, w - 2)
                    if w % 2 == 0:
                        pe.wait_ge(kb_loaded[m], 16 * HT1 * (b + 1))
                    pe.matmul(acc, identr, maskr, start=True, stop=False)
                    first = SHARE1 * (w % 2)
                    product(pe, acc, tokens(qT1[:, b // HALF], m, b % HALF * P, P), hilo(KB[:, m], slice(first, first + SHARE1)), False, True
                            ).then_inc(s1_mm, 1)
                if 2 <= w < UNITS1 + 2:
                    v = w - 2
                    pe.wait_ge(s1_exp, v + 1)
                    if v == 0:
                        pe.wait_ge(q1_lo, 2 * M1)
                    if v >= 2:
                        pe.wait_ge(p1_copy, v - 1)
                    for h in range(SHARE1):
                        mm = pe.transpose(bank[3 + v % 2][:, h * P:(h + 1) * P], prob1[:, v % 4, h * P:(h + 1) * P], ident[:, :])
                    mm.then_inc(p1_T, 1)
                v = w - 3
                if 0 <= v < UNITS1:
                    b, g = v // G1, v % G1
                    pe.wait_ge(p1_copy, v + 1)
                    if g % 4 == 0 and b >= 1:
                        pe.wait_ge(o1_row, 2 * b - 1 + g // 4)
                    for h in range(SHARE1):
                        at = (g % 4 * SHARE1 + h) * (D1 + 1)
                        mm = pe.matmul(bank[5 + g // 4][:, at:at + D1 + 1], probT1[:, v % 4, h * P:(h + 1) * P],
                                       V1[:, b, g, :], start=True, stop=True)
                    mm.then_inc(o1_mm, 1)
                if w >= 11 and (w - 11) % G1 == 0 and (w - 11) // G1 < B:
                    b = (w - 11) // G1
                    pe.wait_ge(o1_row, 2 * b + 2)
                    if b:
                        pe.wait_ge(g1_part, CHOICE * (b - 1) + 1)
                    for k in range(KT):
                        mm = pe.transpose(bank[7][:, k * P:(k + 1) * P], hrow[:, b % 2, k * P:(k + 1) * P], ident[:, :])
                    mm.then_inc(o1_T, 1)
                if w >= 13 and (w - 13) % G1 == 0 and (w - 13) // G1 < B:
                    b = (w - 13) // G1
                    if b == 0:
                        pe.wait_ge(chunk_split, C_EX)
                    pe.wait_ge(o1_lo, b + 1)
                    mm = contract(pe, bank[7], [(hilo(OT1[:, b % 2], k), hilo(wout_r, k)) for k in range(KT)])
                    mm.then_inc(y1_mm, 1)
                if w >= 16 and (w - 16) % G1 == 0:
                    b = (w - 16) // G1
                    pe.wait_ge(y1_acc, b + 1)
                    ln_transpose(3 * B + b)
                if w >= 17 and (w - 17) % G1 == 0:
                    b = (w - 17) // G1
                    pe.wait_ge(g1_xt, b + 1)
                    for k in range(KT):
                        mm = pe.matmul(bank[7][:, 0:NE], hrow[:, b % 2, k * P:(k + 1) * P], gw1[:, k, :],
                                       start=k == 0, stop=k == KT - 1)
                    mm.then_inc(g1_mm, 1)

            pe.wait_ge(g1_part, CHOICE * B)
            pe.wait_ge(tables_made, 6)
            pe.wait_ge(s1_sub, UNITS1)
            pe.matmul(bank[2][:, 0:(B + 1) * NE], ones, chosen.rearrange("p b e -> p (b e)"), start=True, stop=False)
            mm = pe.matmul(bank[2][:, 0:B * NE], before, oneh.rearrange("p b e -> p (b e)"), start=False, stop=True)
            mm.then_inc(g1_rank, 1)
            for b in range(B):
                mm = pe.transpose(PS[0:NE, 6 + b // 4, (b % 4) * P:(b % 4 + 1) * P], oneh[:, b, :], ident[:, :])
            mm.then_inc(g1_T, 1)

            def block_of(j):
                return pe.value_load(tile_block[0:1, j:j + 1], min_val=1, max_val=NE)

            pe.wait_ge(g1_copy, 1)
            pe.wait_ge(eb_lo, 1)
            for b in range(B):
                if b >= 2:
                    pe.wait_ge(b1_acc, b - 1)
                for part in range(2):
                    mm = pe.matmul(bank[6 + b % 2], onehT[:, b * P:(b + 1) * P], ebias_r[:, part, :],
                                   start=part == 0, stop=part == 1)
                mm.then_inc(b1_mm, 1)
            pe.wait_ge(blocks_made, 1)
            tile_blocks = [block_of(j) for j in range(2)]

            def tile_transpose(j):
                pe.wait_ge(xs_loaded[j % 4], 16 * (j // 4 + 1))
                if j >= 2:
                    pe.wait_ge(xs_lo, j - 1)
                for k in range(KT):
                    mm = pe.transpose(bank[4 + j % 2][:, k * P:(k + 1) * P], xs_raw[:, j % 4, k * P:(k + 1) * P], ident[:, :])
                mm.then_inc(xs_T, 1)

            tile_transpose(0)
            pe.wait_ge(chunk_split, C_POOL)
            pe.wait_ge(ex_lo, C_ALL - C_POOL)
            for j in range(TILES):
                if j + 1 < TILES:
                    tile_transpose(j + 1)
                if j + 2 < TILES:
                    tile_blocks.append(block_of(j + 2))
                pe.wait_ge(xs_lo, j + 1)
                if j >= 4:
                    pe.wait_ge(y_copied, j - 3)
                weights = [[blocks[:, bass.ds(tile_blocks[j], 1), part, k, :].rearrange("p a n -> p (a n)")
                            for part in range(2)] for k in range(KT)]
                contract(pe, bank[j % 4], [(hilo(XST[:, j % 2], k), weights[k]) for k in range(KT)]).then_inc(e_mm, 1)


_ORDER = ["x", "ctxT", "mask", "g_xattn", "g_ffn", "Wq", "Wk", "Wv", "Wo", "gate0", "up_w", "down_w", "fc1_w", "fc2_w",
          "latent_w", "ln_gamma", "ln_beta", "wqT", "wkT", "wvT", "woutT", "gate1T", "gate1_b", "expertT", "expert_b"]


def kernel(**inputs):
    import numpy as _np
    import concourse.bacc as _bacc
    from concourse import mybir as _mybir
    from concourse.bass_utils import run_bass_kernel_spmd as _run

    a = {k: _np.asarray(v) for k, v in inputs.items()}
    laid = {
        "x": a["x"],
        "ctxT": a["ctx_4096"].reshape(-1, a["ctx_4096"].shape[-1]).T,
        "mask": a["mask_SxS2_bk0"],
        "g_xattn": a["g_xattn"], "g_ffn": a["g_ffn"],
        "Wq": a["L0_xattn_Wq"], "Wk": a["L0_xattn_Wk"], "Wv": a["L0_xattn_Wv"], "Wo": a["L0_xattn_Wo"],
        "gate0": a["L0_ffn_gate_w"], "up_w": a["L0_ffn_up_w"], "down_w": a["L0_ffn_down_w"],
        "fc1_w": a["L0_ffn_fc1_w"], "fc2_w": a["L0_ffn_fc2_w"], "latent_w": a["L0_ffn_expert_w"],
        "ln_gamma": a["L0_ffn_ln_gamma"], "ln_beta": a["L0_ffn_ln_beta"],
        "wqT": a["L1_xattn_w_q"].T, "wkT": a["L1_xattn_w_k"].T, "wvT": a["L1_xattn_w_v"].T,
        "woutT": a["L1_xattn_w_out"].T,
        "gate1T": a["L1_ffn_gate_w"].T, "gate1_b": a["L1_ffn_gate_b"],
        "expertT": a["L1_ffn_expert_w"].transpose(0, 2, 1), "expert_b": a["L1_ffn_expert_b"],
    }
    nc = _bacc.Bacc("TRN2", target_bir_lowering=False, num_devices=1)
    arrays, args = {}, []
    for name in _ORDER:
        v = _np.ascontiguousarray(laid[name])
        arrays[f"in_{name}"] = v
        args.append(nc.dram_tensor(f"in_{name}", v.shape, _mybir.dt.from_np(v.dtype), kind="ExternalInput").ap())
    shape = a["x"].shape
    args.append(nc.dram_tensor("out_0", shape, _mybir.dt.float32, kind="ExternalOutput").ap())
    program(nc, *args)
    r = _run(nc, [arrays], core_ids=[0])
    return r.results[0]["out_0"]
```
